# Optimizing a Trainium2 kernel written in Bass

```python
import numpy as np
import jax
import jax.numpy as jnp

def _softmax(x, axis=-1):
    return jax.nn.softmax(x, axis=axis)

def _gelu(x):
    return jax.nn.gelu(x, approximate=True)

def _silu(x):
    return jax.nn.silu(x)

def _sigmoid(x):
    return jax.nn.sigmoid(x)

def _layernorm(x, axis=-1, eps=1e-05):
    m = jnp.mean(x, axis=axis, keepdims=True)
    v = jnp.var(x, axis=axis, keepdims=True)
    return (x - m) / jnp.sqrt(v + eps)

def _scatter_add(tgt, idx, src, axis=0):
    return tgt.at[idx].add(src)

def _segment_sum(src, seg, n):
    return jax.ops.segment_sum(src, seg, n)
kernel_name = 'mk_adaln_d1_jaxref_r4_c38039'

def setup_inputs(seed: int=0):
    np.random.seed(seed)
    _w = jnp.asarray

    def _L0_attn_setup():
        import jax, jax.numpy as jnp
        import numpy as np
        D_MODEL = 256
        N_HEADS = 16
        ORDER = 6
        P2 = 2 * ORDER - 1
        EPS_CLAMP = 1e-06
        EPS_DEN = 1e-07

        def _beta_np():
            j = np.arange(ORDER, dtype=np.float32)
            alpha = (j + 1.0) ** (-1.5)
            tail = np.flip(np.cumsum(np.flip(alpha)))
            beta = np.concatenate([np.zeros(1, np.float32), tail[1:].astype(np.float32), np.zeros(ORDER - 1, np.float32)])
            return beta / beta.sum()

        def _cheb(x):
            T = [jnp.ones_like(x), x]
            for _ in range(2, P2):
                T.append(2.0 * x * T[-1] - T[-2])
            return jnp.stack(T, axis=3)
        key = jax.random.key(seed)
        k1, k2, k3 = jax.random.split(key, 3)
        B, S, D = (2, 256, D_MODEL)
        x = jax.random.normal(k1, (B, S, D), dtype=jnp.float32)
        W_in = jax.random.normal(k2, (3 * D, D), dtype=jnp.float32) * 0.02
        W_out = jax.random.normal(k3, (D, D), dtype=jnp.float32) * 0.02
        return {'x': x, 'W_in': W_in, 'W_out': W_out}
    _L0_attn_in = _L0_attn_setup()

    def _L0_ffn_setup():
        import jax, jax.numpy as jnp
        import numpy as np
        E = 8
        K = 2
        key = jax.random.key(seed)
        ks = jax.random.split(key, 8)
        B, T, d = (4, 512, 256)
        h = 4 * d // E
        s = 0.02
        X = jax.random.normal(ks[0], (B, T, d), jnp.float32)
        routing_W = jax.random.normal(ks[1], (E, d), jnp.float32) * s
        expert_bias = jnp.zeros((E,), jnp.float32)
        sW1 = jax.random.normal(ks[2], (d, h), jnp.float32) * s
        sb1 = jnp.zeros((h,), jnp.float32)
        sW2 = jax.random.normal(ks[3], (h, d), jnp.float32) * s
        sb2 = jnp.zeros((d,), jnp.float32)
        rW1 = jax.random.normal(ks[4], (E, d, h), jnp.float32) * s
        rb1 = jnp.zeros((E, h), jnp.float32)
        rW2 = jax.random.normal(ks[5], (E, h, d), jnp.float32) * s
        rb2 = jnp.zeros((E, d), jnp.float32)
        return dict(X=X, routing_W=routing_W, expert_bias=expert_bias, sW1=sW1, sb1=sb1, sW2=sW2, sb2=sb2, rW1=rW1, rb1=rb1, rW2=rW2, rb2=rb2)
    _L0_ffn_in = _L0_ffn_setup()
    _L0_c = _w((lambda *s: np.random.randn(*s).astype(np.float32) * 0.05)(8, 256))
    _L0_wmod = _w((lambda *s: np.random.randn(*s).astype(np.float32) * 0.05)(256, 6 * 256) * 256 ** (-0.5))
    _d = {'L0_attn_x': _L0_attn_in['x'], 'L0_attn_W_in': _L0_attn_in['W_in'], 'L0_attn_W_out': _L0_attn_in['W_out'], 'L0_ffn_routing_W': _L0_ffn_in['routing_W'], 'L0_ffn_expert_bias': _L0_ffn_in['expert_bias'], 'L0_ffn_sW1': _L0_ffn_in['sW1'], 'L0_ffn_sb1': _L0_ffn_in['sb1'], 'L0_ffn_sW2': _L0_ffn_in['sW2'], 'L0_ffn_sb2': _L0_ffn_in['sb2'], 'L0_ffn_rW1': _L0_ffn_in['rW1'], 'L0_ffn_rb1': _L0_ffn_in['rb1'], 'L0_ffn_rW2': _L0_ffn_in['rW2'], 'L0_ffn_rb2': _L0_ffn_in['rb2'], 'L0_c': _L0_c, 'L0_wmod': _L0_wmod}
    _x0 = _d['L0_attn_x']
    _d['L0_attn_x'] = jax.random.normal(jax.random.fold_in(jax.random.key(seed), 1), (8, 1024, 256), dtype=_x0.dtype)
    del _x0
    return _d

def reference(L0_attn_x, L0_attn_W_in, L0_attn_W_out, L0_ffn_routing_W, L0_ffn_expert_bias, L0_ffn_sW1, L0_ffn_sb1, L0_ffn_sW2, L0_ffn_sb2, L0_ffn_rW1, L0_ffn_rb1, L0_ffn_rW2, L0_ffn_rb2, L0_c, L0_wmod):

    def _L0_attn_ref(x, W_in, W_out):
        import jax, jax.numpy as jnp
        import numpy as np
        D_MODEL = 256
        N_HEADS = 16
        ORDER = 6
        P2 = 2 * ORDER - 1
        EPS_CLAMP = 1e-06
        EPS_DEN = 1e-07

        def _beta_np():
            j = np.arange(ORDER, dtype=np.float32)
            alpha = (j + 1.0) ** (-1.5)
            tail = np.flip(np.cumsum(np.flip(alpha)))
            beta = np.concatenate([np.zeros(1, np.float32), tail[1:].astype(np.float32), np.zeros(ORDER - 1, np.float32)])
            return beta / beta.sum()

        def _cheb(x):
            T = [jnp.ones_like(x), x]
            for _ in range(2, P2):
                T.append(2.0 * x * T[-1] - T[-2])
            return jnp.stack(T, axis=3)
        B, S, D = x.shape
        H, Dh = (N_HEADS, D // N_HEADS)
        qkv = jnp.einsum('bsd,ed->bse', x, W_in)
        q, k, v = jnp.split(qkv, 3, axis=-1)
        q = q.reshape(B, S, H, Dh).transpose(0, 2, 1, 3)
        k = k.reshape(B, S, H, Dh).transpose(0, 2, 1, 3)
        v = v.reshape(B, S, H, Dh).transpose(0, 2, 1, 3)
        inv_sqrt_d = 1.0 / jnp.sqrt(jnp.float32(Dh))
        xq = jnp.clip(q * inv_sqrt_d, -1.0 + EPS_CLAMP, 1.0 - EPS_CLAMP)
        xk = jnp.clip(k * inv_sqrt_d, -1.0 + EPS_CLAMP, 1.0 - EPS_CLAMP)
        Tq = _cheb(xq)
        Tk = _cheb(xk)
        beta = jnp.asarray(_beta_np())
        Tv = Tk * v[:, :, :, None, :]
        kv_prefix = jnp.cumsum(Tv, axis=2)
        ks_prefix = jnp.cumsum(Tk.sum(axis=-1), axis=2)
        kv_beta = kv_prefix * beta[None, None, None, :, None]
        k_beta = ks_prefix * beta[None, None, None, :]
        num = (Tq * kv_beta).sum(axis=3)
        den = (Tq.sum(axis=-1) * k_beta).sum(axis=3)
        out_h = num / (den[..., None] + EPS_DEN)
        out = out_h.transpose(0, 2, 1, 3).reshape(B, S, H * Dh)
        return jnp.einsum('bsd,ed->bse', out, W_out)

    def _L0_ffn_ref(X, routing_W, expert_bias, sW1, sb1, sW2, sb2, rW1, rb1, rW2, rb2):
        import jax, jax.numpy as jnp
        import numpy as np
        E = 8
        K = 2
        B, T, d = X.shape
        shared = jax.nn.silu(X @ sW1 + sb1) @ sW2 + sb2
        logits = jnp.einsum('btd,ed->bte', X, routing_W) + expert_bias
        activation = jnp.sqrt(jax.nn.softplus(logits))
        top_vals, top_idx = jax.lax.top_k(activation, K)
        combine = jnp.sum(jax.nn.one_hot(top_idx, E, dtype=X.dtype) * top_vals[..., None], axis=-2)
        Xf = X.reshape(-1, d)
        cf = combine.reshape(-1, E)
        hdn = jax.nn.silu(jnp.einsum('nd,edh->enh', Xf, rW1) + rb1[:, None, :])
        y = jnp.einsum('enh,ehd->end', hdn, rW2) + rb2[:, None, :]
        routed = jnp.einsum('ne,end->nd', cf, y).reshape(B, T, d)
        return shared + routed
    x = L0_attn_x
    mod = (_silu(L0_c) @ L0_wmod).reshape(L0_c.shape[0], 6, 1, -1)
    sa, ca, ga, sb, cb, gb = (mod[:, 0], mod[:, 1], mod[:, 2], mod[:, 3], mod[:, 4], mod[:, 5])
    ga = (2 * (ga >= 0) - 1) * jnp.maximum(jnp.abs(ga), 0.25)
    gb = (2 * (gb >= 0) - 1) * jnp.maximum(jnp.abs(gb), 0.25)
    h = _layernorm(x, axis=-1) * (1 + ca) + sa
    x = x + ga * _L0_attn_ref(h, L0_attn_W_in, L0_attn_W_out)
    h = _layernorm(x, axis=-1) * (1 + cb) + sb
    x = x + gb * _L0_ffn_ref(h, L0_ffn_routing_W, L0_ffn_expert_bias, L0_ffn_sW1, L0_ffn_sb1, L0_ffn_sW2, L0_ffn_sb2, L0_ffn_rW1, L0_ffn_rb1, L0_ffn_rW2, L0_ffn_rb2)
    return x

_drawn_inputs = setup_inputs


def setup_inputs(seed=0):
    import zlib

    import numpy as np

    out = dict(_drawn_inputs(seed))
    spreads = {'L0_ffn_expert_bias': (0.0, 0.37),
     'L0_ffn_sb1': (0.0, 0.8),
     'L0_ffn_sb2': (0.0, 0.3),
     'L0_ffn_rb1': (0.0, 0.8),
     'L0_ffn_rb2': (0.0, 0.293)}
    factors = {'L0_attn_W_in': 8.0,
     'L0_attn_W_out': 8.0,
     'L0_ffn_sW1': 6.123,
     'L0_ffn_sW2': 5.803,
     'L0_ffn_rW1': 4.422,
     'L0_ffn_rW2': 4.147}
    for name, (base, spread) in spreads.items():
        noise = np.random.default_rng([zlib.crc32(name.encode()), seed]).standard_normal(out[name].shape)
        drawn = base * np.exp(spread * noise) if base else spread * noise
        out[name] = jnp.asarray(drawn.astype(out[name].dtype))
    for name, factor in factors.items():
        out[name] = (out[name] * factor).astype(out[name].dtype)
    return out
```

```python
import concourse.bass as bass
from concourse import mybir
from contextlib import ExitStack
import numpy as np

B, S, D = 8, 1024, 256
P = 128
KD = D // P
H, DH = 16, 16
E = 8
NE = E + 1
HID = 4 * D // E
CT = 512
NT = CT // P
CB = S // CT
NC = B * CB
ORDER = 6
ND = ORDER - 1
CLIP = 1.0 - 1e-6
HPH = H // KD
QS = 32
SPL = 2 * (3 * E + 1)
XS = 4


def chebyshev_weights():
    j = np.arange(ORDER, dtype=np.float32)
    alpha = (j + 1.0) ** (-1.5)
    tail = np.flip(np.cumsum(np.flip(alpha)))
    beta = np.concatenate([np.zeros(1, np.float32), tail[1:].astype(np.float32), np.zeros(ORDER - 1, np.float32)])
    beta = (beta / beta.sum()).astype(np.float32)
    return [float(beta[n]) * 4.0 ** (n - 1) for n in range(1, ORDER)]


GAMMA = chebyshev_weights()


def head_rows():
    rows = {}
    for n in range(4):
        rows[n, 0], rows[n, 1] = (n, 0), (n, 2 * HPH)
    rows[4, 0], rows[4, 1] = (0, HPH), (1, 3 * HPH)
    return rows


ROWS = head_rows()

CONSTS = {"ident": P, "headsum": 4 * QS, "densum": QS, "headsel": NT * KD * P, "kshift": 1, "rowmask": 2,
          "biases": 2, "before": E * E, "after": E * E, "cfsel": E * P}


def constants():
    c = {k: np.zeros((P, n), np.float32) for k, n in CONSTS.items()}
    c["ident"] = np.eye(P, dtype=np.float32)
    ch = np.arange(P)
    for o in range(4):
        c["headsum"][ch, o * QS + o * HPH + ch // DH] = 1.0
    for (n, half), (g, r) in ROWS.items():
        for h in range(HPH):
            row = g * QS + r + h
            w = GAMMA[n] if n in (0, 2, 4) else 1.0
            for copy in range(QS // H):
                c["densum"][row, copy * H + half * HPH + h] = w
            c["kshift"][row, 0] = {1: -0.5 * DH, 3: -0.125 * DH}.get(n, 0.0)
    for q in range(4):
        for half in range(KD):
            c["headsel"][q * QS + half * HPH + ch // DH, (q * KD + half) * P + ch] = 1.0
    c["rowmask"][:SPL // 2, 0] = 1.0
    c["rowmask"][SPL // 2:SPL, 1] = 1.0
    c["biases"][:, 0], c["biases"][:, 1] = -0.5, -0.625
    e, j = np.meshgrid(np.arange(E), np.arange(E), indexing="ij")
    c["before"][:] = (j < e).astype(np.float32).ravel()
    c["after"][:] = (j > e).astype(np.float32).ravel()
    for x in range(E):
        for part in range(3):
            c["cfsel"][part * E + x, x * P:(x + 1) * P] = 1.0
    return np.concatenate([c[k] for k in CONSTS], axis=1)


def build(nc, x_d, w_in_d, w_out_d, rout_d, ebias_d, sw1_d, sb1_d, sw2_d, sb2_d,
          rw1_d, rb1_d, rw2_d, rb2_d, c_d, wmod_d, const_d, out_d):
    f32, f32r, bf16 = mybir.dt.float32, mybir.dt.float32r, mybir.dt.bfloat16
    ALU = mybir.AluOpType
    ACT = mybir.ActivationFunctionType
    AX = mybir.AxisListType
    EPS_LN, EPS_DEN = 1e-5, 1e-7

    ctx = ExitStack()
    with ctx:
        def sb(name, shape, dt=f32):
            return ctx.enter_context(nc.sbuf_tensor(name, shape, dt))

        def sem(name):
            return ctx.enter_context(nc.semaphore(name))

        const = sb("const", [P, sum(CONSTS.values()) - CONSTS["cfsel"]])
        cv, at = {}, 0
        for k, n in CONSTS.items():
            if k != "cfsel":
                cv[k] = const[:, at:at + n]
                at += n
        ident = cv["ident"]
        before = cv["before"].unsqueeze(1).to_broadcast([P, NT, E * E])
        after = cv["after"].unsqueeze(1).to_broadcast([P, NT, E * E])
        PC = ("-half", "half", "one", "eps", "1/D") + tuple(range(15, 0, -2))
        pool_c = sb("pool_c", [P, len(PC)])
        cfsel = sb("cfsel", [SPL // 2, E, P], bf16)
        winH = sb("winH", [P, KD, 3 * D], f32r)
        winL = sb("winL", [P, KD, 3 * D], f32r)
        w1H = sb("w1H", [P, NE, KD, HID], f32r)
        w1L = sb("w1L", [P, NE, KD, HID], f32r)
        w2 = sb("w2", [P, NE, D])
        wo = sb("wo", [P, KD, D])
        rtH = sb("rtH", [P, KD, E], f32r)
        rtL = sb("rtL", [P, KD, E], f32r)
        r2 = sb("r2", [SPL, D], f32r)
        mods = sb("mods", [P, 4, KD, B])
        gates = sb("gates", [P, 2, D])
        gate_rows = nc.dram_tensor("gate_rows", [B, 2 * D], f32).ap()
        bqkv = sb("bqkv", [P, 6, B])
        b1 = sb("b1", [P, B, NE])
        b1row = sb("b1row", [P, NE])
        blog = sb("blog", [E, B])

        xin = sb("xin", [P, XS, NT, D])
        x1 = sb("x1", [P, 2, NT, D])
        ntok = sb("ntok", [P, 2, NT, D])
        stats = sb("stats", [P, 2, NT, 6])
        ms = sb("ms", [P, 2, 10, NT])
        n1H = sb("n1H", [P, KD, CT], f32r)
        n1L = sb("n1L", [P, KD, CT], f32r)
        n2H = sb("n2H", [P, 2, KD, CT], f32r)
        n2L = sb("n2L", [P, 2, KD, CT], f32r)
        NF = 18
        feat = sb("feat", [P, NF, KD, CT])
        K0, K1, Q0, Q1, V0, KS, KT3, KA, KT5, QSQ, QT3, QA, QT5, W = range(14)
        attn = feat[:, W + 1]
        gated = feat[:, W + 3].rearrange("p h (t d) -> p h t d", t=2)
        carry = sb("carry", [P, ND, KD])
        zero = sb("zero", [P, 1])
        prod = sb("prod", [P, CT])
        kcarry = sb("kcarry", [P, 1])
        denom = sb("denom", [P, 2, P])
        logT = sb("logT", [P, CT])
        route = sb("route", [P, 12, NT * E])
        L_, NEG, U, MX, DN, RC, Z, Z2, PL, SP, AC, CF = range(12)
        pair = sb("pair", [P, 2, NT, E, E])
        rank = sb("rank", [P, NT * E])
        part = sb("part", [P, 2, NT, E], bf16)
        rest = sb("rest", [P, NT, E])
        split = sb("split", [P, NT, P])
        cfR = sb("cfR", [SPL, CT], f32r)
        cfB = sb("cfB", [SPL // 2, CT], bf16)
        NG = 3
        hid = sb("hid", [P, NG, CT])
        fin = sb("fin", [P, NT, D])

        flat = feat[:, :, :, :].rearrange("p n h t -> p (n h t)")
        used = [0]

        def tmp(n):
            v = flat[:, used[0]:used[0] + n]
            used[0] += n
            return v

        win_rows = tmp(6 * D).rearrange("p (m d) -> p m d", m=6)
        winT = tmp(KD * 3 * D).rearrange("p (k e) -> p k e", k=KD)
        wout_rows = tmp(2 * D).rearrange("p (m d) -> p m d", m=2)
        wmod = tmp(KD * 6 * D).rearrange("p (k n) -> p k n", k=KD)
        w1f = tmp(NE * KD * HID).rearrange("p (e k h) -> p e k h", e=NE, k=KD)
        cfself = tmp(E * P)
        c_rows = tmp(D)
        silu_c = tmp(D)
        scT = tmp(KD * B).rearrange("p (k b) -> p k b", k=KD)
        rt_rows = tmp(D)
        rtF = tmp(KD * E).rearrange("p (k e) -> p k e", k=KD)
        b1_rows = tmp(HID)
        b1T = tmp(NE)
        eb = tmp(1)
        r2f, r2h, r2l = tmp(D), tmp(D), tmp(D)
        gsign, gneg, gabs, gfull = tmp(2 * D), tmp(2 * D), tmp(2 * D), tmp(2 * D)
        assert used[0] <= NF * KD * CT

        tr = [ctx.enter_context(nc.psum_tensor(f"tr{k}", [P, CT], f32)) for k in range(2)]
        ring = [ctx.enter_context(nc.psum_tensor(f"ring{k}", [P, CT], f32)) for k in range(2)]
        cfb = ctx.enter_context(nc.psum_tensor("cfb", [P, CT], f32))
        misc = ctx.enter_context(nc.psum_tensor("misc", [P, CT], f32))
        acc = [ctx.enter_context(nc.psum_tensor(f"acc{k}", [P, 2, D], f32)) for k in range(2)]

        in_win, in_wout, in_small, in_const, in_wmod, in_w1, in_w2, in_r2, in_gates = (
            sem(f"in_{n}") for n in ("win", "wout", "small", "const", "wmod", "w1", "w2", "r2", "gate_rows"))
        s_tr = sem("setup_transposed")
        s_silu, s_scT = sem("setup_silu"), sem("setup_scT")
        s_hi, s_mods, s_modps, s_gps, s_g1, s_g2 = (sem(f"setup_{n}") for n in (
            "high_parts", "mods", "mod_products", "gate_products", "gate_sign", "gate_abs"))
        s_bias, s_b1T, s_r2 = sem("setup_bias_products"), sem("setup_b1T"), sem("setup_r2")
        s_winT, s_rtT, s_wo, s_pow = sem("setup_winT"), sem("setup_rtT"), sem("setup_wo"), sem("setup_exponents")

        with nc.Block() as block:
            @block.sync
            def _(sp):
                sp.dma_start(c_rows[0:B, :], c_d).then_inc(in_small, 16)
                sp.dma_start(rt_rows[0:E, :], rout_d).then_inc(in_small, 16)
                sp.dma_start(b1_rows[0:1, :], sb1_d.rearrange("(a h) -> a h", a=1)).then_inc(in_small, 16)
                sp.dma_start(b1_rows[1:NE, :], rb1_d).then_inc(in_small, 16)
                sp.dma_start(eb[0:E, :], ebias_d.rearrange("(e a) -> e a", a=1)).then_inc(in_small, 16)
                sp.dma_start(win_rows, w_in_d.rearrange("(m p) d -> p m d", p=P)).then_inc(in_win, 16)
                sp.dma_start(wmod, wmod_d.rearrange("(k p) n -> p k n", p=P)).then_inc(in_wmod, 16)
                sp.dma_start(wout_rows, w_out_d.rearrange("(m p) d -> p m d", p=P)).then_inc(in_wout, 16)
                sp.dma_start(w1f[:, 0], sw1_d.rearrange("(k p) h -> p k h", p=P)).then_inc(in_w1, 16)
                sp.dma_start(w1f[:, 1:NE].rearrange("p e k h -> p (e k) h"),
                             rw1_d.rearrange("e (k p) h -> p (e k) h", p=P)).then_inc(in_w1, 16)
                sp.wait_ge(s_g2, 1)
                sp.dma_start(gate_rows, gfull[0:B, :]).then_inc(in_gates, 16)
                sp.wait_ge(in_gates, 16)

            @block.gpsimd
            def _(pool):
                for n, what in enumerate(PC):
                    value = {"-half": -0.5, "half": 0.5, "one": 1.0, "eps": EPS_LN, "1/D": 1.0 / D}.get(what) or 2.0 / what
                    nc.gpsimd.memset(pool_c[:, n:n + 1], value).then_inc(s_pow, 1)
                nc.gpsimd.memset(split[:, :, :], 1.0).then_inc(s_pow, 1)
                nc.gpsimd.memset(zero[:, :], 0.0).then_inc(s_pow, 1)
                nc.gpsimd.memset(logT[:, :], 0.0).then_inc(s_pow, 1)
                pool.wait_ge(s_pow, len(PC) + 3)

            @block.scalar
            def _(act):
                act.dma_start(const[:, :], const_d[:, 0:at]).then_inc(in_const, 16)
                act.dma_start(cfself, const_d[:, at:at + E * P]).then_inc(in_const, 16)
                act.dma_start(w2[:, 0], sw2_d).then_inc(in_w2, 16)
                act.dma_start(w2[:, 1:NE], rw2_d.rearrange("e h d -> h e d")).then_inc(in_w2, 16)
                for half in range(2):
                    r = half * (SPL // 2)
                    for copy in range(3):
                        act.dma_start(r2f[r + copy * E:r + (copy + 1) * E, :], rb2_d).then_inc(in_r2, 16)
                    act.dma_start(r2f[r + 3 * E:r + 3 * E + 1, :],
                                  sb2_d.rearrange("(a d) -> a d", a=1)).then_inc(in_r2, 16)
                act.wait_ge(in_small, 5 * 16)
                nc.scalar.activation(silu_c[0:B, :], c_rows[0:B, :], ACT.Silu).then_inc(s_silu, 1)
                for m in range(6):
                    act.wait_ge(s_tr, 2 + m)
                    for k in range(KD):
                        last = nc.scalar.activation(winT[:, k, m * P:(m + 1) * P], ring[m % 2][:, k * P:(k + 1) * P],
                                                    ACT.Copy, scale=0.25 if m < 4 else 1.0)
                    last.then_inc(s_winT, 1)
                act.wait_ge(s_winT, 6)
                nc.scalar.activation(winH[:, :, :], winT, ACT.Copy).then_inc(s_hi, 1)
                for m in range(2):
                    act.wait_ge(s_tr, 8 + m)
                    for k in range(KD):
                        last = nc.scalar.activation(wo[:, k, m * P:(m + 1) * P], ring[m % 2][:, k * P:(k + 1) * P],
                                                    ACT.Copy)
                    last.then_inc(s_wo, 1)
                act.wait_ge(in_w1, 32)
                nc.scalar.activation(w1H[:, :, :, :], w1f, ACT.Copy).then_inc(s_hi, 1)
                act.wait_ge(s_wo, 2)

            @block.vector
            def _(dve):
                dve.wait_ge(s_tr, 1)
                nc.vector.tensor_copy(scT, tr[0][:, 0:KD * B].rearrange("p (k b) -> p k b", k=KD)).then_inc(s_scT, 1)
                nc.vector.tensor_copy(rtF, tr[0][:, 64:64 + KD * E].rearrange("p (k e) -> p k e", k=KD)).then_inc(s_rtT, 1)
                nc.vector.tensor_copy(b1T, tr[0][:, 128:128 + NE]).then_inc(s_b1T, 1)
                dve.wait_ge(s_rtT, 1)
                nc.vector.tensor_copy(rtH[:, :, :], rtF).then_inc(s_rtT, 1)
                dve.wait_ge(s_rtT, 2)
                nc.vector.tensor_tensor(rtL[:, :, :], rtF, rtH[:, :, :].bitcast(f32), ALU.subtract).then_inc(s_rtT, 1)
                dve.wait_ge(s_modps, 1)
                mp = misc[:, 0:4 * KD * B].rearrange("p (v k b) -> p v k b", v=4, k=KD)
                for v in range(4):
                    last = nc.vector.tensor_scalar(mods[:, v], mp[:, v], float(v % 2), None, ALU.add)
                last.then_inc(s_mods, 1)
                dve.wait_ge(s_gps, 1)
                g = acc[0][0:B].rearrange("p g d -> p (g d)")
                nc.vector.tensor_scalar(gsign[0:B], g, 0.0, 2.0, ALU.is_ge, ALU.mult).then_inc(s_g1, 1)
                nc.vector.tensor_scalar(gneg[0:B], g, -1.0, 0.25, ALU.mult, ALU.max).then_inc(s_g1, 1)
                dve.wait_ge(s_g1, 2)
                nc.vector.tensor_tensor(gabs[0:B], g, gneg[0:B], ALU.max).then_inc(s_g1, 1)
                dve.wait_ge(s_g1, 3)
                nc.vector.scalar_tensor_tensor(out=gfull[0:B], in0=gsign[0:B], scalar=-1.0, in1=gabs[0:B],
                                               op0=ALU.add, op1=ALU.mult).then_inc(s_g2, 1)
                dve.wait_ge(s_hi, 1)
                nc.vector.tensor_tensor(winL[:, :, :], winT, winH[:, :, :].bitcast(f32), ALU.subtract)
                dve.wait_ge(s_hi, 2)
                nc.vector.tensor_tensor(w1L[:, :, :, :], w1f, w1H[:, :, :, :].bitcast(f32), ALU.subtract)
                dve.wait_ge(s_bias, 1)
                nc.vector.tensor_copy(bqkv[:, :, :], misc[:, 128:128 + 6 * B].rearrange("p (m b) -> p m b", m=6))
                dve.wait_ge(s_b1T, 1)
                nc.vector.tensor_tensor(b1.rearrange("p b m -> p m b"), misc[:, 192:192 + NE * B].rearrange("p (m b) -> p m b", m=NE),
                                        b1T.unsqueeze(2).to_broadcast([P, NE, B]), ALU.add)
                nc.vector.tensor_scalar(blog[:, :], misc[0:E, 320:320 + B], eb[0:E, :], None, ALU.add)
                dve.wait_ge(in_r2, 8 * 16)
                nc.vector.tensor_copy(r2[:, :], r2f[0:SPL, :]).then_inc(s_r2, 1)
                dve.wait_ge(s_r2, 1)
                nc.vector.tensor_tensor(r2l[0:SPL, :], r2f[0:SPL, :], r2[:, :].bitcast(f32), ALU.subtract).then_inc(s_r2, 1)
                nc.vector.tensor_scalar(r2h[0:SPL, :], r2[:, :].bitcast(f32), cv["rowmask"][0:SPL, 0:1], None,
                                        ALU.mult).then_inc(s_r2, 1)
                dve.wait_ge(s_r2, 3)
                nc.vector.scalar_tensor_tensor(out=r2[:, :], in0=r2l[0:SPL, :], scalar=cv["rowmask"][0:SPL, 1:2],
                                               in1=r2h[0:SPL, :], op0=ALU.mult, op1=ALU.add).then_inc(s_r2, 1)
                nc.vector.tensor_copy(cfsel[:, :, :], cfself[0:SPL // 2, :].rearrange("p (e m) -> p e m", e=E)).then_inc(s_r2, 1)
                dve.wait_ge(s_r2, 5)
                dve.wait_ge(in_w2, 32)

            @block.tensor
            def _(pe):
                pe.wait_ge(in_const, 32)
                pe.wait_ge(in_small, 5 * 16)
                pe.wait_ge(s_silu, 1)
                for k in range(KD):
                    nc.tensor.transpose(tr[0][:, k * B:(k + 1) * B], silu_c[0:B, k * P:(k + 1) * P], ident[0:B, 0:B])
                    nc.tensor.transpose(tr[0][:, 64 + k * E:64 + (k + 1) * E], rt_rows[0:E, k * P:(k + 1) * P],
                                        ident[0:E, 0:E])
                nc.tensor.transpose(tr[0][:, 128:128 + NE], b1_rows[0:NE, :], ident[0:NE, 0:NE]).then_inc(s_tr, 1)
                pe.wait_ge(in_win, 16)
                for m in range(6):
                    if m >= 2:
                        pe.wait_ge(s_winT, m - 1)
                    for k in range(KD):
                        last = nc.tensor.transpose(ring[m % 2][:, k * P:(k + 1) * P], win_rows[:, m, k * P:(k + 1) * P],
                                                   ident)
                    last.then_inc(s_tr, 1)
                pe.wait_ge(in_wout, 16)
                for m in range(2):
                    pe.wait_ge(s_winT, 5 + m)
                    for k in range(KD):
                        last = nc.tensor.transpose(ring[m % 2][:, k * P:(k + 1) * P], wout_rows[:, m, k * P:(k + 1) * P],
                                                   ident)
                    last.then_inc(s_tr, 1)
                pe.wait_ge(in_wmod, 16)
                pe.wait_ge(s_scT, 1)
                for v, col in enumerate((0, 1, 3, 4)):
                    for ch in range(KD):
                        o = (v * KD + ch) * B
                        for k in range(KD):
                            last = nc.tensor.matmul(misc[:, o:o + B], wmod[:, k, col * D + ch * P:col * D + (ch + 1) * P],
                                                    scT[:, k], start=(k == 0), stop=(k == KD - 1))
                last.then_inc(s_modps, 1)
                gcols = wmod.rearrange("p k (s n) -> p k s n", s=2)[:, :, :, 2 * D:3 * D]
                for k in range(KD):
                    last = nc.tensor.matmul(acc[0][0:B], scT[:, k], gcols[:, k], start=(k == 0), stop=(k == KD - 1))
                last.then_inc(s_gps, 1)
                pe.wait_ge(s_mods, 1)
                pe.wait_ge(s_winT, 6)
                pe.wait_ge(in_w1, 32)
                pe.wait_ge(s_rtT, 1)
                for m in range(6):
                    for k in range(KD):
                        nc.tensor.matmul(misc[:, 128 + m * B:128 + (m + 1) * B], winT[:, k, m * P:(m + 1) * P],
                                         mods[:, 0, k], start=(k == 0), stop=(k == KD - 1))
                for e in range(NE):
                    for k in range(KD):
                        nc.tensor.matmul(misc[:, 192 + e * B:192 + (e + 1) * B], w1f[:, e, k], mods[:, 2, k],
                                         start=(k == 0), stop=(k == KD - 1))
                for k in range(KD):
                    last = nc.tensor.matmul(misc[0:E, 320:320 + B], rtF[:, k], mods[:, 2, k],
                                            start=(k == 0), stop=(k == KD - 1))
                last.then_inc(s_bias, 1)

        x_loaded = [sem(f"x_loaded{p}") for p in range(CB)]
        stored = [sem(f"stored{p}") for p in range(CB)]
        stats_ready = [sem(f"stats{n}_ready") for n in range(2)]
        mv_steps = [sem(f"mean_var{n}_steps") for n in range(2)]
        rstd_ready = [sem(f"rstd{n}_ready") for n in range(2)]
        norm_ready = [sem(f"normalised{n}") for n in range(2)]
        transposed = [sem(f"transposed{n}") for n in range(2)]
        high_ready = [sem(f"high{n}_ready") for n in range(2)]
        low_ready = [sem(f"low{n}_ready") for n in range(2)]
        ring_filled, ring_copied = sem("ring_filled"), sem("ring_copied")
        clipped = sem("clipped")
        squares = sem("squares")
        even_scaled = sem("q_even_scaled")
        odd_ready = sem("odd_ready")
        weighted = sem("values_weighted")
        scanned = sem("prefix_sums")
        carried, kcarried = sem("carried"), sem("head_sums_carried")
        products = sem("order_products")
        added = sem("orders_added")
        numerator = sem("numerator")
        summed = sem("head_sums")
        ksum_ready, prod_ready = sem("key_prefix_sums"), sem("denominator_products")
        den_ready, den_eps, den_inv = sem("denominators"), sem("denominators_eps"), sem("denominators_inverse")
        inv_spread = sem("inverse_spread")
        attn_ready = sem("attention_ready")
        projected = sem("projected")
        gated_ready = sem("gated")
        x1_ready = sem("x1_ready")
        logits_ready, logT_ready, log_tok = sem("logits"), sem("logits_copied"), sem("logits_by_token")
        log_parts = sem("logit_parts")
        exp_ready, inv2_ready = sem("exp_ready"), sem("inverse_of_2_plus_u")
        score_steps, rank_steps = sem("score_steps"), sem("rank_steps")
        split_steps = sem("split_steps")
        split_T, cf_ready = sem("combine_transposed"), sem("combine_rows")
        cfb_ready, hidw_ready = sem("combine_spread"), sem("hidden_weighted")
        expert_done = sem("expert_done")
        ffn_gated, fin_ready = sem("ffn_gated"), sem("output_ready")
        NSCORE, NRANK, NSPLIT, NMV = 19, 7, 7, 9

        b1_row = sem("expert_biases_of_row")
        gate_loaded = [sem("ga_loaded"), sem("gb_loaded")]
        x_v = x_d.rearrange("b (c t p) d -> b c p t d", c=CB, p=P)
        o_v = out_d.rearrange("b (c t p) d -> b c p t d", c=CB, p=P)

        ALL = dict(norm=True, qkv=True, attn=True, second=True, ffn=True)

        def some(*names):
            return {k: k in names for k in ALL}

        FIRST = [(0, 0, some("norm", "qkv", "attn")), (0, 1, some("norm", "qkv", "attn", "second"))]
        LAST = [(B - 1, 0, some("qkv", "attn", "second", "ffn")), (B - 1, 1, some("attn", "second", "ffn")),
                (B, 0, some("second", "ffn")), (B, 1, some("ffn"))]
        USES = 6 + NE

        def number(i, p):
            return CB * i + p

        def later(i, p, n):
            return i + (p + n) // CB, (p + n) % CB

        def ring_at(i, p, st):
            if st["ffn"]:
                n = USES * CB * i + USES * p - 12
                if isinstance(i, int) and i == B:
                    n = USES * (B * CB - 1) - 12 + NE * (p + 1)
                bank = n % 2 if isinstance(i, int) else p % 2
            else:
                n, bank = 6 * (1 + number(i, p)), 0
            return (n, bank), (n + 6 * st["qkv"], bank)

        def ge(eng, s, value):
            if not isinstance(value, int) or value > 0:
                eng.wait_ge(s, value)

        def xin_of(i, p):
            if isinstance(i, int):
                return xin[:, CB * (i % 2) + p]
            return xin[:, bass.ds(CB * (i % 2) + p, 1)].rearrange("p a t d -> p (a t) d")

        def col(t, i):
            return t[:, i:i + 1] if isinstance(i, int) else t[:, bass.ds(i, 1)]

        def gate(which):
            return gates[:, which:which + 1].to_broadcast([P, 2, D])

        def f(n):
            return feat[:, n]

        block = ctx.enter_context(nc.Block())

        @block.sync
        def _(sp):
            def load(i, p):
                ge(sp, x_loaded[p], 16 * i)
                sp.dma_start(xin_of(i, p), x_v[i, p]).then_inc(x_loaded[p], 16)

            def store(i, p):
                sp.wait_ge(fin_ready, 2 * number(i, p) + 2)
                sp.dma_start(o_v[i, p], fin[:, :, :]).then_inc(stored[p], 16)

            def load_gate(i, which):
                sp.dma_start(gates[:, which], gate_rows[i, which * D:(which + 1) * D].partition_broadcast(P)) \
                    .then_inc(gate_loaded[which], 16)

            def step(i, p, stores, loads):
                if p == 0:
                    if loads or i < B:
                        if not isinstance(i, int) or i:
                            sp.wait_ge(x1_ready, 2 * number(i, 0))
                        load_gate(i, 0)
                    if stores:
                        load_gate(i - 1, 1)
                if stores:
                    store(i - 1, p)
                if loads:
                    sp.wait_ge(x1_ready, 2 * number(i, p) + 2)
                    load(i + 2, p)

            for c in range(XS):
                load(c // CB, c % CB)
            for p in range(CB):
                step(0, p, False, True)
            with sp.Fori(1, B - 2) as i:
                for p in range(CB):
                    step(i, p, True, True)
            for i in (B - 2, B - 1, B):
                for p in range(CB):
                    step(i, p, True, False)
            for p in range(CB):
                sp.wait_ge(stored[p], 16 * B)

        @block.gpsimd
        def _(pool):
            g = nc.gpsimd

            def k_(what, n):
                at = PC.index(what)
                return pool_c[:, at:at + 1].to_broadcast([P, n])

            def inv_std(n, i, p):
                c = number(i, p)
                pool.wait_ge(stats_ready[n], c + 1)
                ge(pool, norm_ready[n], c)
                m0, m1, s0, s1 = (stats[:, n, :, k] for k in (1, 4, 2, 5))
                t = lambda k: ms[:, n, k]
                g.tensor_tensor(t(0), m0, m1, ALU.add).then_inc(mv_steps[n], 1)
                g.tensor_tensor(t(1), m0, m1, ALU.subtract).then_inc(mv_steps[n], 1)
                g.tensor_tensor(t(2), s0, s1, ALU.add).then_inc(mv_steps[n], 1)
                pool.wait_ge(mv_steps[n], NMV * c + 3)
                g.tensor_tensor(t(3), t(0), k_("half", NT), ALU.mult).then_inc(mv_steps[n], 1)
                g.tensor_tensor(t(4), t(1), k_("half", NT), ALU.mult).then_inc(mv_steps[n], 1)
                g.tensor_tensor(t(5), t(2), k_("1/D", NT), ALU.mult).then_inc(mv_steps[n], 1)
                pool.wait_ge(mv_steps[n], NMV * c + 6)
                g.tensor_tensor(t(6), t(4), t(4), ALU.mult).then_inc(mv_steps[n], 1)
                g.tensor_tensor(t(7), t(5), k_("eps", NT), ALU.add).then_inc(mv_steps[n], 1)
                pool.wait_ge(mv_steps[n], NMV * c + 8)
                g.tensor_tensor(t(8), t(6), t(7), ALU.add).then_inc(mv_steps[n], 1)
                pool.wait_ge(mv_steps[n], NMV * c + 9)
                g.tensor_tensor(t(9), t(8), k_("-half", NT), ALU.pow).then_inc(rstd_ready[n], 1)

            def add_orders(i, p):
                c = number(i, p)
                pool.wait_ge(products, ND * c + 2)
                g.tensor_tensor(f(W), f(W), f(W + 1), ALU.add).then_inc(added, 1)
                pool.wait_ge(products, ND * c + 4)
                g.tensor_tensor(f(W + 2), f(W + 2), f(W + 3), ALU.add).then_inc(added, 1)
                pool.wait_ge(added, 3 * c + 2)
                g.tensor_tensor(f(W), f(W), f(W + 2), ALU.add).then_inc(added, 1)

            def scores(i, p):
                c = number(i, p)
                n = [0]

                def then(ins):
                    n[0] += 1
                    ins.then_inc(score_steps, 1)
                    pool.wait_ge(score_steps, NSCORE * c + n[0])

                r = lambda k: route[:, k]
                pool.wait_ge(inv2_ready, 2 * c + 2)
                then(g.tensor_tensor(r(Z), r(U), r(RC), ALU.mult))
                then(g.tensor_tensor(r(Z2), r(Z), r(Z), ALU.mult))
                then(g.tensor_tensor(r(PL), r(Z2), k_(15, NT * E), ALU.mult))
                for m in (13, 11, 9, 7, 5, 3):
                    then(g.tensor_tensor(r(PL), r(PL), k_(m, NT * E), ALU.add))
                    then(g.tensor_tensor(r(PL), r(PL), r(Z2), ALU.mult))
                then(g.tensor_tensor(r(PL), r(PL), k_(1, NT * E), ALU.add))
                then(g.tensor_tensor(r(PL), r(PL), r(Z), ALU.mult))
                pool.wait_ge(log_parts, 3 * c + 3)
                then(g.tensor_tensor(r(SP), r(PL), r(MX), ALU.add))
                then(g.tensor_tensor(r(AC), r(SP), k_("half", NT * E), ALU.pow))
                assert n[0] == NSCORE, n

            def split_weights(i, p):
                c = number(i, p)
                n = [0]

                def then(ins):
                    n[0] += 1
                    ins.then_inc(split_steps, 1)
                    pool.wait_ge(split_steps, NSPLIT * c + n[0])

                pool.wait_ge(rank_steps, NRANK * c + NRANK)
                ge(pool, split_T, c)
                cf = route[:, CF].rearrange("p (t e) -> p t e", t=NT)

                def copy(out, in_):
                    ones = k_("one", NT * out.shape[2]).rearrange("p (t e) -> p t e", t=NT)
                    then(g.tensor_tensor(out, in_, ones, ALU.mult))

                copy(part[:, 0], cf)
                then(g.tensor_tensor(rest[:, :, :], cf, part[:, 0], ALU.subtract))
                copy(part[:, 1], rest[:, :, :])
                then(g.tensor_tensor(split[:, :, 2 * E:3 * E], rest[:, :, :], part[:, 1], ALU.subtract))
                copy(split[:, :, 0:E], part[:, 0])
                copy(split[:, :, E:2 * E], part[:, 1])
                h = SPL // 2
                copy(split[:, :, h:h + 3 * E], split[:, :, 0:3 * E])
                assert n[0] == NSPLIT, n

            def step(i, p, st):
                if st["second"]:
                    scores(*later(i, p, -1))
                if st["attn"]:
                    add_orders(i, p)
                if st["second"]:
                    split_weights(*later(i, p, -1))
                if st["attn"]:
                    inv_std(1, i, p)
                if st["norm"]:
                    inv_std(0, *later(i, p, 2))

            inv_std(0, 0, 0)
            inv_std(0, 0, 1)
            for i, p, st in FIRST:
                step(i, p, st)
            with pool.Fori(1, B - 1) as i:
                for p in range(CB):
                    step(i, p, ALL)
            for i, p, st in LAST:
                step(i, p, st)

        @block.scalar
        def _(act):
            a = nc.scalar

            def highs(n, i, p):
                c = number(i, p)
                for k in range(KD):
                    act.wait_ge(transposed[n], 2 * c + k + 1)
                    out = n1H[:, k] if n == 0 else n2H[:, p, k]
                    a.activation(out, tr[k][:, :], ACT.Copy,
                                 scale=col(mods[:, 2 * n + 1, k], i)).then_inc(high_ready[n], 1)

            def copy_qkv(i, p, at, bank, m):
                act.wait_ge(ring_filled, at + m + 1)
                if m >= 4:
                    ge(act, weighted, ND * number(i, p))
                a.activation(feat[:, (K0 + p, Q0 + p, V0)[m // 2], m % 2], ring[(bank + m) % 2][:, :], ACT.Identity,
                             bias=col(bqkv[:, (2, 3, 0, 1, 4, 5)[m]], i)).then_inc(ring_copied, 1)

            def square(i, p, q, which):
                c = number(i, p)
                x, s, qa, qb = ((K0 + p, KS, KA, KT5), (Q0 + p, QSQ, QA, QT5))[q]
                if which == 0:
                    act.wait_ge(clipped, 2 * c + q + 1)
                    if q == 0:
                        ge(act, summed, 2 * c)
                        ge(act, products, ND * c)
                    a.activation(f(s), f(x), ACT.Square).then_inc(squares, 1)
                else:
                    act.wait_ge(squares, 6 * c + 3 * q + 1)
                    a.activation(f((qa, qb)[which - 1]), f(s), ACT.Square,
                                 bias=cv["biases"][:, which - 1:which]).then_inc(squares, 1)

            def scale_even(i, p):
                c = number(i, p)
                act.wait_ge(squares, 6 * c + 6)
                act.wait_ge(odd_ready, 4 * c + 3)
                a.activation(f(QSQ), f(QSQ), ACT.Copy, scale=GAMMA[1], bias=-0.5 * GAMMA[1]).then_inc(even_scaled, 1)
                a.activation(f(QA), f(QA), ACT.Copy, scale=GAMMA[3], bias=-0.125 * GAMMA[3]).then_inc(even_scaled, 1)

            def row_biases(i, at):
                act.wait_ge(ring_copied, at)
                a.activation(b1row[:, :], b1[:, i] if isinstance(i, int) else b1[:, bass.ds(i, 1)].rearrange("p a e -> p (a e)"),
                             ACT.Copy).then_inc(b1_row, 1)

            def hidden(i, p, at, bank, e):
                act.wait_ge(ring_filled, at + e + 1)
                if e == 0 and p == 0:
                    act.wait_ge(b1_row, i + 1)
                a.activation(hid[:, e % NG], ring[(bank + e) % 2][:, :], ACT.Silu,
                             bias=b1row[:, e:e + 1]).then_inc(ring_copied, 1)

            def copy_logits(i, p):
                c = number(i, p)
                act.wait_ge(logits_ready, c + 1)
                ge(act, log_tok, c)
                a.activation(logT[0:E, :], misc[0:E, :], ACT.Identity, bias=col(blog, i)).then_inc(logT_ready, 1)

            def exps(i, p):
                c = number(i, p)
                act.wait_ge(log_parts, 3 * c + 2)
                ge(act, score_steps, NSCORE * c)
                a.activation(route[:, U], route[:, NEG], ACT.Exp).then_inc(exp_ready, 1)

            def combine_rows(i, p):
                c = number(i, p)
                act.wait_ge(split_T, c + 1)
                a.activation(cfB[:, :], misc[0:SPL // 2, :], ACT.Copy).then_inc(cf_ready, 1)
                a.activation(cfR[:, :], misc[0:SPL, :], ACT.Copy).then_inc(cf_ready, 1)

            def step(i, p, st):
                (qa, qbank), (fa, fbank) = ring_at(i, p, st)
                nxt, prev, exp = later(i, p, 1), later(i, p, -1), later(i, p, -2)
                if st["qkv"]:
                    highs(0, *nxt)
                for m in range(6):
                    if st["qkv"]:
                        copy_qkv(*nxt, qa, qbank, m)
                    if st["attn"]:
                        square(i, p, m // 3, m % 3)
                if st["second"]:
                    highs(1, *prev)
                    copy_logits(*prev)
                if st["attn"]:
                    scale_even(i, p)
                if st["ffn"]:
                    if exp[1] == 0:
                        row_biases(exp[0], fa)
                    for e in range(3):
                        hidden(*exp, fa, fbank, e)
                if st["second"]:
                    exps(*prev)
                if st["ffn"]:
                    for e in range(3, NE):
                        hidden(*exp, fa, fbank, e)
                if st["second"]:
                    combine_rows(*prev)

            highs(0, 0, 0)
            for m in range(6):
                copy_qkv(0, 0, 0, 0, m)
            for i, p, st in FIRST:
                step(i, p, st)
            with act.Fori(1, B - 1) as i:
                for p in range(CB):
                    step(i, p, ALL)
            for i, p, st in LAST:
                step(i, p, st)

        @block.vector
        def _(dve):
            v = nc.vector

            def token_stats(n, i, p):
                c = number(i, p)
                ge(dve, rstd_ready[n], c)
                if n == 0:
                    dve.wait_ge(x_loaded[p], 16 * (i + 1))
                src = xin_of(i, p) if n == 0 else x1[:, p]
                for t in range(NT):
                    if n == 1:
                        dve.wait_ge(x1_ready, 2 * c + 1 + t // 2)
                    last = v.bn_stats(stats[:, n, t], src[:, t])
                last.then_inc(stats_ready[n], 1)

            def normalise(n, i, p):
                c = number(i, p)
                dve.wait_ge(rstd_ready[n], c + 1)
                ge(dve, transposed[n], 2 * c)
                src = xin_of(i, p) if n == 0 else x1[:, p]
                for t in range(NT):
                    last = v.tensor_scalar(ntok[:, n, t], src[:, t], ms[:, n, 3, t:t + 1], ms[:, n, 9, t:t + 1],
                                           ALU.subtract, ALU.mult)
                last.then_inc(norm_ready[n], 1)

            def lows(n, i, p):
                c = number(i, p)
                for k in range(KD):
                    dve.wait_ge(high_ready[n], 2 * c + k + 1)
                    hi = n1H[:, k] if n == 0 else n2H[:, p, k]
                    out = n1L[:, k] if n == 0 else n2L[:, p, k]
                    v.scalar_tensor_tensor(out=out, in0=tr[k][:, :], scalar=col(mods[:, 2 * n + 1, k], i),
                                           in1=hi.bitcast(f32), op0=ALU.mult, op1=ALU.subtract).then_inc(low_ready[n], 1)

            def clip(i, p, at, q):
                dve.wait_ge(ring_copied, at + 2 * q + 2)
                x = (K0, Q0)[q] + p
                v.tensor_scalar(f(x), f(x), CLIP, -CLIP, ALU.min, ALU.max).then_inc(clipped, 1)

            def odd(i, p, q):
                c = number(i, p)
                x, s, t3, t5 = ((K0 + p, KS, KT3, KT5), (Q0 + p, QSQ, QT3, QT5))[q]
                dve.wait_ge(squares, 6 * c + 3 * q + 3)
                if q == 0:
                    ge(dve, summed, 2 * c)
                v.scalar_tensor_tensor(out=f(t3), in0=f(s), scalar=-0.75, in1=f(x),
                                       op0=ALU.add, op1=ALU.mult).then_inc(odd_ready, 1)
                v.scalar_tensor_tensor(out=f(t5), in0=f(t5), scalar=-0.078125, in1=f(x),
                                       op0=ALU.add, op1=ALU.mult).then_inc(odd_ready, 1)

            ORDERS = (0, 1, 3, 2, 4)

            def weigh(i, p, j):
                c = number(i, p)
                n = ORDERS[j]
                val = f(V0)
                if j == 1:
                    ge(dve, projected, 2 * c)
                if j == 0:
                    v.tensor_tensor(f(W), f(K0 + p), val, ALU.mult).then_inc(weighted, 1)
                elif n == 1 or n == 3:
                    v.scalar_tensor_tensor(out=f(W + n), in0=f(KS if n == 1 else KA), scalar=-0.5 if n == 1 else -0.125,
                                           in1=val, op0=ALU.add, op1=ALU.mult).then_inc(weighted, 1)
                else:
                    dve.wait_ge(odd_ready, 4 * c + n // 2)
                    v.tensor_tensor(f(W + n), f(KT3 if n == 2 else KT5), val, ALU.mult).then_inc(weighted, 1)

            def prefix(i, p, j):
                c = number(i, p)
                n = ORDERS[j]
                dve.wait_ge(weighted, ND * c + j + 1)
                if p:
                    dve.wait_ge(carried, i + 1)
                for h in range(KD):
                    last = v.tensor_tensor_scan(feat[:, W + n, h], zero[:, 0:1].to_broadcast([P, CT]), feat[:, W + n, h],
                                                carry[:, n, h:h + 1] if p else 0.0, ALU.add, ALU.add)
                last.then_inc(scanned, 1)

            def carry_over(i, p):
                if p == 0:
                    dve.wait_ge(scanned, ND * number(i, p) + ND)
                    v.tensor_copy(carry[:, :, :], feat[:, W:W + ND, :, CT - 1]).then_inc(carried, 1)

            def order_product(i, p, n):
                c = number(i, p)
                w = f(W + n)
                if n == 0:
                    dve.wait_ge(scanned, ND * c + ND)
                    if p == 0:
                        dve.wait_ge(carried, i + 1)
                if n in (1, 3):
                    dve.wait_ge(even_scaled, 2 * c + (n + 1) // 2)
                    v.tensor_tensor(w, w, f(QSQ if n == 1 else QA), ALU.mult).then_inc(products, 1)
                else:
                    if n:
                        dve.wait_ge(odd_ready, 4 * c + 2 + n // 2)
                    v.scalar_tensor_tensor(out=w, in0=w, scalar=GAMMA[n], in1=f((Q0 + p, 0, QT3, 0, QT5)[n]),
                                           op0=ALU.mult, op1=ALU.mult).then_inc(products, 1)

            def den_products(i, p):
                c = number(i, p)
                dve.wait_ge(summed, 2 * c + 1)
                if p:
                    dve.wait_ge(kcarried, i + 1)
                v.tensor_tensor_scan(prod[:, :], cv["kshift"].to_broadcast([P, CT]), tr[0][:, :],
                                     kcarry[:, :] if p else 0.0, ALU.add, ALU.add).then_inc(ksum_ready, 1)
                dve.wait_ge(summed, 2 * c + 2)
                dve.wait_ge(ksum_ready, c + 1)
                if p == 0:
                    v.tensor_copy(kcarry[:, :], prod[:, CT - 1:CT]).then_inc(kcarried, 1)
                    dve.wait_ge(kcarried, i + 1)
                v.tensor_tensor(prod[:, :], tr[1][:, :], prod[:, :], ALU.mult).then_inc(prod_ready, 1)

            def invert(i, p):
                c = number(i, p)
                dve.wait_ge(den_ready, c + 1)
                v.tensor_scalar(denom[:, 0], misc[:, 0:P], EPS_DEN, None, ALU.add).then_inc(den_eps, 1)
                dve.wait_ge(den_eps, c + 1)
                v.reciprocal(denom[:, 1], denom[:, 0]).then_inc(den_inv, 1)

            def finish_numerator(i, p):
                dve.wait_ge(added, 3 * number(i, p) + 3)
                dve.wait_ge(products, ND * number(i, p) + ND)
                v.tensor_tensor(f(W), f(W), f(W + 4), ALU.add).then_inc(numerator, 1)

            def divide(i, p):
                c = number(i, p)
                dve.wait_ge(numerator, c + 1)
                for k in range(KD):
                    dve.wait_ge(inv_spread, 2 * c + k + 1)
                    v.tensor_tensor(attn[:, k], feat[:, W, k], tr[k][:, :], ALU.mult).then_inc(attn_ready, 1)

            def residual(i, p):
                c = number(i, p)
                dve.wait_ge(gate_loaded[0], 16 * (i + 1))
                for h in range(2):
                    dve.wait_ge(projected, 2 * c + h + 1)
                    v.tensor_tensor(gated[:, h], tr[h][:, :].rearrange("p (t d) -> p t d", t=2), gate(0),
                                    ALU.mult).then_inc(gated_ready, 1)
                ge(dve, fin_ready, 2 * c - 2)
                for h in range(2):
                    dve.wait_ge(gated_ready, 2 * c + h + 1)
                    v.tensor_tensor(x1[:, p, 2 * h:2 * h + 2], gated[:, h], xin_of(i, p)[:, 2 * h:2 * h + 2],
                                    ALU.add).then_inc(x1_ready, 1)

            def logit_parts(i, p):
                c = number(i, p)
                dve.wait_ge(log_tok, c + 1)
                ge(dve, score_steps, NSCORE * c)
                v.tensor_copy(route[:, L_].rearrange("p (t e) -> p t e", t=NT),
                              misc.rearrange("p (t e) -> p t e", t=NT)[:, :, 0:E]).then_inc(log_parts, 1)
                dve.wait_ge(log_parts, 3 * c + 1)
                v.scalar_tensor_tensor(out=route[:, NEG], in0=route[:, L_], scalar=-1.0, in1=route[:, L_],
                                       op0=ALU.mult, op1=ALU.min).then_inc(log_parts, 1)
                v.tensor_scalar(route[:, MX], route[:, L_], 0.0, None, ALU.max).then_inc(log_parts, 1)

            def inverse2(i, p):
                c = number(i, p)
                dve.wait_ge(exp_ready, c + 1)
                v.tensor_scalar(route[:, DN], route[:, U], 2.0, None, ALU.add).then_inc(inv2_ready, 1)
                dve.wait_ge(inv2_ready, 2 * c + 1)
                v.reciprocal(route[:, RC], route[:, DN]).then_inc(inv2_ready, 1)

            def choose(i, p):
                c = number(i, p)
                at = NRANK * c
                dve.wait_ge(score_steps, NSCORE * c + NSCORE)
                s = route[:, AC].rearrange("p (t e) -> p t e", t=NT)
                others = s.unsqueeze(2).to_broadcast([P, NT, E, E])
                own = s.unsqueeze(3).to_broadcast([P, NT, E, E])
                v.tensor_tensor(pair[:, 0], others, own, ALU.is_ge).then_inc(rank_steps, 1)
                v.tensor_tensor(pair[:, 1], others, own, ALU.is_gt).then_inc(rank_steps, 1)
                dve.wait_ge(rank_steps, at + 1)
                g0, g1 = (pair[:, k].rearrange("p t e j -> p t (e j)") for k in range(2))
                v.tensor_tensor(g0, g0, before, ALU.mult).then_inc(rank_steps, 1)
                dve.wait_ge(rank_steps, at + 2)
                v.tensor_tensor(g1, g1, after, ALU.mult).then_inc(rank_steps, 1)
                dve.wait_ge(rank_steps, at + 4)
                v.tensor_tensor(pair[:, 0], pair[:, 0], pair[:, 1], ALU.add).then_inc(rank_steps, 1)
                dve.wait_ge(rank_steps, at + 5)
                v.tensor_reduce(rank[:, :], pair[:, 0].rearrange("p t e j -> p (t e) j"), AX.X,
                                ALU.add).then_inc(rank_steps, 1)
                dve.wait_ge(rank_steps, at + 6)
                ge(dve, split_steps, NSPLIT * c)
                v.scalar_tensor_tensor(out=route[:, CF], in0=rank[:, :], scalar=2.0, in1=route[:, AC],
                                       op0=ALU.is_lt, op1=ALU.mult).then_inc(rank_steps, 1)

            def weigh_hidden(i, p, at, e):
                c = number(i, p)
                dve.wait_ge(ring_copied, at + e + 1)
                dve.wait_ge(cfb_ready, E * c + e)
                v.tensor_tensor(hid[:, e % NG], hid[:, e % NG], cfb[:, :], ALU.mult).then_inc(hidw_ready, 1)

            def output(i, p):
                c = number(i, p)
                dve.wait_ge(expert_done, NE * c + NE)
                dve.wait_ge(gate_loaded[1], 16 * (i + 1))
                ge(dve, stored[1 - p], 16 * (i + p))
                for h in range(2):
                    v.tensor_tensor(fin[:, 2 * h:2 * h + 2], acc[h][:, :, :], gate(1), ALU.mult).then_inc(ffn_gated, 1)
                for h in range(2):
                    dve.wait_ge(ffn_gated, 2 * c + h + 1)
                    o = fin[:, 2 * h:2 * h + 2]
                    v.tensor_tensor(o, o, x1[:, p, 2 * h:2 * h + 2], ALU.add).then_inc(fin_ready, 1)

            def step(i, p, st):
                (qa, _), (fa, _) = ring_at(i, p, st)
                nxt, prev, exp = later(i, p, 1), later(i, p, -1), later(i, p, -2)
                attn_, ffn, second = st["attn"], st["ffn"], st["second"]

                def expert(e):
                    if ffn:
                        weigh_hidden(*exp, fa, e)

                if st["qkv"]:
                    lows(0, *nxt)
                if attn_:
                    odd(i, p, 0)
                    for j in range(ND):
                        weigh(i, p, j)
                if second:
                    lows(1, *prev)
                if attn_:
                    odd(i, p, 1)
                if second:
                    logit_parts(*prev)
                if attn_:
                    prefix(i, p, 0)
                expert(1)
                if attn_:
                    prefix(i, p, 1)
                    den_products(i, p)
                expert(2)
                if attn_:
                    prefix(i, p, 2)
                    prefix(i, p, 3)
                expert(3)
                if attn_:
                    prefix(i, p, 4)
                if second:
                    inverse2(*prev)
                if attn_:
                    carry_over(i, p)
                    invert(i, p)
                expert(4)
                if attn_:
                    order_product(i, p, 0)
                    order_product(i, p, 1)
                expert(5)
                if attn_:
                    for n in range(2, ND):
                        order_product(i, p, n)
                if second:
                    choose(*prev)
                expert(6)
                if st["qkv"]:
                    clip(*nxt, qa, 0)
                    clip(*nxt, qa, 1)
                expert(7)
                if attn_:
                    finish_numerator(i, p)
                    divide(i, p)
                expert(8)
                if ffn:
                    output(*exp)
                if attn_:
                    residual(i, p)
                    token_stats(1, i, p)
                if st["norm"]:
                    token_stats(0, *later(i, p, 2))
                if attn_:
                    normalise(1, i, p)
                if st["norm"]:
                    normalise(0, *later(i, p, 2))

            for c in range(2):
                token_stats(0, 0, c)
                normalise(0, 0, c)
                if c == 0:
                    lows(0, 0, 0)
                    clip(0, 0, 0, 0)
                    clip(0, 0, 0, 1)
            for i, p, st in FIRST:
                step(i, p, st)
            for p in range(CB):
                step(1, p, ALL)
            with dve.Fori(2, B - 1) as i:
                for p in range(CB):
                    step(i, p, ALL)
            for i, p, st in LAST:
                step(i, p, st)

        @block.tensor
        def _(pe):
            mm = nc.tensor.matmul

            def transposes(n, i, p, behind_norm=False):
                c = number(i, p)
                pe.wait_ge(norm_ready[n], c + 1)
                if behind_norm:
                    pe.wait_ge(low_ready[0], 2 * (c + 3))
                else:
                    ge(pe, gated_ready, 2 * (c - 1 if n == 0 else c + 1))
                for k in range(KD):
                    for t in range(NT):
                        last = nc.tensor.transpose(tr[k][:, t * P:(t + 1) * P], ntok[:, n, t, k * P:(k + 1) * P], ident)
                    last.then_inc(transposed[n], 1)

            def split_product(out, wH, wL, xH, xL):
                terms = [(wH[k], xH[k]) for k in range(KD)] + [(wH[k], xL[k]) for k in range(KD)] \
                    + [(wL[k], xH[k]) for k in range(KD)]
                for n, (w, x) in enumerate(terms):
                    last = mm(out, w, x, start=(n == 0), stop=(n == len(terms) - 1))
                return last

            halves = lambda t: [t[:, k] for k in range(KD)]

            def project(i, p, at, bank):
                c = number(i, p)
                pe.wait_ge(high_ready[0], 2 * c + 2)
                pe.wait_ge(low_ready[0], 2 * c + 2)
                for m in range(6):
                    ge(pe, ring_copied, at + m - 1)
                    w = (2, 3, 0, 1, 4, 5)[m]
                    cols = slice(w * P, (w + 1) * P)
                    split_product(ring[(bank + m) % 2][:, :], [winH[:, k, cols] for k in range(KD)],
                                  [winL[:, k, cols] for k in range(KD)], halves(n1H), halves(n1L)).then_inc(ring_filled, 1)

            def route_logits(i, p):
                c = number(i, p)
                pe.wait_ge(high_ready[1], 2 * c + 2)
                pe.wait_ge(low_ready[1], 2 * c + 2)
                ge(pe, cf_ready, 2 * c)
                pe.wait_ge(den_eps, c + 1)
                split_product(misc[0:E, :], halves(rtH), halves(rtL), halves(n2H[:, p]), halves(n2L[:, p])) \
                    .then_inc(logits_ready, 1)
                pe.wait_ge(logT_ready, c + 1)
                for t in range(NT):
                    last = nc.tensor.transpose(misc[:, t * P:(t + 1) * P], logT[:, t * P:(t + 1) * P], ident)
                last.then_inc(log_tok, 1)

            def head_sums(i, p, behind_second):
                c = number(i, p)
                if behind_second:
                    pe.wait_ge(low_ready[1], 2 * c)
                else:
                    pe.wait_ge(low_ready[0], 2 * (c + 2))
                for q in range(2):
                    srcs = ((K0 + p, KS, KT3, KA, KT5), (Q0 + p, QSQ, QT3, QA, QT5))[q]
                    pe.wait_ge(odd_ready, 4 * c + 2 * q + 2)
                    if q:
                        pe.wait_ge(even_scaled, 2 * c + 2)
                    order = [(0, 0), (1, 0), (2, 0), (3, 0), (0, 1), (1, 1), (2, 1), (3, 1), (4, 0), (4, 1)]
                    final = {0: (4, 0), 1: (4, 1), 2: (2, 1), 3: (3, 1)}
                    for n, h in order:
                        g_, r = ROWS[n, h]
                        last = mm(tr[q][g_ * QS:(g_ + 1) * QS, :],
                                  cv["headsum"][:, (r // HPH) * QS:(r // HPH + 1) * QS], feat[:, srcs[n], h],
                                  start=(n < 4 and h == 0), stop=(final[g_] == (n, h)))
                    last.then_inc(summed, 1)

            def denominators(i, p):
                c = number(i, p)
                pe.wait_ge(prod_ready, c + 1)
                ge(pe, log_parts, 3 * (c - 1) + 1)
                for t in range(NT):
                    last = mm(misc[t * QS:(t + 1) * QS, 0:P], cv["densum"],
                              prod[:, t * P:(t + 1) * P], start=True, stop=True)
                last.then_inc(den_ready, 1)

            def spread_inverse(i, p):
                c = number(i, p)
                pe.wait_ge(den_inv, c + 1)
                for k in range(KD):
                    for t in range(NT):
                        last = mm(tr[k][:, t * P:(t + 1) * P], cv["headsel"][:, (t * KD + k) * P:(t * KD + k + 1) * P], denom[:, 1],
                                  start=True, stop=True)
                    last.then_inc(inv_spread, 1)

            def project_out(i, p):
                c = number(i, p)
                pe.wait_ge(attn_ready, 2 * c + 2)
                for t in range(NT):
                    for k in range(KD):
                        last = mm(tr[t // 2][:, (t % 2) * D:(t % 2 + 1) * D], attn[:, k, t * P:(t + 1) * P], wo[:, k],
                                  start=(k == 0), stop=(k == KD - 1))
                    if t % 2:
                        last.then_inc(projected, 1)

            def combine_by_expert(i, p, behind_attn):
                c = number(i, p)
                pe.wait_ge(split_steps, NSPLIT * c + NSPLIT)
                if behind_attn:
                    pe.wait_ge(den_eps, c + 2)
                else:
                    pe.wait_ge(log_parts, 3 * c + 1)
                for t in range(NT):
                    last = nc.tensor.transpose(misc[:, t * P:(t + 1) * P], split[:, t], ident)
                last.then_inc(split_T, 1)

            def expert_up(i, p, at, bank, e):
                pe.wait_ge(ring_copied, at + e - 1)
                split_product(ring[(bank + e) % 2][:, :], halves(w1H[:, e]), halves(w1L[:, e]),
                              halves(n2H[:, p]), halves(n2L[:, p])).then_inc(ring_filled, 1)

            def spread_weights(i, p, e):
                mm(cfb[:, :], cfsel[:, e - 1], cfB[:, :], start=True, stop=True).then_inc(cfb_ready, 1)

            def second_biases(i, p):
                c = number(i, p)
                pe.wait_ge(cf_ready, 2 * c + 2)
                ge(pe, ffn_gated, 2 * c)
                for t in range(NT):
                    mm(acc[t // 2][:, t % 2], cfR[:, t * P:(t + 1) * P], r2[:, :], start=(t % 2 == 0), stop=False,
                       skip_group_check=True)

            def expert_down(i, p, at, e):
                c = number(i, p)
                if e == 0:
                    pe.wait_ge(ring_copied, at + 1)
                else:
                    pe.wait_ge(hidw_ready, E * c + e)
                if e < E:
                    spread_weights(i, p, e + 1)
                for t in range(NT):
                    last = mm(acc[t // 2][:, t % 2], hid[:, e % NG, t * P:(t + 1) * P], w2[:, e], start=False,
                              stop=(e == E), skip_group_check=True)
                last.then_inc(expert_done, 1)

            def step(i, p, st):
                (qa, qbank), (fa, fbank) = ring_at(i, p, st)
                nxt, prev, exp = later(i, p, 1), later(i, p, -1), later(i, p, -2)

                def expert(e):
                    if st["ffn"]:
                        if e + 2 < NE:
                            expert_up(*exp, fa, fbank, e + 2)
                        expert_down(*exp, fa, e)

                if st["qkv"]:
                    transposes(0, *nxt)
                    project(*nxt, qa, qbank)
                if st["second"]:
                    transposes(1, *prev, behind_norm=st["qkv"])
                    route_logits(*prev)
                if st["ffn"]:
                    second_biases(*exp)
                    expert_up(*exp, fa, fbank, 0)
                    expert_up(*exp, fa, fbank, 1)
                expert(0)
                if st["attn"]:
                    head_sums(i, p, st["second"])
                expert(1)
                expert(2)
                expert(3)
                if st["attn"]:
                    denominators(i, p)
                expert(4)
                expert(5)
                if st["attn"]:
                    spread_inverse(i, p)
                expert(6)
                expert(7)
                if st["attn"]:
                    project_out(i, p)
                expert(8)
                if st["second"]:
                    combine_by_expert(*prev, st["attn"])

            transposes(0, 0, 0)
            project(0, 0, 0, 0)
            for i, p, st in FIRST:
                step(i, p, st)
            for p in range(CB):
                step(1, p, ALL)
            with pe.Fori(2, B - 1) as i:
                for p in range(CB):
                    step(i, p, ALL)
            for i, p, st in LAST:
                step(i, p, st)


_INS = ['L0_attn_x', 'L0_attn_W_in', 'L0_attn_W_out', 'L0_ffn_routing_W', 'L0_ffn_expert_bias', 'L0_ffn_sW1',
        'L0_ffn_sb1', 'L0_ffn_sW2', 'L0_ffn_sb2', 'L0_ffn_rW1', 'L0_ffn_rb1', 'L0_ffn_rW2', 'L0_ffn_rb2', 'L0_c',
        'L0_wmod']


def kernel(**inputs):
    import concourse.bacc as _bacc
    from concourse.bass_utils import run_bass_kernel_spmd as _run

    nc = _bacc.Bacc("TRN2", target_bir_lowering=False, num_devices=1)
    arrays, args = {}, []
    for name in _INS:
        a = np.ascontiguousarray(inputs[name])
        arrays[f"in_{name}"] = a
        args.append(nc.dram_tensor(f"in_{name}", a.shape, mybir.dt.from_np(a.dtype), kind="ExternalInput").ap())
    a = constants()
    arrays["in_constants"] = a
    args.append(nc.dram_tensor("in_constants", a.shape, mybir.dt.float32, kind="ExternalInput").ap())
    args.append(nc.dram_tensor("out", (B, S, D), mybir.dt.float32, kind="ExternalOutput").ap())
    build(nc, *args)
    r = _run(nc, [arrays], core_ids=[0])
    return r.results[0]["out"]
```

```python
import concourse.bass as bass
from concourse import mybir
from contextlib import ExitStack
import numpy as np

B, S, D = 8, 1024, 256
P = 128
KD = D // P
H, DH = 16, 16
E = 8
NE = E + 1
HID = 4 * D // E
CT = 512
NT = CT // P
CB = S // CT
NC = B * CB
ORDER = 6
ND = ORDER - 1
CLIP = 1.0 - 1e-6
HPH = H // KD
QS = 32
SPL = 2 * (3 * E + 1)
XS = 4


def chebyshev_weights():
    j = np.arange(ORDER, dtype=np.float32)
    alpha = (j + 1.0) ** (-1.5)
    tail = np.flip(np.cumsum(np.flip(alpha)))
    beta = np.concatenate([np.zeros(1, np.float32), tail[1:].astype(np.float32), np.zeros(ORDER - 1, np.float32)])
    beta = (beta / beta.sum()).astype(np.float32)
    return [float(beta[n]) * 4.0 ** (n - 1) for n in range(1, ORDER)]


GAMMA = chebyshev_weights()


def head_rows():
    rows = {}
    for n in range(4):
        rows[n, 0], rows[n, 1] = (n, 0), (n, 2 * HPH)
    rows[4, 0], rows[4, 1] = (0, HPH), (1, 3 * HPH)
    return rows


ROWS = head_rows()

CONSTS = {"ident": P, "headsum": 4 * QS, "densum": QS, "headsel": NT * KD * P, "kshift": 1, "rowmask": 2,
          "biases": 2, "before": E * E, "after": E * E, "cfsel": E * P}


def constants():
    c = {k: np.zeros((P, n), np.float32) for k, n in CONSTS.items()}
    c["ident"] = np.eye(P, dtype=np.float32)
    ch = np.arange(P)
    for o in range(4):
        c["headsum"][ch, o * QS + o * HPH + ch // DH] = 1.0
    for (n, half), (g, r) in ROWS.items():
        for h in range(HPH):
            row = g * QS + r + h
            w = GAMMA[n] if n in (0, 2, 4) else 1.0
            for copy in range(QS // H):
                c["densum"][row, copy * H + half * HPH + h] = w
            c["kshift"][row, 0] = {1: -0.5 * DH, 3: -0.125 * DH}.get(n, 0.0)
    for q in range(4):
        for half in range(KD):
            c["headsel"][q * QS + half * HPH + ch // DH, (q * KD + half) * P + ch] = 1.0
    c["rowmask"][:SPL // 2, 0] = 1.0
    c["rowmask"][SPL // 2:SPL, 1] = 1.0
    c["biases"][:, 0], c["biases"][:, 1] = -0.5, -0.625
    e, j = np.meshgrid(np.arange(E), np.arange(E), indexing="ij")
    c["before"][:] = (j < e).astype(np.float32).ravel()
    c["after"][:] = (j > e).astype(np.float32).ravel()
    for x in range(E):
        for part in range(3):
            c["cfsel"][part * E + x, x * P:(x + 1) * P] = 1.0
    return np.concatenate([c[k] for k in CONSTS], axis=1)


def build(nc, x_d, w_in_d, w_out_d, rout_d, ebias_d, sw1_d, sb1_d, sw2_d, sb2_d,
          rw1_d, rb1_d, rw2_d, rb2_d, c_d, wmod_d, const_d, out_d):
    f32, f32r, bf16 = mybir.dt.float32, mybir.dt.float32r, mybir.dt.bfloat16
    ALU = mybir.AluOpType
    ACT = mybir.ActivationFunctionType
    AX = mybir.AxisListType
    EPS_LN, EPS_DEN = 1e-5, 1e-7

    ctx = ExitStack()
    with ctx:
        def sb(name, shape, dt=f32):
            return ctx.enter_context(nc.sbuf_tensor(name, shape, dt))

        def sem(name):
            return ctx.enter_context(nc.semaphore(name))

        const = sb("const", [P, sum(CONSTS.values()) - CONSTS["cfsel"]])
        cv, at = {}, 0
        for k, n in CONSTS.items():
            if k != "cfsel":
                cv[k] = const[:, at:at + n]
                at += n
        ident = cv["ident"]
        before = cv["before"].unsqueeze(1).to_broadcast([P, NT, E * E])
        after = cv["after"].unsqueeze(1).to_broadcast([P, NT, E * E])
        PC = ("-half", "half", "one", "eps", "1/D") + tuple(range(15, 0, -2))
        pool_c = sb("pool_c", [P, len(PC)])
        cfsel = sb("cfsel", [SPL // 2, E, P], bf16)
        winH = sb("winH", [P, KD, 3 * D], f32r)
        winL = sb("winL", [P, KD, 3 * D], f32r)
        w1H = sb("w1H", [P, NE, KD, HID], f32r)
        w1L = sb("w1L", [P, NE, KD, HID], f32r)
        w2 = sb("w2", [P, NE, D])
        wo = sb("wo", [P, KD, D])
        rtH = sb("rtH", [P, KD, E], f32r)
        rtL = sb("rtL", [P, KD, E], f32r)
        r2 = sb("r2", [SPL, D], f32r)
        mods = sb("mods", [P, 4, KD, B])
        gates = sb("gates", [P, 2, D])
        gate_rows = nc.dram_tensor("gate_rows", [B, 2 * D], f32).ap()
        bqkv = sb("bqkv", [P, 6, B])
        b1 = sb("b1", [P, B, NE])
        b1row = sb("b1row", [P, NE])
        blog = sb("blog", [E, B])

        xin = sb("xin", [P, XS, NT, D])
        x1 = sb("x1", [P, 2, NT, D])
        ntok = sb("ntok", [P, 2, NT, D])
        stats = sb("stats", [P, 2, NT, 6])
        ms = sb("ms", [P, 2, 10, NT])
        n1H = sb("n1H", [P, KD, CT], f32r)
        n1L = sb("n1L", [P, KD, CT], f32r)
        n2H = sb("n2H", [P, 2, KD, CT], f32r)
        n2L = sb("n2L", [P, 2, KD, CT], f32r)
        NF = 18
        feat = sb("feat", [P, NF, KD, CT])
        K0, K1, Q0, Q1, V0, KS, KT3, KA, KT5, QSQ, QT3, QA, QT5, W = range(14)
        attn = feat[:, W + 1]
        gated = feat[:, W + 3].rearrange("p h (t d) -> p h t d", t=2)
        carry = sb("carry", [P, ND, KD])
        zero = sb("zero", [P, 1])
        prod = sb("prod", [P, CT])
        kcarry = sb("kcarry", [P, 1])
        denom = sb("denom", [P, 2, P])
        logT = sb("logT", [P, CT])
        route = sb("route", [P, 12, NT * E])
        L_, NEG, U, MX, DN, RC, Z, Z2, PL, SP, AC, CF = range(12)
        pair = sb("pair", [P, 2, NT, E, E])
        rank = sb("rank", [P, NT * E])
        part = sb("part", [P, 2, NT, E], bf16)
        rest = sb("rest", [P, NT, E])
        split = sb("split", [P, NT, P])
        cfR = sb("cfR", [SPL, CT], f32r)
        cfB = sb("cfB", [SPL // 2, CT], bf16)
        NG = 3
        hid = sb("hid", [P, NG, CT])
        fin = sb("fin", [P, NT, D])

        flat = feat[:, :, :, :].rearrange("p n h t -> p (n h t)")
        used = [0]

        def tmp(n):
            v = flat[:, used[0]:used[0] + n]
            used[0] += n
            return v

        win_rows = tmp(6 * D).rearrange("p (m d) -> p m d", m=6)
        winT = tmp(KD * 3 * D).rearrange("p (k e) -> p k e", k=KD)
        wout_rows = tmp(2 * D).rearrange("p (m d) -> p m d", m=2)
        wmod = tmp(KD * 6 * D).rearrange("p (k n) -> p k n", k=KD)
        w1f = tmp(NE * KD * HID).rearrange("p (e k h) -> p e k h", e=NE, k=KD)
        cfself = tmp(E * P)
        c_rows = tmp(D)
        silu_c = tmp(D)
        scT = tmp(KD * B).rearrange("p (k b) -> p k b", k=KD)
        rt_rows = tmp(D)
        rtF = tmp(KD * E).rearrange("p (k e) -> p k e", k=KD)
        b1_rows = tmp(HID)
        b1T = tmp(NE)
        eb = tmp(1)
        r2f, r2h, r2l = tmp(D), tmp(D), tmp(D)
        gsign, gneg, gabs, gfull = tmp(2 * D), tmp(2 * D), tmp(2 * D), tmp(2 * D)
        assert used[0] <= NF * KD * CT

        tr = [ctx.enter_context(nc.psum_tensor(f"tr{k}", [P, CT], f32)) for k in range(2)]
        ring = [ctx.enter_context(nc.psum_tensor(f"ring{k}", [P, CT], f32)) for k in range(2)]
        cfb = ctx.enter_context(nc.psum_tensor("cfb", [P, CT], f32))
        misc = ctx.enter_context(nc.psum_tensor("misc", [P, CT], f32))
        acc = [ctx.enter_context(nc.psum_tensor(f"acc{k}", [P, 2, D], f32)) for k in range(2)]

        x_loaded = [sem(f"x_loaded{p}") for p in range(CB)]
        stored = [sem(f"stored{p}") for p in range(CB)]
        stats_ready = [sem(f"stats{n}_ready") for n in range(2)]
        mv_steps = [sem(f"mean_var{n}_steps") for n in range(2)]
        rstd_ready = [sem(f"rstd{n}_ready") for n in range(2)]
        norm_ready = [sem(f"normalised{n}") for n in range(2)]
        transposed = [sem(f"transposed{n}") for n in range(2)]
        high_ready = [sem(f"high{n}_ready") for n in range(2)]
        low_ready = [sem(f"low{n}_ready") for n in range(2)]
        ring_filled, ring_copied = sem("ring_filled"), sem("ring_copied")
        clipped = sem("clipped")
        squares = sem("squares")
        even_scaled = sem("q_even_scaled")
        odd_ready = sem("odd_ready")
        weighted = sem("values_weighted")
        scanned = sem("prefix_sums")
        carried, kcarried = sem("carried"), sem("head_sums_carried")
        products = sem("order_products")
        added = sem("orders_added")
        numerator = sem("numerator")
        summed = sem("head_sums")
        ksum_ready, prod_ready = sem("key_prefix_sums"), sem("denominator_products")
        den_ready, den_eps, den_inv = sem("denominators"), sem("denominators_eps"), sem("denominators_inverse")
        inv_spread = sem("inverse_spread")
        attn_ready = sem("attention_ready")
        projected = sem("projected")
        gated_ready = sem("gated")
        x1_ready = sem("x1_ready")
        logits_ready, logT_ready, log_tok = sem("logits"), sem("logits_copied"), sem("logits_by_token")
        log_parts = sem("logit_parts")
        exp_ready, inv2_ready = sem("exp_ready"), sem("inverse_of_2_plus_u")
        score_steps, rank_steps = sem("score_steps"), sem("rank_steps")
        split_steps = sem("split_steps")
        split_T, cf_ready = sem("combine_transposed"), sem("combine_rows")
        cfb_ready, hidw_ready = sem("combine_spread"), sem("hidden_weighted")
        expert_done = sem("expert_done")
        ffn_gated, fin_ready = sem("ffn_gated"), sem("output_ready")
        NSCORE, NRANK, NSPLIT, NMV = 19, 7, 7, 9

        b1_row = sem("expert_biases_of_row")
        gate_loaded = [sem("ga_loaded"), sem("gb_loaded")]
        x_v = x_d.rearrange("b (c t p) d -> b c p t d", c=CB, p=P)
        o_v = out_d.rearrange("b (c t p) d -> b c p t d", c=CB, p=P)

        ALL = dict(norm=True, qkv=True, attn=True, second=True, ffn=True)

        def some(*names):
            return {k: k in names for k in ALL}

        FIRST = [(0, 0, some("norm", "qkv", "attn")), (0, 1, some("norm", "qkv", "attn", "second"))]
        LAST = [(B - 1, 0, some("qkv", "attn", "second", "ffn")), (B - 1, 1, some("attn", "second", "ffn")),
                (B, 0, some("second", "ffn")), (B, 1, some("ffn"))]
        RING = ["e0", "e1", "e2", "k0", "k1", "q0", "q1", "e3", "e4", "e5", "v0", "v1", "e6", "e7", "e8"]
        USES = len(RING)

        def number(i, p):
            return CB * i + p

        def later(i, p, n):
            return i + (p + n) // CB, (p + n) % CB

        def ring_of(i, p, st):
            names = [u for u in RING if st["ffn" if u[0] == "e" else "qkv"]]
            if st["ffn"]:
                n = USES * CB * i + USES * p - 12
                if isinstance(i, int) and i == B:
                    n = USES * (B * CB - 1) - 12 + NE * (p + 1)
                bank = n % 2 if isinstance(i, int) else p % 2
            else:
                n, bank = 6 * (1 + number(i, p)), 0
            return {u: (n + k, (bank + k) % 2) for k, u in enumerate(names)}

        HALVES = ["k0", "k1", "q0", "q1", "v0", "v1"]
        CHUNK0 = {u: (k, k % 2) for k, u in enumerate(HALVES)}

        def ge(eng, s, value):
            if not isinstance(value, int) or value > 0:
                eng.wait_ge(s, value)

        def xin_of(i, p):
            if isinstance(i, int):
                return xin[:, CB * (i % 2) + p]
            return xin[:, bass.ds(CB * (i % 2) + p, 1)].rearrange("p a t d -> p (a t) d")

        def col(t, i):
            return t[:, i:i + 1] if isinstance(i, int) else t[:, bass.ds(i, 1)]

        def gate(which):
            return gates[:, which:which + 1].to_broadcast([P, 2, D])

        def f(n):
            return feat[:, n]

        def k_(what, n):
            at = PC.index(what)
            return pool_c[:, at:at + 1].to_broadcast([P, n])

        def inv_std(pool, n, i, p):
            c = number(i, p)
            pool.wait_ge(stats_ready[n], c + 1)
            ge(pool, norm_ready[n], c)
            m0, m1, s0, s1 = (stats[:, n, :, k] for k in (1, 4, 2, 5))
            t = lambda k: ms[:, n, k]
            nc.gpsimd.tensor_tensor(t(0), m0, m1, ALU.add).then_inc(mv_steps[n], 1)
            nc.gpsimd.tensor_tensor(t(1), m0, m1, ALU.subtract).then_inc(mv_steps[n], 1)
            nc.gpsimd.tensor_tensor(t(2), s0, s1, ALU.add).then_inc(mv_steps[n], 1)
            pool.wait_ge(mv_steps[n], NMV * c + 3)
            nc.gpsimd.tensor_tensor(t(3), t(0), k_("half", NT), ALU.mult).then_inc(mv_steps[n], 1)
            nc.gpsimd.tensor_tensor(t(4), t(1), k_("half", NT), ALU.mult).then_inc(mv_steps[n], 1)
            nc.gpsimd.tensor_tensor(t(5), t(2), k_("1/D", NT), ALU.mult).then_inc(mv_steps[n], 1)
            pool.wait_ge(mv_steps[n], NMV * c + 6)
            nc.gpsimd.tensor_tensor(t(6), t(4), t(4), ALU.mult).then_inc(mv_steps[n], 1)
            nc.gpsimd.tensor_tensor(t(7), t(5), k_("eps", NT), ALU.add).then_inc(mv_steps[n], 1)
            pool.wait_ge(mv_steps[n], NMV * c + 8)
            nc.gpsimd.tensor_tensor(t(8), t(6), t(7), ALU.add).then_inc(mv_steps[n], 1)
            pool.wait_ge(mv_steps[n], NMV * c + 9)
            nc.gpsimd.tensor_tensor(t(9), t(8), k_("-half", NT), ALU.pow).then_inc(rstd_ready[n], 1)

        def token_stats(dve, n, i, p):
            c = number(i, p)
            ge(dve, rstd_ready[n], c)
            if n == 0:
                dve.wait_ge(x_loaded[p], 16 * (i + 1))
            src = xin_of(i, p) if n == 0 else x1[:, p]
            for t in range(NT):
                if n == 1:
                    dve.wait_ge(x1_ready, 2 * c + 1 + t // 2)
                last = nc.vector.bn_stats(stats[:, n, t], src[:, t])
            last.then_inc(stats_ready[n], 1)

        def normalise(dve, n, i, p):
            c = number(i, p)
            dve.wait_ge(rstd_ready[n], c + 1)
            ge(dve, transposed[n], 2 * c)
            src = xin_of(i, p) if n == 0 else x1[:, p]
            for t in range(NT):
                last = nc.vector.tensor_scalar(ntok[:, n, t], src[:, t], ms[:, n, 3, t:t + 1], ms[:, n, 9, t:t + 1],
                                       ALU.subtract, ALU.mult)
            last.then_inc(norm_ready[n], 1)

        def load(sp, i, p):
            ge(sp, x_loaded[p], 16 * i)
            sp.dma_start(xin_of(i, p), x_v[i, p]).then_inc(x_loaded[p], 16)

        in_win, in_wout, in_small, in_const, in_wmod, in_w1, in_w2, in_r2, in_gates = (
            sem(f"in_{n}") for n in ("win", "wout", "small", "const", "wmod", "w1", "w2", "r2", "gate_rows"))
        s_tr = sem("setup_transposed")
        s_silu, s_scT = sem("setup_silu"), sem("setup_scT")
        s_hi, s_mods, s_modps, s_gps, s_g1, s_g2 = (sem(f"setup_{n}") for n in (
            "high_parts", "mods", "mod_products", "gate_products", "gate_sign", "gate_abs"))
        s_bias, s_b1T, s_r2 = sem("setup_bias_products"), sem("setup_b1T"), sem("setup_r2")
        s_winT, s_rtT, s_wo, s_pow = sem("setup_winT"), sem("setup_rtT"), sem("setup_wo"), sem("setup_exponents")

        with nc.Block() as block:
            @block.sync
            def _(sp):
                sp.dma_start(c_rows[0:B, :], c_d).then_inc(in_small, 16)
                sp.dma_start(rt_rows[0:E, :], rout_d).then_inc(in_small, 16)
                sp.dma_start(b1_rows[0:1, :], sb1_d.rearrange("(a h) -> a h", a=1)).then_inc(in_small, 16)
                sp.dma_start(b1_rows[1:NE, :], rb1_d).then_inc(in_small, 16)
                sp.dma_start(eb[0:E, :], ebias_d.rearrange("(e a) -> e a", a=1)).then_inc(in_small, 16)
                sp.dma_start(win_rows, w_in_d.rearrange("(m p) d -> p m d", p=P)).then_inc(in_win, 16)
                for p in range(CB):
                    load(sp, 0, p)
                sp.dma_start(wmod, wmod_d.rearrange("(k p) n -> p k n", p=P)).then_inc(in_wmod, 16)
                sp.dma_start(wout_rows, w_out_d.rearrange("(m p) d -> p m d", p=P)).then_inc(in_wout, 16)
                sp.dma_start(w1f[:, 0], sw1_d.rearrange("(k p) h -> p k h", p=P)).then_inc(in_w1, 16)
                sp.dma_start(w1f[:, 1:NE].rearrange("p e k h -> p (e k) h"),
                             rw1_d.rearrange("e (k p) h -> p (e k) h", p=P)).then_inc(in_w1, 16)
                sp.wait_ge(s_g2, 1)
                sp.dma_start(gate_rows, gfull[0:B, :]).then_inc(in_gates, 16)
                sp.wait_ge(in_gates, 16)

            @block.gpsimd
            def _(pool):
                for n, what in enumerate(PC):
                    value = {"-half": -0.5, "half": 0.5, "one": 1.0, "eps": EPS_LN, "1/D": 1.0 / D}.get(what) or 2.0 / what
                    nc.gpsimd.memset(pool_c[:, n:n + 1], value).then_inc(s_pow, 1)
                nc.gpsimd.memset(split[:, :, :], 1.0).then_inc(s_pow, 1)
                nc.gpsimd.memset(zero[:, :], 0.0).then_inc(s_pow, 1)
                nc.gpsimd.memset(logT[:, :], 0.0).then_inc(s_pow, 1)
                pool.wait_ge(s_pow, len(PC) + 3)
                for p in range(CB):
                    inv_std(pool, 0, 0, p)

            @block.scalar
            def _(act):
                act.dma_start(const[:, :], const_d[:, 0:at]).then_inc(in_const, 16)
                act.dma_start(cfself, const_d[:, at:at + E * P]).then_inc(in_const, 16)
                act.dma_start(w2[:, 0], sw2_d).then_inc(in_w2, 16)
                act.dma_start(w2[:, 1:NE], rw2_d.rearrange("e h d -> h e d")).then_inc(in_w2, 16)
                for half in range(2):
                    r = half * (SPL // 2)
                    for copy in range(3):
                        act.dma_start(r2f[r + copy * E:r + (copy + 1) * E, :], rb2_d).then_inc(in_r2, 16)
                    act.dma_start(r2f[r + 3 * E:r + 3 * E + 1, :],
                                  sb2_d.rearrange("(a d) -> a d", a=1)).then_inc(in_r2, 16)
                act.wait_ge(in_small, 5 * 16)
                nc.scalar.activation(silu_c[0:B, :], c_rows[0:B, :], ACT.Silu).then_inc(s_silu, 1)
                for m in range(6):
                    act.wait_ge(s_tr, 2 + m)
                    for k in range(KD):
                        last = nc.scalar.activation(winT[:, k, m * P:(m + 1) * P], ring[m % 2][:, k * P:(k + 1) * P],
                                                    ACT.Copy, scale=0.25 if m < 4 else 1.0)
                    last.then_inc(s_winT, 1)
                act.wait_ge(s_winT, 6)
                nc.scalar.activation(winH[:, :, :], winT, ACT.Copy).then_inc(s_hi, 1)
                for m in range(2):
                    act.wait_ge(s_tr, 8 + m)
                    for k in range(KD):
                        last = nc.scalar.activation(wo[:, k, m * P:(m + 1) * P], ring[m % 2][:, k * P:(k + 1) * P],
                                                    ACT.Copy)
                    last.then_inc(s_wo, 1)
                act.wait_ge(in_w1, 32)
                nc.scalar.activation(w1H[:, :, :, :], w1f, ACT.Copy).then_inc(s_hi, 1)
                act.wait_ge(s_wo, 2)

            @block.vector
            def _(dve):
                dve.wait_ge(s_tr, 1)
                nc.vector.tensor_copy(scT, tr[0][:, 0:KD * B].rearrange("p (k b) -> p k b", k=KD)).then_inc(s_scT, 1)
                nc.vector.tensor_copy(rtF, tr[0][:, 64:64 + KD * E].rearrange("p (k e) -> p k e", k=KD)).then_inc(s_rtT, 1)
                nc.vector.tensor_copy(b1T, tr[0][:, 128:128 + NE]).then_inc(s_b1T, 1)
                dve.wait_ge(s_rtT, 1)
                nc.vector.tensor_copy(rtH[:, :, :], rtF).then_inc(s_rtT, 1)
                dve.wait_ge(s_rtT, 2)
                nc.vector.tensor_tensor(rtL[:, :, :], rtF, rtH[:, :, :].bitcast(f32), ALU.subtract).then_inc(s_rtT, 1)
                token_stats(dve, 0, 0, 0)
                dve.wait_ge(s_modps, 1)
                mp = misc[:, 0:4 * KD * B].rearrange("p (v k b) -> p v k b", v=4, k=KD)
                for v in range(4):
                    last = nc.vector.tensor_scalar(mods[:, v], mp[:, v], float(v % 2), None, ALU.add)
                last.then_inc(s_mods, 1)
                dve.wait_ge(s_gps, 1)
                g = acc[0][0:B].rearrange("p g d -> p (g d)")
                nc.vector.tensor_scalar(gsign[0:B], g, 0.0, 2.0, ALU.is_ge, ALU.mult).then_inc(s_g1, 1)
                nc.vector.tensor_scalar(gneg[0:B], g, -1.0, 0.25, ALU.mult, ALU.max).then_inc(s_g1, 1)
                dve.wait_ge(s_g1, 2)
                nc.vector.tensor_tensor(gabs[0:B], g, gneg[0:B], ALU.max).then_inc(s_g1, 1)
                dve.wait_ge(s_g1, 3)
                nc.vector.scalar_tensor_tensor(out=gfull[0:B], in0=gsign[0:B], scalar=-1.0, in1=gabs[0:B],
                                               op0=ALU.add, op1=ALU.mult).then_inc(s_g2, 1)
                normalise(dve, 0, 0, 0)
                token_stats(dve, 0, 0, 1)
                dve.wait_ge(s_hi, 1)
                nc.vector.tensor_tensor(winL[:, :, :], winT, winH[:, :, :].bitcast(f32), ALU.subtract)
                dve.wait_ge(s_hi, 2)
                nc.vector.tensor_tensor(w1L[:, :, :, :], w1f, w1H[:, :, :, :].bitcast(f32), ALU.subtract)
                dve.wait_ge(s_bias, 1)
                nc.vector.tensor_copy(bqkv[:, :, :], misc[:, 128:128 + 6 * B].rearrange("p (m b) -> p m b", m=6))
                dve.wait_ge(s_b1T, 1)
                nc.vector.tensor_tensor(b1.rearrange("p b m -> p m b"), misc[:, 192:192 + NE * B].rearrange("p (m b) -> p m b", m=NE),
                                        b1T.unsqueeze(2).to_broadcast([P, NE, B]), ALU.add)
                nc.vector.tensor_scalar(blog[:, :], misc[0:E, 320:320 + B], eb[0:E, :], None, ALU.add)
                dve.wait_ge(in_r2, 8 * 16)
                nc.vector.tensor_copy(r2[:, :], r2f[0:SPL, :]).then_inc(s_r2, 1)
                dve.wait_ge(s_r2, 1)
                nc.vector.tensor_tensor(r2l[0:SPL, :], r2f[0:SPL, :], r2[:, :].bitcast(f32), ALU.subtract).then_inc(s_r2, 1)
                nc.vector.tensor_scalar(r2h[0:SPL, :], r2[:, :].bitcast(f32), cv["rowmask"][0:SPL, 0:1], None,
                                        ALU.mult).then_inc(s_r2, 1)
                dve.wait_ge(s_r2, 3)
                nc.vector.scalar_tensor_tensor(out=r2[:, :], in0=r2l[0:SPL, :], scalar=cv["rowmask"][0:SPL, 1:2],
                                               in1=r2h[0:SPL, :], op0=ALU.mult, op1=ALU.add).then_inc(s_r2, 1)
                nc.vector.tensor_copy(cfsel[:, :, :], cfself[0:SPL // 2, :].rearrange("p (e m) -> p e m", e=E)).then_inc(s_r2, 1)
                dve.wait_ge(s_r2, 5)
                dve.wait_ge(in_w2, 32)

            @block.tensor
            def _(pe):
                pe.wait_ge(in_const, 32)
                pe.wait_ge(in_small, 5 * 16)
                pe.wait_ge(s_silu, 1)
                for k in range(KD):
                    nc.tensor.transpose(tr[0][:, k * B:(k + 1) * B], silu_c[0:B, k * P:(k + 1) * P], ident[0:B, 0:B])
                    nc.tensor.transpose(tr[0][:, 64 + k * E:64 + (k + 1) * E], rt_rows[0:E, k * P:(k + 1) * P],
                                        ident[0:E, 0:E])
                nc.tensor.transpose(tr[0][:, 128:128 + NE], b1_rows[0:NE, :], ident[0:NE, 0:NE]).then_inc(s_tr, 1)
                pe.wait_ge(in_win, 16)
                for m in range(6):
                    if m >= 2:
                        pe.wait_ge(s_winT, m - 1)
                    for k in range(KD):
                        last = nc.tensor.transpose(ring[m % 2][:, k * P:(k + 1) * P], win_rows[:, m, k * P:(k + 1) * P],
                                                   ident)
                    last.then_inc(s_tr, 1)
                pe.wait_ge(in_wout, 16)
                for m in range(2):
                    pe.wait_ge(s_winT, 5 + m)
                    for k in range(KD):
                        last = nc.tensor.transpose(ring[m % 2][:, k * P:(k + 1) * P], wout_rows[:, m, k * P:(k + 1) * P],
                                                   ident)
                    last.then_inc(s_tr, 1)
                pe.wait_ge(in_wmod, 16)
                pe.wait_ge(s_scT, 1)
                for v, col in enumerate((0, 1, 3, 4)):
                    for ch in range(KD):
                        o = (v * KD + ch) * B
                        for k in range(KD):
                            last = nc.tensor.matmul(misc[:, o:o + B], wmod[:, k, col * D + ch * P:col * D + (ch + 1) * P],
                                                    scT[:, k], start=(k == 0), stop=(k == KD - 1))
                last.then_inc(s_modps, 1)
                gcols = wmod.rearrange("p k (s n) -> p k s n", s=2)[:, :, :, 2 * D:3 * D]
                for k in range(KD):
                    last = nc.tensor.matmul(acc[0][0:B], scT[:, k], gcols[:, k], start=(k == 0), stop=(k == KD - 1))
                last.then_inc(s_gps, 1)
                pe.wait_ge(s_mods, 1)
                pe.wait_ge(s_winT, 6)
                pe.wait_ge(in_w1, 32)
                pe.wait_ge(s_rtT, 1)
                for m in range(6):
                    for k in range(KD):
                        nc.tensor.matmul(misc[:, 128 + m * B:128 + (m + 1) * B], winT[:, k, m * P:(m + 1) * P],
                                         mods[:, 0, k], start=(k == 0), stop=(k == KD - 1))
                for e in range(NE):
                    for k in range(KD):
                        nc.tensor.matmul(misc[:, 192 + e * B:192 + (e + 1) * B], w1f[:, e, k], mods[:, 2, k],
                                         start=(k == 0), stop=(k == KD - 1))
                for k in range(KD):
                    last = nc.tensor.matmul(misc[0:E, 320:320 + B], rtF[:, k], mods[:, 2, k],
                                            start=(k == 0), stop=(k == KD - 1))
                last.then_inc(s_bias, 1)

        block = ctx.enter_context(nc.Block())

        @block.sync
        def _(sp):
            def store(i, p):
                sp.wait_ge(fin_ready, 2 * number(i, p) + 2)
                sp.dma_start(o_v[i, p], fin[:, :, :]).then_inc(stored[p], 16)

            def load_gate(i, which):
                sp.dma_start(gates[:, which], gate_rows[i, which * D:(which + 1) * D].partition_broadcast(P)) \
                    .then_inc(gate_loaded[which], 16)

            def step(i, p, stores, loads):
                if p == 0:
                    if loads or i < B:
                        if not isinstance(i, int) or i:
                            sp.wait_ge(x1_ready, 2 * number(i, 0))
                        load_gate(i, 0)
                    if stores:
                        load_gate(i - 1, 1)
                if stores:
                    store(i - 1, p)
                if loads:
                    sp.wait_ge(x1_ready, 2 * number(i, p) + 2)
                    load(sp, i + 2, p)

            for p in range(CB):
                load(sp, 1, p)
            for p in range(CB):
                step(0, p, False, True)
            with sp.Fori(1, B - 2) as i:
                for p in range(CB):
                    step(i, p, True, True)
            for i in (B - 2, B - 1, B):
                for p in range(CB):
                    step(i, p, True, False)
            for p in range(CB):
                sp.wait_ge(stored[p], 16 * B)

        @block.gpsimd
        def _(pool):
            g = nc.gpsimd

            def add_orders(i, p):
                c = number(i, p)
                pool.wait_ge(products, ND * c + 2)
                g.tensor_tensor(f(W), f(W), f(W + 1), ALU.add).then_inc(added, 1)
                pool.wait_ge(products, ND * c + 4)
                g.tensor_tensor(f(W + 2), f(W + 2), f(W + 3), ALU.add).then_inc(added, 1)
                pool.wait_ge(added, 3 * c + 2)
                g.tensor_tensor(f(W), f(W), f(W + 2), ALU.add).then_inc(added, 1)

            def scores(i, p):
                c = number(i, p)
                n = [0]

                def then(ins):
                    n[0] += 1
                    ins.then_inc(score_steps, 1)
                    pool.wait_ge(score_steps, NSCORE * c + n[0])

                r = lambda k: route[:, k]
                pool.wait_ge(inv2_ready, 2 * c + 2)
                then(g.tensor_tensor(r(Z), r(U), r(RC), ALU.mult))
                then(g.tensor_tensor(r(Z2), r(Z), r(Z), ALU.mult))
                then(g.tensor_tensor(r(PL), r(Z2), k_(15, NT * E), ALU.mult))
                for m in (13, 11, 9, 7, 5, 3):
                    then(g.tensor_tensor(r(PL), r(PL), k_(m, NT * E), ALU.add))
                    then(g.tensor_tensor(r(PL), r(PL), r(Z2), ALU.mult))
                then(g.tensor_tensor(r(PL), r(PL), k_(1, NT * E), ALU.add))
                then(g.tensor_tensor(r(PL), r(PL), r(Z), ALU.mult))
                pool.wait_ge(log_parts, 3 * c + 3)
                then(g.tensor_tensor(r(SP), r(PL), r(MX), ALU.add))
                then(g.tensor_tensor(r(AC), r(SP), k_("half", NT * E), ALU.pow))
                assert n[0] == NSCORE, n

            def split_weights(i, p):
                c = number(i, p)
                n = [0]

                def then(ins):
                    n[0] += 1
                    ins.then_inc(split_steps, 1)
                    pool.wait_ge(split_steps, NSPLIT * c + n[0])

                pool.wait_ge(rank_steps, NRANK * c + NRANK)
                ge(pool, split_T, c)
                cf = route[:, CF].rearrange("p (t e) -> p t e", t=NT)

                def copy(out, in_):
                    ones = k_("one", NT * out.shape[2]).rearrange("p (t e) -> p t e", t=NT)
                    then(g.tensor_tensor(out, in_, ones, ALU.mult))

                copy(part[:, 0], cf)
                then(g.tensor_tensor(rest[:, :, :], cf, part[:, 0], ALU.subtract))
                copy(part[:, 1], rest[:, :, :])
                then(g.tensor_tensor(split[:, :, 2 * E:3 * E], rest[:, :, :], part[:, 1], ALU.subtract))
                copy(split[:, :, 0:E], part[:, 0])
                copy(split[:, :, E:2 * E], part[:, 1])
                h = SPL // 2
                copy(split[:, :, h:h + 3 * E], split[:, :, 0:3 * E])
                assert n[0] == NSPLIT, n

            def add_residual(i, p):
                c = number(i, p)
                for h in range(2):
                    pool.wait_ge(ffn_gated, 2 * c + h + 1)
                    o = fin[:, 2 * h:2 * h + 2]
                    g.tensor_tensor(o, o, x1[:, p, 2 * h:2 * h + 2], ALU.add).then_inc(fin_ready, 1)

            def step(i, p, st):
                if st["second"]:
                    inv_std(pool, 1, *later(i, p, -1))
                if st["norm"]:
                    inv_std(pool, 0, *later(i, p, 2))
                if st["second"]:
                    scores(*later(i, p, -1))
                if st["attn"]:
                    add_orders(i, p)
                if st["second"]:
                    split_weights(*later(i, p, -1))
                if st["ffn"]:
                    add_residual(*later(i, p, -2))

            for i, p, st in FIRST:
                step(i, p, st)
            with pool.Fori(1, B - 1) as i:
                for p in range(CB):
                    step(i, p, ALL)
            for i, p, st in LAST:
                step(i, p, st)

        @block.scalar
        def _(act):
            a = nc.scalar

            def highs(n, i, p):
                c = number(i, p)
                for k in range(KD):
                    act.wait_ge(transposed[n], 2 * c + k + 1)
                    out = n1H[:, k] if n == 0 else n2H[:, p, k]
                    a.activation(out, tr[k][:, :], ACT.Copy,
                                 scale=col(mods[:, 2 * n + 1, k], i)).then_inc(high_ready[n], 1)

            def copy_qkv(i, p, use, half):
                at, bank = use[half]
                m = HALVES.index(half)
                act.wait_ge(ring_filled, at + 1)
                if m >= 4:
                    ge(act, weighted, ND * number(i, p))
                a.activation(feat[:, (K0 + p, Q0 + p, V0)[m // 2], m % 2], ring[bank][:, :], ACT.Identity,
                             bias=col(bqkv[:, (2, 3, 0, 1, 4, 5)[m]], i)).then_inc(ring_copied, 1)

            def square(i, p, q, which):
                c = number(i, p)
                x, s, qa, qb = ((K0 + p, KS, KA, KT5), (Q0 + p, QSQ, QA, QT5))[q]
                if which == 0:
                    act.wait_ge(clipped, 2 * c + q + 1)
                    if q == 0:
                        ge(act, summed, 2 * c)
                        ge(act, products, ND * c)
                    a.activation(f(s), f(x), ACT.Square).then_inc(squares, 1)
                else:
                    act.wait_ge(squares, 6 * c + 3 * q + 1)
                    a.activation(f((qa, qb)[which - 1]), f(s), ACT.Square,
                                 bias=cv["biases"][:, which - 1:which]).then_inc(squares, 1)

            def scale_even(i, p):
                c = number(i, p)
                act.wait_ge(squares, 6 * c + 6)
                act.wait_ge(odd_ready, 4 * c + 3)
                a.activation(f(QSQ), f(QSQ), ACT.Copy, scale=GAMMA[1], bias=-0.5 * GAMMA[1]).then_inc(even_scaled, 1)
                a.activation(f(QA), f(QA), ACT.Copy, scale=GAMMA[3], bias=-0.125 * GAMMA[3]).then_inc(even_scaled, 1)

            def row_biases(i, use):
                act.wait_ge(ring_copied, use["e0"][0])
                a.activation(b1row[:, :], b1[:, i] if isinstance(i, int) else b1[:, bass.ds(i, 1)].rearrange("p a e -> p (a e)"),
                             ACT.Copy).then_inc(b1_row, 1)

            def hidden(i, p, use, e):
                at, bank = use[f"e{e}"]
                act.wait_ge(ring_filled, at + 1)
                if e == 0 and p == 0:
                    act.wait_ge(b1_row, i + 1)
                a.activation(hid[:, e % NG], ring[bank][:, :], ACT.Silu,
                             bias=b1row[:, e:e + 1]).then_inc(ring_copied, 1)

            def copy_logits(i, p):
                c = number(i, p)
                act.wait_ge(logits_ready, c + 1)
                ge(act, log_tok, c)
                a.activation(logT[0:E, :], misc[0:E, :], ACT.Identity, bias=col(blog, i)).then_inc(logT_ready, 1)

            def exps(i, p):
                c = number(i, p)
                act.wait_ge(log_parts, 3 * c + 2)
                ge(act, score_steps, NSCORE * c)
                a.activation(route[:, U], route[:, NEG], ACT.Exp).then_inc(exp_ready, 1)

            def combine_rows(i, p):
                c = number(i, p)
                act.wait_ge(split_T, c + 1)
                a.activation(cfB[:, :], misc[0:SPL // 2, :], ACT.Copy).then_inc(cf_ready, 1)
                a.activation(cfR[:, :], misc[0:SPL, :], ACT.Copy).then_inc(cf_ready, 1)

            def step(i, p, st):
                use = ring_of(i, p, st)
                nxt, prev, exp = later(i, p, 1), later(i, p, -1), later(i, p, -2)
                qkv, attn_, second, ffn = st["qkv"], st["attn"], st["second"], st["ffn"]

                def silu(e):
                    if ffn:
                        hidden(*exp, use, e)

                def copy(half):
                    if qkv:
                        copy_qkv(*nxt, use, half)

                if ffn and exp[1] == 0:
                    row_biases(exp[0], use)
                silu(0)
                silu(1)
                if qkv:
                    highs(0, *nxt)
                silu(2)
                if attn_:
                    scale_even(i, p)
                for half in HALVES[:4]:
                    copy(half)
                silu(3)
                if second:
                    highs(1, *prev)
                silu(4)
                if second:
                    copy_logits(*prev)
                if second:
                    exps(*prev)
                silu(5)
                copy("v0")
                copy("v1")
                for e in range(6, NE):
                    silu(e)
                if qkv:
                    for q in range(2):
                        for which in range(3):
                            square(*nxt, q, which)
                if second:
                    combine_rows(*prev)

            highs(0, 0, 0)
            for half in HALVES:
                copy_qkv(0, 0, CHUNK0, half)
            for q in range(2):
                for which in range(3):
                    square(0, 0, q, which)
            for i, p, st in FIRST:
                step(i, p, st)
            with act.Fori(1, B - 1) as i:
                for p in range(CB):
                    step(i, p, ALL)
            for i, p, st in LAST:
                step(i, p, st)

        @block.vector
        def _(dve):
            v = nc.vector

            def lows(n, i, p):
                c = number(i, p)
                for k in range(KD):
                    dve.wait_ge(high_ready[n], 2 * c + k + 1)
                    hi = n1H[:, k] if n == 0 else n2H[:, p, k]
                    out = n1L[:, k] if n == 0 else n2L[:, p, k]
                    v.scalar_tensor_tensor(out=out, in0=tr[k][:, :], scalar=col(mods[:, 2 * n + 1, k], i),
                                           in1=hi.bitcast(f32), op0=ALU.mult, op1=ALU.subtract).then_inc(low_ready[n], 1)

            def clip(i, p, use, q):
                dve.wait_ge(ring_copied, use[("k1", "q1")[q]][0] + 1)
                x = (K0, Q0)[q] + p
                v.tensor_scalar(f(x), f(x), CLIP, -CLIP, ALU.min, ALU.max).then_inc(clipped, 1)

            def odd(i, p, q):
                c = number(i, p)
                x, s, t3, t5 = ((K0 + p, KS, KT3, KT5), (Q0 + p, QSQ, QT3, QT5))[q]
                dve.wait_ge(squares, 6 * c + 3 * q + 3)
                if q == 0:
                    ge(dve, summed, 2 * c)
                v.scalar_tensor_tensor(out=f(t3), in0=f(s), scalar=-0.75, in1=f(x),
                                       op0=ALU.add, op1=ALU.mult).then_inc(odd_ready, 1)
                v.scalar_tensor_tensor(out=f(t5), in0=f(t5), scalar=-0.078125, in1=f(x),
                                       op0=ALU.add, op1=ALU.mult).then_inc(odd_ready, 1)

            ORDERS = (0, 1, 3, 2, 4)

            def weigh(i, p, j):
                c = number(i, p)
                n = ORDERS[j]
                val = f(V0)
                if j == 1:
                    ge(dve, projected, 2 * c)
                if j == 0:
                    v.tensor_tensor(f(W), f(K0 + p), val, ALU.mult).then_inc(weighted, 1)
                elif n == 1 or n == 3:
                    v.scalar_tensor_tensor(out=f(W + n), in0=f(KS if n == 1 else KA), scalar=-0.5 if n == 1 else -0.125,
                                           in1=val, op0=ALU.add, op1=ALU.mult).then_inc(weighted, 1)
                else:
                    dve.wait_ge(odd_ready, 4 * c + n // 2)
                    v.tensor_tensor(f(W + n), f(KT3 if n == 2 else KT5), val, ALU.mult).then_inc(weighted, 1)

            def prefix(i, p, j):
                c = number(i, p)
                n = ORDERS[j]
                dve.wait_ge(weighted, ND * c + j + 1)
                if p:
                    dve.wait_ge(carried, i + 1)
                for h in range(KD):
                    last = v.tensor_tensor_scan(feat[:, W + n, h], zero[:, 0:1].to_broadcast([P, CT]), feat[:, W + n, h],
                                                carry[:, n, h:h + 1] if p else 0.0, ALU.add, ALU.add)
                last.then_inc(scanned, 1)

            def carry_over(i, p):
                if p == 0:
                    dve.wait_ge(scanned, ND * number(i, p) + ND)
                    v.tensor_copy(carry[:, :, :], feat[:, W:W + ND, :, CT - 1]).then_inc(carried, 1)

            def order_product(i, p, n):
                c = number(i, p)
                w = f(W + n)
                if n == 0:
                    dve.wait_ge(scanned, ND * c + ND)
                    if p == 0:
                        dve.wait_ge(carried, i + 1)
                if n in (1, 3):
                    dve.wait_ge(even_scaled, 2 * c + (n + 1) // 2)
                    v.tensor_tensor(w, w, f(QSQ if n == 1 else QA), ALU.mult).then_inc(products, 1)
                else:
                    if n:
                        dve.wait_ge(odd_ready, 4 * c + 2 + n // 2)
                    v.scalar_tensor_tensor(out=w, in0=w, scalar=GAMMA[n], in1=f((Q0 + p, 0, QT3, 0, QT5)[n]),
                                           op0=ALU.mult, op1=ALU.mult).then_inc(products, 1)

            def den_products(i, p):
                c = number(i, p)
                dve.wait_ge(summed, 2 * c + 1)
                if p:
                    dve.wait_ge(kcarried, i + 1)
                v.tensor_tensor_scan(prod[:, :], cv["kshift"].to_broadcast([P, CT]), tr[0][:, :],
                                     kcarry[:, :] if p else 0.0, ALU.add, ALU.add).then_inc(ksum_ready, 1)
                dve.wait_ge(summed, 2 * c + 2)
                dve.wait_ge(ksum_ready, c + 1)
                if p == 0:
                    v.tensor_copy(kcarry[:, :], prod[:, CT - 1:CT]).then_inc(kcarried, 1)
                    dve.wait_ge(kcarried, i + 1)
                v.tensor_tensor(prod[:, :], tr[1][:, :], prod[:, :], ALU.mult).then_inc(prod_ready, 1)

            def invert(i, p):
                c = number(i, p)
                dve.wait_ge(den_ready, c + 1)
                v.tensor_scalar(denom[:, 0], misc[:, 0:P], EPS_DEN, None, ALU.add).then_inc(den_eps, 1)
                dve.wait_ge(den_eps, c + 1)
                v.reciprocal(denom[:, 1], denom[:, 0]).then_inc(den_inv, 1)

            def finish_numerator(i, p):
                dve.wait_ge(added, 3 * number(i, p) + 3)
                dve.wait_ge(products, ND * number(i, p) + ND)
                v.tensor_tensor(f(W), f(W), f(W + 4), ALU.add).then_inc(numerator, 1)

            def divide(i, p):
                c = number(i, p)
                dve.wait_ge(numerator, c + 1)
                for k in range(KD):
                    dve.wait_ge(inv_spread, 2 * c + k + 1)
                    v.tensor_tensor(attn[:, k], feat[:, W, k], tr[k][:, :], ALU.mult).then_inc(attn_ready, 1)

            def residual(i, p):
                c = number(i, p)
                dve.wait_ge(gate_loaded[0], 16 * (i + 1))
                for h in range(2):
                    dve.wait_ge(projected, 2 * c + h + 1)
                    v.tensor_tensor(gated[:, h], tr[h][:, :].rearrange("p (t d) -> p t d", t=2), gate(0),
                                    ALU.mult).then_inc(gated_ready, 1)
                ge(dve, fin_ready, 2 * c - 2)
                for h in range(2):
                    dve.wait_ge(gated_ready, 2 * c + h + 1)
                    v.tensor_tensor(x1[:, p, 2 * h:2 * h + 2], gated[:, h], xin_of(i, p)[:, 2 * h:2 * h + 2],
                                    ALU.add).then_inc(x1_ready, 1)

            def logit_parts(i, p):
                c = number(i, p)
                dve.wait_ge(log_tok, c + 1)
                ge(dve, score_steps, NSCORE * c)
                v.tensor_copy(route[:, L_].rearrange("p (t e) -> p t e", t=NT),
                              misc.rearrange("p (t e) -> p t e", t=NT)[:, :, 0:E]).then_inc(log_parts, 1)
                dve.wait_ge(log_parts, 3 * c + 1)
                v.scalar_tensor_tensor(out=route[:, NEG], in0=route[:, L_], scalar=-1.0, in1=route[:, L_],
                                       op0=ALU.mult, op1=ALU.min).then_inc(log_parts, 1)
                v.tensor_scalar(route[:, MX], route[:, L_], 0.0, None, ALU.max).then_inc(log_parts, 1)

            def inverse2(i, p):
                c = number(i, p)
                dve.wait_ge(exp_ready, c + 1)
                v.tensor_scalar(route[:, DN], route[:, U], 2.0, None, ALU.add).then_inc(inv2_ready, 1)
                dve.wait_ge(inv2_ready, 2 * c + 1)
                v.reciprocal(route[:, RC], route[:, DN]).then_inc(inv2_ready, 1)

            def choose(i, p):
                c = number(i, p)
                at = NRANK * c
                dve.wait_ge(score_steps, NSCORE * c + NSCORE)
                s = route[:, AC].rearrange("p (t e) -> p t e", t=NT)
                others = s.unsqueeze(2).to_broadcast([P, NT, E, E])
                own = s.unsqueeze(3).to_broadcast([P, NT, E, E])
                v.tensor_tensor(pair[:, 0], others, own, ALU.is_ge).then_inc(rank_steps, 1)
                v.tensor_tensor(pair[:, 1], others, own, ALU.is_gt).then_inc(rank_steps, 1)
                dve.wait_ge(rank_steps, at + 1)
                g0, g1 = (pair[:, k].rearrange("p t e j -> p t (e j)") for k in range(2))
                v.tensor_tensor(g0, g0, before, ALU.mult).then_inc(rank_steps, 1)
                dve.wait_ge(rank_steps, at + 2)
                v.tensor_tensor(g1, g1, after, ALU.mult).then_inc(rank_steps, 1)
                dve.wait_ge(rank_steps, at + 4)
                v.tensor_tensor(pair[:, 0], pair[:, 0], pair[:, 1], ALU.add).then_inc(rank_steps, 1)
                dve.wait_ge(rank_steps, at + 5)
                v.tensor_reduce(rank[:, :], pair[:, 0].rearrange("p t e j -> p (t e) j"), AX.X,
                                ALU.add).then_inc(rank_steps, 1)
                dve.wait_ge(rank_steps, at + 6)
                ge(dve, split_steps, NSPLIT * c)
                v.scalar_tensor_tensor(out=route[:, CF], in0=rank[:, :], scalar=2.0, in1=route[:, AC],
                                       op0=ALU.is_lt, op1=ALU.mult).then_inc(rank_steps, 1)

            def weigh_hidden(i, p, use, e):
                c = number(i, p)
                dve.wait_ge(ring_copied, use[f"e{e}"][0] + 1)
                dve.wait_ge(cfb_ready, E * c + e)
                v.tensor_tensor(hid[:, e % NG], hid[:, e % NG], cfb[:, :], ALU.mult).then_inc(hidw_ready, 1)

            def output(i, p):
                c = number(i, p)
                dve.wait_ge(expert_done, NE * c + NE)
                dve.wait_ge(gate_loaded[1], 16 * (i + 1))
                ge(dve, stored[1 - p], 16 * (i + p))
                for h in range(2):
                    v.tensor_tensor(fin[:, 2 * h:2 * h + 2], acc[h][:, :, :], gate(1), ALU.mult).then_inc(ffn_gated, 1)

            def step(i, p, st):
                use = ring_of(i, p, st)
                nxt, prev, exp, after2 = later(i, p, 1), later(i, p, -1), later(i, p, -2), later(i, p, 2)
                norm, qkv, attn_, second, ffn = (st[k] for k in ("norm", "qkv", "attn", "second", "ffn"))

                def expert(e):
                    if ffn:
                        weigh_hidden(*exp, use, e)

                if second:
                    residual(*prev)
                    token_stats(dve, 1, *prev)
                if qkv:
                    lows(0, *nxt)
                if attn_:
                    weigh(i, p, 0)
                expert(1)
                if attn_:
                    weigh(i, p, 1)
                    weigh(i, p, 2)
                if second:
                    normalise(dve, 1, *prev)
                if attn_:
                    weigh(i, p, 3)
                    weigh(i, p, 4)
                expert(2)
                if norm:
                    token_stats(dve, 0, *after2)
                if second:
                    lows(1, *prev)
                if attn_:
                    prefix(i, p, 0)
                    prefix(i, p, 1)
                expert(3)
                if attn_:
                    prefix(i, p, 2)
                if second:
                    logit_parts(*prev)
                if attn_:
                    den_products(i, p)
                if second:
                    inverse2(*prev)
                expert(4)
                if attn_:
                    prefix(i, p, 3)
                if qkv:
                    clip(*nxt, use, 0)
                    clip(*nxt, use, 1)
                if attn_:
                    prefix(i, p, 4)
                    carry_over(i, p)
                expert(5)
                if attn_:
                    invert(i, p)
                    order_product(i, p, 0)
                    order_product(i, p, 1)
                expert(6)
                if attn_:
                    for n in range(2, ND):
                        order_product(i, p, n)
                expert(7)
                if second:
                    choose(*prev)
                expert(8)
                if attn_:
                    finish_numerator(i, p)
                    divide(i, p)
                if ffn:
                    output(*exp)
                if qkv:
                    odd(*nxt, 0)
                    odd(*nxt, 1)
                if norm:
                    normalise(dve, 0, *after2)

            lows(0, 0, 0)
            normalise(dve, 0, 0, 1)
            for q in range(2):
                clip(0, 0, CHUNK0, q)
            for q in range(2):
                odd(0, 0, q)
            for i, p, st in FIRST:
                step(i, p, st)
            for p in range(CB):
                step(1, p, ALL)
            with dve.Fori(2, B - 1) as i:
                for p in range(CB):
                    step(i, p, ALL)
            for i, p, st in LAST:
                step(i, p, st)

        @block.tensor
        def _(pe):
            mm = nc.tensor.matmul

            def transposes(n, i, p, behind_norm=False):
                c = number(i, p)
                pe.wait_ge(norm_ready[n], c + 1)
                if behind_norm:
                    pe.wait_ge(low_ready[0], 2 * (c + 3))
                else:
                    ge(pe, gated_ready, 2 * (c - 1 if n == 0 else c + 1))
                for k in range(KD):
                    for t in range(NT):
                        last = nc.tensor.transpose(tr[k][:, t * P:(t + 1) * P], ntok[:, n, t, k * P:(k + 1) * P], ident)
                    last.then_inc(transposed[n], 1)

            def split_product(out, wH, wL, xH, xL):
                terms = [(wH[k], xH[k]) for k in range(KD)] + [(wH[k], xL[k]) for k in range(KD)] \
                    + [(wL[k], xH[k]) for k in range(KD)]
                for n, (w, x) in enumerate(terms):
                    last = mm(out, w, x, start=(n == 0), stop=(n == len(terms) - 1))
                return last

            halves = lambda t: [t[:, k] for k in range(KD)]

            def project(i, p, use, half):
                c = number(i, p)
                pe.wait_ge(high_ready[0], 2 * c + 2)
                pe.wait_ge(low_ready[0], 2 * c + 2)
                at, bank = use[half]
                ge(pe, ring_copied, at - 1)
                w = (2, 3, 0, 1, 4, 5)[HALVES.index(half)]
                cols = slice(w * P, (w + 1) * P)
                split_product(ring[bank][:, :], [winH[:, k, cols] for k in range(KD)],
                              [winL[:, k, cols] for k in range(KD)], halves(n1H), halves(n1L)).then_inc(ring_filled, 1)

            def route_logits(i, p):
                c = number(i, p)
                pe.wait_ge(high_ready[1], 2 * c + 2)
                pe.wait_ge(low_ready[1], 2 * c + 2)
                ge(pe, cf_ready, 2 * c)
                pe.wait_ge(den_eps, c + 1)
                split_product(misc[0:E, :], halves(rtH), halves(rtL), halves(n2H[:, p]), halves(n2L[:, p])) \
                    .then_inc(logits_ready, 1)

            def logits_by_token(i, p):
                c = number(i, p)
                pe.wait_ge(logT_ready, c + 1)
                for t in range(NT):
                    last = nc.tensor.transpose(misc[:, t * P:(t + 1) * P], logT[:, t * P:(t + 1) * P], ident)
                last.then_inc(log_tok, 1)

            def head_sums(i, p, q, behind_second):
                c = number(i, p)
                if behind_second:
                    pe.wait_ge(low_ready[1], 2 * c)
                else:
                    pe.wait_ge(low_ready[0], 2 * (c + 2))
                srcs = ((K0 + p, KS, KT3, KA, KT5), (Q0 + p, QSQ, QT3, QA, QT5))[q]
                pe.wait_ge(odd_ready, 4 * c + 2 * q + 2)
                if q:
                    pe.wait_ge(even_scaled, 2 * c + 2)
                order = [(0, 0), (1, 0), (2, 0), (3, 0), (0, 1), (1, 1), (2, 1), (3, 1), (4, 0), (4, 1)]
                final = {0: (4, 0), 1: (4, 1), 2: (2, 1), 3: (3, 1)}
                for n, h in order:
                    g_, r = ROWS[n, h]
                    last = mm(tr[q][g_ * QS:(g_ + 1) * QS, :],
                              cv["headsum"][:, (r // HPH) * QS:(r // HPH + 1) * QS], feat[:, srcs[n], h],
                              start=(n < 4 and h == 0), stop=(final[g_] == (n, h)))
                last.then_inc(summed, 1)

            def denominators(i, p):
                c = number(i, p)
                pe.wait_ge(prod_ready, c + 1)
                ge(pe, log_parts, 3 * (c - 1) + 1)
                for t in range(NT):
                    last = mm(misc[t * QS:(t + 1) * QS, 0:P], cv["densum"],
                              prod[:, t * P:(t + 1) * P], start=True, stop=True)
                last.then_inc(den_ready, 1)

            def spread_inverse(i, p):
                c = number(i, p)
                pe.wait_ge(den_inv, c + 1)
                for k in range(KD):
                    for t in range(NT):
                        last = mm(tr[k][:, t * P:(t + 1) * P], cv["headsel"][:, (t * KD + k) * P:(t * KD + k + 1) * P], denom[:, 1],
                                  start=True, stop=True)
                    last.then_inc(inv_spread, 1)

            def project_out(i, p):
                c = number(i, p)
                pe.wait_ge(attn_ready, 2 * c + 2)
                for t in range(NT):
                    for k in range(KD):
                        last = mm(tr[t // 2][:, (t % 2) * D:(t % 2 + 1) * D], attn[:, k, t * P:(t + 1) * P], wo[:, k],
                                  start=(k == 0), stop=(k == KD - 1))
                    if t % 2:
                        last.then_inc(projected, 1)

            def combine_by_expert(i, p, behind_attn):
                c = number(i, p)
                pe.wait_ge(split_steps, NSPLIT * c + NSPLIT)
                if behind_attn:
                    pe.wait_ge(den_eps, c + 2)
                else:
                    pe.wait_ge(log_parts, 3 * c + 1)
                for t in range(NT):
                    last = nc.tensor.transpose(misc[:, t * P:(t + 1) * P], split[:, t], ident)
                last.then_inc(split_T, 1)

            def expert_up(i, p, use, e):
                at, bank = use[f"e{e}"]
                pe.wait_ge(ring_copied, at - 1)
                split_product(ring[bank][:, :], halves(w1H[:, e]), halves(w1L[:, e]),
                              halves(n2H[:, p]), halves(n2L[:, p])).then_inc(ring_filled, 1)

            def spread_weights(i, p, e):
                mm(cfb[:, :], cfsel[:, e - 1], cfB[:, :], start=True, stop=True).then_inc(cfb_ready, 1)

            def second_biases(i, p):
                c = number(i, p)
                pe.wait_ge(cf_ready, 2 * c + 2)
                ge(pe, ffn_gated, 2 * c)
                for t in range(NT):
                    mm(acc[t // 2][:, t % 2], cfR[:, t * P:(t + 1) * P], r2[:, :], start=(t % 2 == 0), stop=False,
                       skip_group_check=True)

            def expert_down(i, p, use, e):
                c = number(i, p)
                if e == 0:
                    pe.wait_ge(ring_copied, use["e0"][0] + 1)
                else:
                    pe.wait_ge(hidw_ready, E * c + e)
                if e < E:
                    spread_weights(i, p, e + 1)
                for t in range(NT):
                    last = mm(acc[t // 2][:, t % 2], hid[:, e % NG, t * P:(t + 1) * P], w2[:, e], start=False,
                              stop=(e == E), skip_group_check=True)
                last.then_inc(expert_done, 1)

            def step(i, p, st):
                use = ring_of(i, p, st)
                nxt, prev, exp = later(i, p, 1), later(i, p, -1), later(i, p, -2)
                qkv, attn_, second, ffn = st["qkv"], st["attn"], st["second"], st["ffn"]

                def expert(e):
                    if ffn:
                        if e + 2 < NE:
                            expert_up(*exp, use, e + 2)
                        expert_down(*exp, use, e)

                if ffn:
                    expert_up(*exp, use, 0)
                    expert_up(*exp, use, 1)
                    second_biases(*exp)
                if qkv:
                    transposes(0, *nxt)
                expert(0)
                if qkv:
                    for half in HALVES[:4]:
                        project(*nxt, use, half)
                expert(1)
                if second:
                    transposes(1, *prev, behind_norm=qkv)
                expert(2)
                if second:
                    route_logits(*prev)
                if attn_:
                    head_sums(i, p, 0, second)
                if second:
                    logits_by_token(*prev)
                if attn_:
                    head_sums(i, p, 1, second)
                expert(3)
                if qkv:
                    project(*nxt, use, "v0")
                    project(*nxt, use, "v1")
                expert(4)
                if attn_:
                    denominators(i, p)
                expert(5)
                if attn_:
                    spread_inverse(i, p)
                expert(6)
                expert(7)
                expert(8)
                if attn_:
                    project_out(i, p)
                if second:
                    combine_by_expert(*prev, attn_)

            transposes(0, 0, 0)
            for half in HALVES:
                project(0, 0, CHUNK0, half)
            for i, p, st in FIRST:
                step(i, p, st)
            for p in range(CB):
                step(1, p, ALL)
            with pe.Fori(2, B - 1) as i:
                for p in range(CB):
                    step(i, p, ALL)
            for i, p, st in LAST:
                step(i, p, st)


_INS = ['L0_attn_x', 'L0_attn_W_in', 'L0_attn_W_out', 'L0_ffn_routing_W', 'L0_ffn_expert_bias', 'L0_ffn_sW1',
        'L0_ffn_sb1', 'L0_ffn_sW2', 'L0_ffn_sb2', 'L0_ffn_rW1', 'L0_ffn_rb1', 'L0_ffn_rW2', 'L0_ffn_rb2', 'L0_c',
        'L0_wmod']


def kernel(**inputs):
    import concourse.bacc as _bacc
    from concourse.bass_utils import run_bass_kernel_spmd as _run

    nc = _bacc.Bacc("TRN2", target_bir_lowering=False, num_devices=1)
    arrays, args = {}, []
    for name in _INS:
        a = np.ascontiguousarray(inputs[name])
        arrays[f"in_{name}"] = a
        args.append(nc.dram_tensor(f"in_{name}", a.shape, mybir.dt.from_np(a.dtype), kind="ExternalInput").ap())
    a = constants()
    arrays["in_constants"] = a
    args.append(nc.dram_tensor("in_constants", a.shape, mybir.dt.float32, kind="ExternalInput").ap())
    args.append(nc.dram_tensor("out", (B, S, D), mybir.dt.float32, kind="ExternalOutput").ap())
    build(nc, *args)
    r = _run(nc, [arrays], core_ids=[0])
    return r.results[0]["out"]
```

```python
import concourse.bass as bass
from concourse import mybir
from contextlib import ExitStack
import numpy as np

B, S, D = 8, 1024, 256
P = 128
KD = D // P
H, DH = 16, 16
E = 8
NE = E + 1
HID = 4 * D // E
CT = 512
NT = CT // P
CB = S // CT
NC = B * CB
ORDER = 6
ND = ORDER - 1
CLIP = 1.0 - 1e-6
HPH = H // KD
QS = 32
SPL = 2 * (3 * E + 1)
LQ = 2 * QS
XS = 4


def chebyshev_weights():
    j = np.arange(ORDER, dtype=np.float32)
    alpha = (j + 1.0) ** (-1.5)
    tail = np.flip(np.cumsum(np.flip(alpha)))
    beta = np.concatenate([np.zeros(1, np.float32), tail[1:].astype(np.float32), np.zeros(ORDER - 1, np.float32)])
    beta = (beta / beta.sum()).astype(np.float32)
    return [float(beta[n]) * 4.0 ** (n - 1) for n in range(1, ORDER)]


GAMMA = chebyshev_weights()


def head_rows():
    rows = {}
    for n in range(4):
        rows[n, 0], rows[n, 1] = (n, 0), (n, 2 * HPH)
    rows[4, 0], rows[4, 1] = (0, HPH), (1, 3 * HPH)
    return rows


ROWS = head_rows()

CONSTS = {"ident": P, "headsum": 4 * QS, "densum": QS, "headsel": NT * KD * P, "kshift": 1, "rowmask": 2,
          "biases": 2, "before": E * E, "after": E * E, "cfsel": E * P}


def constants():
    c = {k: np.zeros((P, n), np.float32) for k, n in CONSTS.items()}
    c["ident"] = np.eye(P, dtype=np.float32)
    ch = np.arange(P)
    for o in range(4):
        c["headsum"][ch, o * QS + o * HPH + ch // DH] = 1.0
    for (n, half), (g, r) in ROWS.items():
        for h in range(HPH):
            row = g * QS + r + h
            w = GAMMA[n] if n in (0, 2, 4) else 1.0
            for copy in range(QS // H):
                c["densum"][row, copy * H + half * HPH + h] = w
            c["kshift"][row, 0] = {1: -0.5 * DH, 3: -0.125 * DH}.get(n, 0.0)
    for q in range(4):
        for half in range(KD):
            c["headsel"][q * QS + half * HPH + ch // DH, (q * KD + half) * P + ch] = 1.0
    c["rowmask"][:SPL // 2, 0] = 1.0
    c["rowmask"][SPL // 2:SPL, 1] = 1.0
    c["biases"][:, 0], c["biases"][:, 1] = -0.5, -0.625
    e, j = np.meshgrid(np.arange(E), np.arange(E), indexing="ij")
    c["before"][:] = (j < e).astype(np.float32).ravel()
    c["after"][:] = (j > e).astype(np.float32).ravel()
    for x in range(E):
        for part in range(3):
            c["cfsel"][part * E + x, x * P:(x + 1) * P] = 1.0
    return np.concatenate([c[k] for k in CONSTS], axis=1)


def build(nc, x_d, w_in_d, w_out_d, rout_d, ebias_d, sw1_d, sb1_d, sw2_d, sb2_d,
          rw1_d, rb1_d, rw2_d, rb2_d, c_d, wmod_d, const_d, out_d):
    f32, f32r, bf16 = mybir.dt.float32, mybir.dt.float32r, mybir.dt.bfloat16
    ALU = mybir.AluOpType
    ACT = mybir.ActivationFunctionType
    AX = mybir.AxisListType
    EPS_LN, EPS_DEN = 1e-5, 1e-7

    ctx = ExitStack()
    with ctx:
        def sb(name, shape, dt=f32):
            return ctx.enter_context(nc.sbuf_tensor(name, shape, dt))

        def sem(name):
            return ctx.enter_context(nc.semaphore(name))

        const = sb("const", [P, sum(CONSTS.values()) - CONSTS["cfsel"]])
        cv, at = {}, 0
        for k, n in CONSTS.items():
            if k != "cfsel":
                cv[k] = const[:, at:at + n]
                at += n
        ident = cv["ident"]
        before = cv["before"].unsqueeze(1).to_broadcast([P, NT, E * E])
        after = cv["after"].unsqueeze(1).to_broadcast([P, NT, E * E])
        PC = ("-half", "half", "one", "eps", "1/D") + tuple(range(15, 0, -2))
        pool_c = sb("pool_c", [P, len(PC)])
        cfsel = sb("cfsel", [SPL // 2, E, P], bf16)
        winH = sb("winH", [P, KD, 3 * D], f32r)
        winL = sb("winL", [P, KD, 3 * D], f32r)
        w1H = sb("w1H", [P, NE, KD, HID], f32r)
        w1L = sb("w1L", [P, NE, KD, HID], f32r)
        w2 = sb("w2", [P, E // 2 + 1, D])
        w2H = sb("w2H", [P, E // 2, D], f32r)
        w2L = sb("w2L", [P, E // 2, D], f32r)
        wo = sb("wo", [P, KD, D])
        rt = sb("rt", [P, KD, 2, QS], f32r)
        r2 = sb("r2", [SPL, D], f32r)
        mods = sb("mods", [P, 4, KD, B])
        gates = sb("gates", [P, 2, D])
        gate_rows = nc.dram_tensor("gate_rows", [B, 2 * D], f32).ap()
        bqkv = sb("bqkv", [P, 6, B])
        b1 = sb("b1", [P, B, NE])
        b1row = sb("b1row", [P, NE])
        blog = sb("blog", [LQ, B])

        xin = sb("xin", [P, XS, NT, D])
        x1 = sb("x1", [P, 2, NT, D])
        ntok = sb("ntok", [P, NT, D])
        stats = sb("stats", [P, 2, NT, 6])
        ms = sb("ms", [P, 2, 12, NT])
        n1H = sb("n1H", [P, KD, CT], f32r)
        n1L = sb("n1L", [P, KD, CT], f32r)
        n2H = sb("n2H", [P, 2, KD, CT], f32r)
        n2L = sb("n2L", [P, 2, KD, CT], f32r)
        NF = 18
        feat = sb("feat", [P, NF, KD, CT])
        K0, K1, Q0, Q1, V0, KS, KT3, KA, KT5, QSQ, QT3, QA, QT5, W = range(14)
        attn = feat[:, W + 1]
        gated = feat[:, W + 3].rearrange("p h (t d) -> p h t d", t=2)
        carry = sb("carry", [P, ND, KD])
        zero = sb("zero", [P, 1])
        prod = sb("prod", [P, CT])
        kcarry = sb("kcarry", [P, 1])
        denom = sb("denom", [P, 2, P])
        logT = sb("logT", [P, CT])
        route = sb("route", [P, 10, NT * E])
        L_, NEG, U, MX, RC, Z, Z2, PL, AC, CF = range(10)
        DN, SP = Z, RC
        pair = prod.rearrange("p (g t e j) -> p g t e j", g=2, t=NT, e=E)
        rank = route[:, L_]
        part = sb("part", [P, 2, NT, E], bf16)
        rest = sb("rest", [P, NT, E])
        split = sb("split", [P, NT, P])
        cfR = sb("cfR", [SPL, CT], f32r)
        cfB = sb("cfB", [SPL // 2, CT], bf16)
        NG = 3
        hid = sb("hid", [P, NG, CT])
        hidH = sb("hidH", [P, CT], f32r)
        hidL = sb("hidL", [P, CT], f32r)
        fin = sb("fin", [P, NT, D])

        flat = feat[:, :, :, :].rearrange("p n h t -> p (n h t)")
        used = [0]

        def tmp(n):
            v = flat[:, used[0]:used[0] + n]
            used[0] += n
            return v

        win_rows = tmp(6 * D).rearrange("p (m d) -> p m d", m=6)
        winT = tmp(KD * 3 * D).rearrange("p (k e) -> p k e", k=KD)
        wout_rows = tmp(2 * D).rearrange("p (m d) -> p m d", m=2)
        wmod = tmp(KD * 6 * D).rearrange("p (k n) -> p k n", k=KD)
        w2f = tmp(E // 2 * D).rearrange("p (e d) -> p e d", e=E // 2)
        c_rows = tmp(D)
        silu_c = tmp(D)
        scT = tmp(KD * B).rearrange("p (k b) -> p k b", k=KD)
        rt_rows = tmp(D)
        gsign, gneg, gabs, gfull = tmp(2 * D), tmp(2 * D), tmp(2 * D), tmp(2 * D)
        assert used[0] <= NF * KD * CT

        late, at_late = hid.rearrange("p g t -> p (g t)"), [0]

        def tmp_late(n):
            v = late[:, at_late[0]:at_late[0] + n]
            at_late[0] += n
            return v

        w1f = [tmp_late(KD * HID).rearrange("p (k h) -> p k h", k=KD)] \
            + [x1[:, e // (E // 2), e % (E // 2)].rearrange("p (k h) -> p k h", k=KD) for e in range(E)]
        w1f_routed = x1.rearrange("p s t (k h) -> p (s t) k h", k=KD)
        cfself = fin.rearrange("p t d -> p (t d)")
        b1_rows, b1T, eb = tmp_late(HID), tmp_late(NE), tmp_late(1)
        rtF = tmp_late(KD * QS).rearrange("p (k e) -> p k e", k=KD)
        r2f, r2h, r2l = tmp_late(D), tmp_late(D), tmp_late(D)
        assert at_late[0] <= NG * CT and NT * D == KD * HID * (E // 2) and E * P == NT * D

        tr = [ctx.enter_context(nc.psum_tensor(f"tr{k}", [P, CT], f32)) for k in range(2)]
        ring = [ctx.enter_context(nc.psum_tensor(f"ring{k}", [P, CT], f32)) for k in range(2)]
        cfb = ctx.enter_context(nc.psum_tensor("cfb", [P, CT], f32))
        misc = ctx.enter_context(nc.psum_tensor("misc", [P, CT], f32))
        acc = [ctx.enter_context(nc.psum_tensor(f"acc{k}", [P, 2, D], f32)) for k in range(2)]

        x_loaded = [sem(f"x_loaded{p}") for p in range(CB)]
        stored = [sem(f"stored{p}") for p in range(CB)]
        stats_ready = [sem(f"stats{n}_ready") for n in range(2)]
        mv_steps = [sem(f"mean_var{n}_steps") for n in range(2)]
        rstd_ready = [sem(f"rstd{n}_ready") for n in range(2)]
        norm_ready = [sem(f"normalised{n}") for n in range(2)]
        transposed = [sem(f"transposed{n}") for n in range(2)]
        high_ready = [sem(f"high{n}_ready") for n in range(2)]
        low_ready = [sem(f"low{n}_ready") for n in range(2)]
        ring_filled, ring_copied = sem("ring_filled"), sem("ring_copied")
        clipped = sem("clipped")
        squares = sem("squares")
        even_scaled = sem("q_even_scaled")
        odd_ready = sem("odd_ready")
        weighted = sem("values_weighted")
        weighted5 = sem("values_weighted_order_5")
        scanned = sem("prefix_sums")
        carried, kcarried = sem("carried"), sem("head_sums_carried")
        products = sem("order_products")
        added = sem("orders_added")
        numerator = sem("numerator")
        summed = sem("head_sums")
        ksum_ready, prod_ready = sem("key_prefix_sums"), sem("denominator_products")
        den_ready, den_eps, den_inv = sem("denominators"), sem("denominators_eps"), sem("denominators_inverse")
        inv_spread = sem("inverse_spread")
        attn_ready = sem("attention_ready")
        projected = sem("projected")
        gated_ready = sem("gated")
        x1_ready = sem("x1_ready")
        logits_ready, logT_ready, log_tok = sem("logits"), sem("logits_copied"), sem("logits_by_token")
        log_parts = sem("logit_parts")
        exp_ready, inv2_ready = sem("exp_ready"), sem("inverse_of_2_plus_u")
        score_steps, rank_steps = sem("score_steps"), sem("rank_steps")
        split_steps = sem("split_steps")
        split_T, cf_ready = sem("combine_transposed"), sem("combine_rows")
        cfb_ready, hidw_ready = sem("combine_spread"), sem("hidden_weighted")
        hidH_ready, hidL_ready = sem("hidden_high"), sem("hidden_low")
        expert_done = sem("expert_done")
        ffn_gated, fin_ready = sem("ffn_gated"), sem("output_ready")
        NSCORE, NRANK, NSPLIT, NMV = 19, 7, 7, (11, 9)

        late_products, late_biases, late_weights = (sem(f"late_{n}") for n in ("bias_products", "biases", "weights"))
        b1_row = sem("expert_biases_of_row")
        gate_loaded = [sem("ga_loaded"), sem("gb_loaded")]
        x_v = x_d.rearrange("b (c t p) d -> b c p t d", c=CB, p=P)
        o_v = out_d.rearrange("b (c t p) d -> b c p t d", c=CB, p=P)

        ALL = dict(norm=True, qkv=True, attn=True, second=True, ffn=True)

        def some(*names):
            return {k: k in names for k in ALL}

        FIRST = [(0, 0, some("norm", "qkv", "attn")), (0, 1, some("norm", "qkv", "attn", "second"))]
        LAST = [(B - 1, 0, some("qkv", "attn", "second", "ffn")), (B - 1, 1, some("attn", "second", "ffn")),
                (B, 0, some("second", "ffn")), (B, 1, some("ffn"))]
        RING = ["e0", "e1", "e2", "k0", "k1", "q0", "q1", "e3", "e4", "e5", "v0", "v1", "e6", "e7", "e8"]
        USES = len(RING)
        SPLIT = range(0, E, 2)

        def number(i, p):
            return CB * i + p

        def later(i, p, n):
            return i + (p + n) // CB, (p + n) % CB

        def ring_of(i, p, st):
            names = [u for u in RING if st["ffn" if u[0] == "e" else "qkv"]]
            if st["ffn"]:
                n = USES * CB * i + USES * p - 12
                if isinstance(i, int) and i == B:
                    n = USES * (B * CB - 1) - 12 + NE * (p + 1)
                bank = n % 2 if isinstance(i, int) else p % 2
            else:
                n, bank = 6 * (1 + number(i, p)), 0
            return {u: (n + k, (bank + k) % 2) for k, u in enumerate(names)}

        HALVES = ["k0", "k1", "q0", "q1", "v0", "v1"]
        CHUNK0 = {u: (k, k % 2) for k, u in enumerate(HALVES)}

        def ge(eng, s, value):
            if not isinstance(value, int) or value > 0:
                eng.wait_ge(s, value)

        def xin_of(i, p):
            if isinstance(i, int):
                return xin[:, CB * (i % 2) + p]
            return xin[:, bass.ds(CB * (i % 2) + p, 1)].rearrange("p a t d -> p (a t) d")

        def col(t, i):
            return t[:, i:i + 1] if isinstance(i, int) else t[:, bass.ds(i, 1)]

        def gate(which):
            return gates[:, which:which + 1].to_broadcast([P, 2, D])

        def f(n):
            return feat[:, n]

        def k_(what, n):
            at = PC.index(what)
            return pool_c[:, at:at + 1].to_broadcast([P, n])

        def inv_std(pool, n, i, p):
            c = number(i, p)
            pool.wait_ge(stats_ready[n], c + 1)
            ge(pool, norm_ready[n], c)
            m0, m1, s0, s1 = (stats[:, n, :, k] for k in (1, 4, 2, 5))
            t = lambda k: ms[:, n, k]
            nc.gpsimd.tensor_tensor(t(0), m0, m1, ALU.add).then_inc(mv_steps[n], 1)
            nc.gpsimd.tensor_tensor(t(1), m0, m1, ALU.subtract).then_inc(mv_steps[n], 1)
            nc.gpsimd.tensor_tensor(t(2), s0, s1, ALU.add).then_inc(mv_steps[n], 1)
            pool.wait_ge(mv_steps[n], NMV[n] * c + 3)
            nc.gpsimd.tensor_tensor(t(3), t(0), k_("half", NT), ALU.mult).then_inc(mv_steps[n], 1)
            nc.gpsimd.tensor_tensor(t(4), t(1), k_("half", NT), ALU.mult).then_inc(mv_steps[n], 1)
            nc.gpsimd.tensor_tensor(t(5), t(2), k_("1/D", NT), ALU.mult).then_inc(mv_steps[n], 1)
            pool.wait_ge(mv_steps[n], NMV[n] * c + 6)
            nc.gpsimd.tensor_tensor(t(6), t(4), t(4), ALU.mult).then_inc(mv_steps[n], 1)
            nc.gpsimd.tensor_tensor(t(7), t(5), k_("eps", NT), ALU.add).then_inc(mv_steps[n], 1)
            pool.wait_ge(mv_steps[n], NMV[n] * c + 8)
            nc.gpsimd.tensor_tensor(t(8), t(6), t(7), ALU.add).then_inc(mv_steps[n], 1)
            pool.wait_ge(mv_steps[n], NMV[n] * c + 9)
            nc.gpsimd.tensor_tensor(t(9), t(8), k_("-half", NT), ALU.pow) \
                .then_inc(mv_steps[n] if n == 0 else rstd_ready[n], 1)
            if n == 0:
                nc.gpsimd.tensor_tensor(t(10), t(0), k_("-half", NT), ALU.mult).then_inc(mv_steps[n], 1)
                pool.wait_ge(mv_steps[n], NMV[n] * c + 11)
                nc.gpsimd.tensor_tensor(t(11), t(10), t(9), ALU.mult).then_inc(rstd_ready[n], 1)

        def token_stats(dve, n, i, p):
            c = number(i, p)
            ge(dve, rstd_ready[n], c)
            if n == 0:
                dve.wait_ge(x_loaded[p], 16 * (i + 1))
            src = xin_of(i, p) if n == 0 else x1[:, p]
            for t in range(NT):
                if n == 1:
                    dve.wait_ge(x1_ready, 2 * c + 1 + t // 2)
                last = nc.vector.bn_stats(stats[:, n, t], src[:, t])
            last.then_inc(stats_ready[n], 1)

        def normalise_first(act, i, p):
            act.wait_ge(rstd_ready[0], number(i, p) + 1)
            src = xin_of(i, p)
            for t in range(NT):
                last = nc.scalar.activation(ntok[:, t], src[:, t], ACT.Identity, bias=ms[:, 0, 11, t:t + 1],
                                            scale=ms[:, 0, 9, t:t + 1])
            last.then_inc(norm_ready[0], 1)

        def normalise_second(dve, i, p):
            c = number(i, p)
            dve.wait_ge(rstd_ready[1], c + 1)
            ge(dve, transposed[1], 2 * c)
            for t in range(NT):
                last = nc.vector.tensor_scalar(ntok[:, t], x1[:, p, t], ms[:, 1, 3, t:t + 1], ms[:, 1, 9, t:t + 1],
                                               ALU.subtract, ALU.mult)
            last.then_inc(norm_ready[1], 1)

        def load(sp, i, p):
            ge(sp, x_loaded[p], 16 * i)
            sp.dma_start(xin_of(i, p), x_v[i, p]).then_inc(x_loaded[p], 16)

        in_win, in_wout, in_small, in_const, in_wmod, in_w1, in_w2, in_r2, in_gates = (
            sem(f"in_{n}") for n in ("win", "wout", "small", "const", "wmod", "w1", "w2", "r2", "gate_rows"))
        s_tr = sem("setup_transposed")
        s_silu, s_scT = sem("setup_silu"), sem("setup_scT")
        s_hi, s_mods, s_modps, s_gps, s_g1, s_g2 = (sem(f"setup_{n}") for n in (
            "high_parts", "mods", "mod_products", "gate_products", "gate_sign", "gate_abs"))
        s_bias, s_b1T, s_r2 = sem("setup_bias_products"), sem("setup_b1T"), sem("setup_r2")
        s_winT, s_rtT, s_wo, s_pow = sem("setup_winT"), sem("setup_rtT"), sem("setup_wo"), sem("setup_exponents")

        with nc.Block() as block:
            @block.sync
            def _(sp):
                sp.dma_start(c_rows[0:B, :], c_d).then_inc(in_small, 16)
                sp.dma_start(rt_rows[0:E, :], rout_d).then_inc(in_small, 16)
                sp.dma_start(b1_rows[0:1, :], sb1_d.rearrange("(a h) -> a h", a=1)).then_inc(in_small, 16)
                sp.dma_start(b1_rows[1:NE, :], rb1_d).then_inc(in_small, 16)
                sp.dma_start(eb[0:E, :], ebias_d.rearrange("(e a) -> e a", a=1)).then_inc(in_small, 16)
                sp.dma_start(win_rows, w_in_d.rearrange("(m p) d -> p m d", p=P)).then_inc(in_win, 16)
                for p in range(CB):
                    load(sp, 0, p)
                sp.dma_start(wmod, wmod_d.rearrange("(k p) n -> p k n", p=P)).then_inc(in_wmod, 16)
                sp.dma_start(wout_rows, w_out_d.rearrange("(m p) d -> p m d", p=P)).then_inc(in_wout, 16)
                sp.dma_start(w1f[0], sw1_d.rearrange("(k p) h -> p k h", p=P)).then_inc(in_w1, 16)
                sp.dma_start(w1f_routed.rearrange("p e k h -> p (e k) h"),
                             rw1_d.rearrange("e (k p) h -> p (e k) h", p=P)).then_inc(in_w1, 16)
                sp.wait_ge(s_g2, 1)
                sp.dma_start(gate_rows, gfull[0:B, :]).then_inc(in_gates, 16)
                sp.wait_ge(in_gates, 16)

            @block.gpsimd
            def _(pool):
                for n, what in enumerate(PC):
                    value = {"-half": -0.5, "half": 0.5, "one": 1.0, "eps": EPS_LN, "1/D": 1.0 / D}.get(what) or 2.0 / what
                    nc.gpsimd.memset(pool_c[:, n:n + 1], value).then_inc(s_pow, 1)
                nc.gpsimd.memset(split[:, :, :], 1.0).then_inc(s_pow, 1)
                nc.gpsimd.memset(zero[:, :], 0.0).then_inc(s_pow, 1)
                nc.gpsimd.memset(logT[:, :], 0.0).then_inc(s_pow, 1)
                nc.gpsimd.memset(rtF, 0.0).then_inc(s_pow, 1)
                nc.gpsimd.memset(blog[:, :], 0.0).then_inc(s_pow, 1)
                pool.wait_ge(s_pow, len(PC) + 5)
                for p in range(CB):
                    inv_std(pool, 0, 0, p)

            @block.scalar
            def _(act):
                act.dma_start(const[:, :], const_d[:, 0:at]).then_inc(in_const, 16)
                act.dma_start(cfself, const_d[:, at:at + E * P]).then_inc(in_const, 16)
                rw2 = rw2_d.rearrange("(a o) h d -> h o a d", o=2)
                act.dma_start(w2f[:, 0], sw2_d).then_inc(in_w2, 16)
                act.dma_start(w2f[:, 1:E // 2], rw2[:, 1, 0:E // 2 - 1]).then_inc(in_w2, 16)
                act.dma_start(w2[:, 0:E // 2], rw2[:, 0]).then_inc(in_w2, 16)
                act.dma_start(w2[:, E // 2], rw2_d[E - 1]).then_inc(in_w2, 16)
                for half in range(2):
                    r = half * (SPL // 2)
                    for copy in range(3):
                        act.dma_start(r2f[r + copy * E:r + (copy + 1) * E, :], rb2_d).then_inc(in_r2, 16)
                    act.dma_start(r2f[r + 3 * E:r + 3 * E + 1, :],
                                  sb2_d.rearrange("(a d) -> a d", a=1)).then_inc(in_r2, 16)
                act.wait_ge(in_small, 5 * 16)
                nc.scalar.activation(silu_c[0:B, :], c_rows[0:B, :], ACT.Silu).then_inc(s_silu, 1)
                for m in range(6):
                    act.wait_ge(s_tr, 2 + m)
                    for k in range(KD):
                        last = nc.scalar.activation(winT[:, k, m * P:(m + 1) * P], ring[m % 2][:, k * P:(k + 1) * P],
                                                    ACT.Copy, scale=0.25 if m < 4 else 1.0)
                    last.then_inc(s_winT, 1)
                act.wait_ge(s_winT, 6)
                nc.scalar.activation(winH[:, :, :], winT, ACT.Copy).then_inc(s_hi, 1)
                for m in range(2):
                    act.wait_ge(s_tr, 8 + m)
                    for k in range(KD):
                        last = nc.scalar.activation(wo[:, k, m * P:(m + 1) * P], ring[m % 2][:, k * P:(k + 1) * P],
                                                    ACT.Copy)
                    last.then_inc(s_wo, 1)
                normalise_first(act, 0, 0)
                act.wait_ge(in_w1, 32)
                nc.scalar.activation(w1H[:, 0], w1f[0], ACT.Copy)
                nc.scalar.activation(w1H[:, 1:NE], w1f_routed, ACT.Copy).then_inc(s_hi, 1)
                act.wait_ge(in_w2, 64)
                nc.scalar.activation(w2H[:, :, :], w2f, ACT.Copy).then_inc(s_hi, 1)
                act.wait_ge(s_wo, 2)

            @block.vector
            def _(dve):
                dve.wait_ge(s_tr, 1)
                nc.vector.tensor_copy(scT, tr[0][:, 0:KD * B].rearrange("p (k b) -> p k b", k=KD)).then_inc(s_scT, 1)
                dve.wait_ge(s_pow, len(PC) + 5)
                nc.vector.tensor_copy(rtF[:, :, 0:E], tr[0][:, 64:64 + KD * E].rearrange("p (k e) -> p k e", k=KD)).then_inc(s_rtT, 1)
                nc.vector.tensor_copy(b1T, tr[0][:, 128:128 + NE]).then_inc(s_b1T, 1)
                dve.wait_ge(s_rtT, 1)
                nc.vector.tensor_copy(rt[:, :, 0], rtF).then_inc(s_rtT, 1)
                dve.wait_ge(s_rtT, 2)
                nc.vector.tensor_tensor(rt[:, :, 1], rtF, rt[:, :, 0].bitcast(f32), ALU.subtract).then_inc(s_rtT, 1)
                token_stats(dve, 0, 0, 0)
                token_stats(dve, 0, 0, 1)
                dve.wait_ge(s_hi, 1)
                nc.vector.tensor_tensor(winL[:, :, :], winT, winH[:, :, :].bitcast(f32), ALU.subtract)
                dve.wait_ge(s_modps, 1)
                mp = misc[:, 0:4 * KD * B].rearrange("p (v k b) -> p v k b", v=4, k=KD)
                for v in range(4):
                    last = nc.vector.tensor_scalar(mods[:, v], mp[:, v], float(v % 2), None, ALU.add)
                last.then_inc(s_mods, 1)
                dve.wait_ge(s_gps, 1)
                g = acc[0][0:B].rearrange("p g d -> p (g d)")
                nc.vector.tensor_scalar(gsign[0:B], g, 0.0, 2.0, ALU.is_ge, ALU.mult).then_inc(s_g1, 1)
                nc.vector.tensor_scalar(gneg[0:B], g, -1.0, 0.25, ALU.mult, ALU.max).then_inc(s_g1, 1)
                dve.wait_ge(s_g1, 2)
                nc.vector.tensor_tensor(gabs[0:B], g, gneg[0:B], ALU.max).then_inc(s_g1, 1)
                dve.wait_ge(s_g1, 3)
                nc.vector.scalar_tensor_tensor(out=gfull[0:B], in0=gsign[0:B], scalar=-1.0, in1=gabs[0:B],
                                               op0=ALU.add, op1=ALU.mult).then_inc(s_g2, 1)
                dve.wait_ge(s_hi, 3)
                nc.vector.tensor_tensor(w2L[:, :, :], w2f, w2H[:, :, :].bitcast(f32), ALU.subtract)
                dve.wait_ge(s_bias, 1)
                nc.vector.tensor_copy(bqkv[:, :, :], misc[:, 128:128 + 6 * B].rearrange("p (m b) -> p m b", m=6))

            @block.tensor
            def _(pe):
                pe.wait_ge(in_const, 32)
                pe.wait_ge(in_small, 5 * 16)
                pe.wait_ge(s_silu, 1)
                for k in range(KD):
                    nc.tensor.transpose(tr[0][:, k * B:(k + 1) * B], silu_c[0:B, k * P:(k + 1) * P], ident[0:B, 0:B])
                    nc.tensor.transpose(tr[0][:, 64 + k * E:64 + (k + 1) * E], rt_rows[0:E, k * P:(k + 1) * P],
                                        ident[0:E, 0:E])
                nc.tensor.transpose(tr[0][:, 128:128 + NE], b1_rows[0:NE, :], ident[0:NE, 0:NE]).then_inc(s_tr, 1)
                pe.wait_ge(in_win, 16)
                for m in range(6):
                    if m >= 2:
                        pe.wait_ge(s_winT, m - 1)
                    for k in range(KD):
                        last = nc.tensor.transpose(ring[m % 2][:, k * P:(k + 1) * P], win_rows[:, m, k * P:(k + 1) * P],
                                                   ident)
                    last.then_inc(s_tr, 1)
                pe.wait_ge(in_wout, 16)
                for m in range(2):
                    pe.wait_ge(s_winT, 5 + m)
                    for k in range(KD):
                        last = nc.tensor.transpose(ring[m % 2][:, k * P:(k + 1) * P], wout_rows[:, m, k * P:(k + 1) * P],
                                                   ident)
                    last.then_inc(s_tr, 1)
                pe.wait_ge(in_wmod, 16)
                pe.wait_ge(s_scT, 1)
                for v, col in enumerate((0, 1, 3, 4)):
                    for ch in range(KD):
                        o = (v * KD + ch) * B
                        for k in range(KD):
                            last = nc.tensor.matmul(misc[:, o:o + B], wmod[:, k, col * D + ch * P:col * D + (ch + 1) * P],
                                                    scT[:, k], start=(k == 0), stop=(k == KD - 1))
                last.then_inc(s_modps, 1)
                gcols = wmod.rearrange("p k (s n) -> p k s n", s=2)[:, :, :, 2 * D:3 * D]
                for k in range(KD):
                    last = nc.tensor.matmul(acc[0][0:B], scT[:, k], gcols[:, k], start=(k == 0), stop=(k == KD - 1))
                last.then_inc(s_gps, 1)
                pe.wait_ge(s_mods, 1)
                pe.wait_ge(s_winT, 6)
                pe.wait_ge(in_w1, 32)
                pe.wait_ge(s_rtT, 1)
                for m in range(6):
                    for k in range(KD):
                        last = nc.tensor.matmul(misc[:, 128 + m * B:128 + (m + 1) * B], winT[:, k, m * P:(m + 1) * P],
                                         mods[:, 0, k], start=(k == 0), stop=(k == KD - 1))
                last.then_inc(s_bias, 1)

        block = ctx.enter_context(nc.Block())

        @block.sync
        def _(sp):
            def store(i, p):
                sp.wait_ge(fin_ready, 2 * number(i, p) + 2)
                sp.dma_start(o_v[i, p], fin[:, :, :]).then_inc(stored[p], 16)

            def load_gate(i, which):
                sp.dma_start(gates[:, which], gate_rows[i, which * D:(which + 1) * D].partition_broadcast(P)) \
                    .then_inc(gate_loaded[which], 16)

            def step(i, p, stores, loads):
                if p == 0:
                    if loads or i < B:
                        if not isinstance(i, int) or i:
                            sp.wait_ge(x1_ready, 2 * number(i, 0))
                        load_gate(i, 0)
                    if stores:
                        load_gate(i - 1, 1)
                if stores:
                    store(i - 1, p)
                if loads:
                    sp.wait_ge(x1_ready, 2 * number(i, p) + 2)
                    load(sp, i + 2, p)

            for p in range(CB):
                load(sp, 1, p)
            for p in range(CB):
                step(0, p, False, True)
            with sp.Fori(1, B - 2) as i:
                for p in range(CB):
                    step(i, p, True, True)
            for i in (B - 2, B - 1, B):
                for p in range(CB):
                    step(i, p, True, False)
            for p in range(CB):
                sp.wait_ge(stored[p], 16 * B)

        @block.gpsimd
        def _(pool):
            g = nc.gpsimd

            def weigh_order_5(i, p):
                c = number(i, p)
                pool.wait_ge(odd_ready, 4 * c + 2)
                ge(pool, numerator, 2 * c)
                g.tensor_tensor(f(W + 4), f(KT5), f(V0), ALU.mult).then_inc(weighted5, 1)

            def add_orders(i, p):
                c = number(i, p)
                for n in range(2):
                    pool.wait_ge(products, ND * c + 2 * n + 2)
                    g.tensor_tensor(f(W + 2 * n), f(W + 2 * n), f(W + 2 * n + 1), ALU.add).then_inc(added, 1)

            def scores(i, p):
                c = number(i, p)
                n = [0]

                def then(ins):
                    n[0] += 1
                    ins.then_inc(score_steps, 1)
                    pool.wait_ge(score_steps, NSCORE * c + n[0])

                r = lambda k: route[:, k]
                pool.wait_ge(inv2_ready, 2 * c + 2)
                then(g.tensor_tensor(r(Z), r(U), r(RC), ALU.mult))
                then(g.tensor_tensor(r(Z2), r(Z), r(Z), ALU.mult))
                then(g.tensor_tensor(r(PL), r(Z2), k_(15, NT * E), ALU.mult))
                for m in (13, 11, 9, 7, 5, 3):
                    then(g.tensor_tensor(r(PL), r(PL), k_(m, NT * E), ALU.add))
                    then(g.tensor_tensor(r(PL), r(PL), r(Z2), ALU.mult))
                then(g.tensor_tensor(r(PL), r(PL), k_(1, NT * E), ALU.add))
                then(g.tensor_tensor(r(PL), r(PL), r(Z), ALU.mult))
                pool.wait_ge(log_parts, 3 * c + 3)
                then(g.tensor_tensor(r(SP), r(PL), r(MX), ALU.add))
                then(g.tensor_tensor(r(AC), r(SP), k_("half", NT * E), ALU.pow))
                assert n[0] == NSCORE, n

            def split_weights(i, p):
                c = number(i, p)
                n = [0]

                def then(ins):
                    n[0] += 1
                    ins.then_inc(split_steps, 1)
                    pool.wait_ge(split_steps, NSPLIT * c + n[0])

                pool.wait_ge(rank_steps, NRANK * c + NRANK)
                ge(pool, split_T, c)
                cf = route[:, CF].rearrange("p (t e) -> p t e", t=NT)

                def copy(out, in_):
                    ones = k_("one", NT * out.shape[2]).rearrange("p (t e) -> p t e", t=NT)
                    then(g.tensor_tensor(out, in_, ones, ALU.mult))

                copy(part[:, 0], cf)
                then(g.tensor_tensor(rest[:, :, :], cf, part[:, 0], ALU.subtract))
                copy(part[:, 1], rest[:, :, :])
                then(g.tensor_tensor(split[:, :, 2 * E:3 * E], rest[:, :, :], part[:, 1], ALU.subtract))
                copy(split[:, :, 0:E], part[:, 0])
                copy(split[:, :, E:2 * E], part[:, 1])
                h = SPL // 2
                copy(split[:, :, h:h + 3 * E], split[:, :, 0:3 * E])
                assert n[0] == NSPLIT, n

            def add_residual(i, p):
                c = number(i, p)
                for h in range(2):
                    pool.wait_ge(ffn_gated, 2 * c + h + 1)
                    o = fin[:, 2 * h:2 * h + 2]
                    g.tensor_tensor(o, o, x1[:, p, 2 * h:2 * h + 2], ALU.add).then_inc(fin_ready, 1)

            def step(i, p, st):
                if st["second"]:
                    inv_std(pool, 1, *later(i, p, -1))
                if st["attn"]:
                    weigh_order_5(i, p)
                if st["norm"]:
                    inv_std(pool, 0, *later(i, p, 2))
                if st["second"]:
                    scores(*later(i, p, -1))
                if st["attn"]:
                    add_orders(i, p)
                if st["second"]:
                    split_weights(*later(i, p, -1))
                if st["ffn"]:
                    add_residual(*later(i, p, -2))

            for i, p, st in FIRST:
                step(i, p, st)
            with pool.Fori(1, B - 1) as i:
                for p in range(CB):
                    step(i, p, ALL)
            for i, p, st in LAST:
                step(i, p, st)

        @block.scalar
        def _(act):
            a = nc.scalar

            def highs(n, i, p):
                c = number(i, p)
                for k in range(KD):
                    act.wait_ge(transposed[n], 2 * c + k + 1)
                    out = n1H[:, k] if n == 0 else n2H[:, p, k]
                    a.activation(out, tr[k][:, :], ACT.Copy,
                                 scale=col(mods[:, 2 * n + 1, k], i)).then_inc(high_ready[n], 1)

            def copy_qkv(i, p, use, half):
                at, bank = use[half]
                m = HALVES.index(half)
                act.wait_ge(ring_filled, at + 1)
                if m >= 4:
                    ge(act, weighted, (ND - 1) * number(i, p))
                    ge(act, weighted5, number(i, p))
                a.activation(feat[:, (K0 + p, Q0 + p, V0)[m // 2], m % 2], ring[bank][:, :], ACT.Identity,
                             bias=col(bqkv[:, (2, 3, 0, 1, 4, 5)[m]], i)).then_inc(ring_copied, 1)

            def square(i, p, q, which):
                c = number(i, p)
                x, s, qa, qb = ((K0 + p, KS, KA, KT5), (Q0 + p, QSQ, QA, QT5))[q]
                if which == 0:
                    act.wait_ge(clipped, 2 * c + q + 1)
                    if q == 0:
                        ge(act, summed, 2 * c)
                        ge(act, products, ND * c)
                    a.activation(f(s), f(x), ACT.Square).then_inc(squares, 1)
                else:
                    act.wait_ge(squares, 6 * c + 3 * q + 1)
                    a.activation(f((qa, qb)[which - 1]), f(s), ACT.Square,
                                 bias=cv["biases"][:, which - 1:which]).then_inc(squares, 1)

            def scale_even(i, p):
                c = number(i, p)
                act.wait_ge(squares, 6 * c + 6)
                act.wait_ge(odd_ready, 4 * c + 3)
                a.activation(f(QSQ), f(QSQ), ACT.Copy, scale=GAMMA[1], bias=-0.5 * GAMMA[1]).then_inc(even_scaled, 1)
                a.activation(f(QA), f(QA), ACT.Copy, scale=GAMMA[3], bias=-0.125 * GAMMA[3]).then_inc(even_scaled, 1)

            def row_biases(i, use):
                if use:
                    act.wait_ge(ring_copied, use["e8"][0] + 1)
                a.activation(b1row[:, :], b1[:, i] if isinstance(i, int) else b1[:, bass.ds(i, 1)].rearrange("p a e -> p (a e)"),
                             ACT.Copy).then_inc(b1_row, 1)

            def hidden(i, p, use, e):
                at, bank = use[f"e{e}"]
                act.wait_ge(ring_filled, at + 1)
                if e == 0 and p == 0:
                    act.wait_ge(b1_row, i + 1)
                a.activation(hid[:, e % NG], ring[bank][:, :], ACT.Silu,
                             bias=b1row[:, e:e + 1]).then_inc(ring_copied, 1)

            def hidden_high(i, p, use, e):
                if e == 0:
                    act.wait_ge(ring_copied, use["e0"][0] + 1)
                else:
                    act.wait_ge(hidw_ready, E * number(i, p) + e)
                a.activation(hidH[:, :], hid[:, e % NG], ACT.Copy).then_inc(hidH_ready, 1)

            def copy_logits(i, p):
                c = number(i, p)
                act.wait_ge(logits_ready, c + 1)
                ge(act, log_tok, c)
                a.activation(logT[0:LQ, :], misc[0:LQ, :], ACT.Identity, bias=col(blog, i)).then_inc(logT_ready, 1)

            def exps(i, p):
                c = number(i, p)
                act.wait_ge(log_parts, 3 * c + 2)
                ge(act, score_steps, NSCORE * c)
                a.activation(route[:, U], route[:, NEG], ACT.Exp).then_inc(exp_ready, 1)

            def combine_rows(i, p):
                c = number(i, p)
                act.wait_ge(split_T, c + 1)
                a.activation(cfB[:, :], misc[0:SPL // 2, :], ACT.Copy).then_inc(cf_ready, 1)
                a.activation(cfR[:, :], misc[0:SPL, :], ACT.Copy).then_inc(cf_ready, 1)

            def step(i, p, st):
                use = ring_of(i, p, st)
                nxt, prev, exp = later(i, p, 1), later(i, p, -1), later(i, p, -2)
                qkv, attn_, second, ffn = st["qkv"], st["attn"], st["second"], st["ffn"]

                def silu(e):
                    if ffn:
                        hidden(*exp, use, e)

                def high(e):
                    if ffn:
                        hidden_high(*exp, use, e)

                def copy(half):
                    if qkv:
                        copy_qkv(*nxt, use, half)

                silu(0)
                silu(1)
                high(0)
                if qkv:
                    highs(0, *nxt)
                silu(2)
                if attn_:
                    scale_even(i, p)
                for half in HALVES[:4]:
                    copy(half)
                silu(3)
                high(2)
                if second:
                    highs(1, *prev)
                silu(4)
                if second:
                    copy_logits(*prev)
                if st["norm"]:
                    normalise_first(act, *later(i, p, 2))
                if second:
                    exps(*prev)
                silu(5)
                high(4)
                copy("v0")
                copy("v1")
                silu(6)
                silu(7)
                high(6)
                silu(8)
                if qkv:
                    for q in range(2):
                        for which in range(3):
                            square(*nxt, q, which)
                if p == 1 and (not isinstance(i, int) or i < B):
                    row_biases(i, use if ffn else None)
                if second:
                    combine_rows(*prev)

            highs(0, 0, 0)
            normalise_first(act, 0, 1)
            for half in HALVES:
                copy_qkv(0, 0, CHUNK0, half)
            for q in range(2):
                for which in range(3):
                    square(0, 0, q, which)
            for i, p, st in FIRST:
                if number(i, p) == 1:
                    act.wait_ge(late_biases, 2)
                step(i, p, st)
            with act.Fori(1, B - 1) as i:
                for p in range(CB):
                    step(i, p, ALL)
            for i, p, st in LAST:
                step(i, p, st)

        @block.vector
        def _(dve):
            v = nc.vector

            def lows(n, i, p):
                c = number(i, p)
                for k in range(KD):
                    dve.wait_ge(high_ready[n], 2 * c + k + 1)
                    hi = n1H[:, k] if n == 0 else n2H[:, p, k]
                    out = n1L[:, k] if n == 0 else n2L[:, p, k]
                    v.scalar_tensor_tensor(out=out, in0=tr[k][:, :], scalar=col(mods[:, 2 * n + 1, k], i),
                                           in1=hi.bitcast(f32), op0=ALU.mult, op1=ALU.subtract).then_inc(low_ready[n], 1)

            def clip(i, p, use, q):
                dve.wait_ge(ring_copied, use[("k1", "q1")[q]][0] + 1)
                x = (K0, Q0)[q] + p
                v.tensor_scalar(f(x), f(x), CLIP, -CLIP, ALU.min, ALU.max).then_inc(clipped, 1)

            def odd(i, p, q):
                c = number(i, p)
                x, s, t3, t5 = ((K0 + p, KS, KT3, KT5), (Q0 + p, QSQ, QT3, QT5))[q]
                dve.wait_ge(squares, 6 * c + 3 * q + 3)
                if q == 0:
                    ge(dve, summed, 2 * c)
                v.scalar_tensor_tensor(out=f(t3), in0=f(s), scalar=-0.75, in1=f(x),
                                       op0=ALU.add, op1=ALU.mult).then_inc(odd_ready, 1)
                v.scalar_tensor_tensor(out=f(t5), in0=f(t5), scalar=-0.078125, in1=f(x),
                                       op0=ALU.add, op1=ALU.mult).then_inc(odd_ready, 1)

            ORDERS = (0, 1, 3, 2, 4)

            def weigh(i, p, j):
                c = number(i, p)
                n = ORDERS[j]
                val = f(V0)
                if j == 1:
                    ge(dve, projected, 2 * c)
                if j == 0:
                    v.tensor_tensor(f(W), f(K0 + p), val, ALU.mult).then_inc(weighted, 1)
                elif n == 1 or n == 3:
                    v.scalar_tensor_tensor(out=f(W + n), in0=f(KS if n == 1 else KA), scalar=-0.5 if n == 1 else -0.125,
                                           in1=val, op0=ALU.add, op1=ALU.mult).then_inc(weighted, 1)
                else:
                    dve.wait_ge(odd_ready, 4 * c + 1)
                    v.tensor_tensor(f(W + n), f(KT3), val, ALU.mult).then_inc(weighted, 1)

            def prefix(i, p, j):
                c = number(i, p)
                n = ORDERS[j]
                if n < 4:
                    dve.wait_ge(weighted, (ND - 1) * c + j + 1)
                else:
                    dve.wait_ge(weighted5, c + 1)
                if p:
                    dve.wait_ge(carried, i + 1)
                for h in range(KD):
                    last = v.tensor_tensor_scan(feat[:, W + n, h], zero[:, 0:1].to_broadcast([P, CT]), feat[:, W + n, h],
                                                carry[:, n, h:h + 1] if p else 0.0, ALU.add, ALU.add)
                last.then_inc(scanned, 1)

            def carry_over(i, p):
                if p == 0:
                    dve.wait_ge(scanned, ND * number(i, p) + ND)
                    v.tensor_copy(carry[:, :, :], feat[:, W:W + ND, :, CT - 1]).then_inc(carried, 1)

            def order_product(i, p, n):
                c = number(i, p)
                w = f(W + n)
                if n == 0:
                    dve.wait_ge(scanned, ND * c + ND)
                    if p == 0:
                        dve.wait_ge(carried, i + 1)
                if n in (1, 3):
                    dve.wait_ge(even_scaled, 2 * c + (n + 1) // 2)
                    v.tensor_tensor(w, w, f(QSQ if n == 1 else QA), ALU.mult).then_inc(products, 1)
                else:
                    if n:
                        dve.wait_ge(odd_ready, 4 * c + 2 + n // 2)
                    v.scalar_tensor_tensor(out=w, in0=w, scalar=GAMMA[n], in1=f((Q0 + p, 0, QT3, 0, QT5)[n]),
                                           op0=ALU.mult, op1=ALU.mult).then_inc(products, 1)

            def den_key_sums(i, p):
                c = number(i, p)
                dve.wait_ge(summed, 2 * c + 1)
                ge(dve, rank_steps, NRANK * (c - 1))
                if p:
                    dve.wait_ge(kcarried, i + 1)
                v.tensor_tensor_scan(prod[:, :], cv["kshift"].to_broadcast([P, CT]), tr[0][:, :],
                                     kcarry[:, :] if p else 0.0, ALU.add, ALU.add).then_inc(ksum_ready, 1)

            def den_products(i, p):
                c = number(i, p)
                dve.wait_ge(summed, 2 * c + 2)
                dve.wait_ge(ksum_ready, c + 1)
                if p == 0:
                    v.tensor_copy(kcarry[:, :], prod[:, CT - 1:CT]).then_inc(kcarried, 1)
                    dve.wait_ge(kcarried, i + 1)
                v.tensor_tensor(prod[:, :], tr[1][:, :], prod[:, :], ALU.mult).then_inc(prod_ready, 1)

            def invert(i, p):
                c = number(i, p)
                dve.wait_ge(den_ready, c + 1)
                v.tensor_scalar(denom[:, 0], misc[:, 0:P], EPS_DEN, None, ALU.add).then_inc(den_eps, 1)
                dve.wait_ge(den_eps, c + 1)
                v.reciprocal(denom[:, 1], denom[:, 0]).then_inc(den_inv, 1)

            def finish_numerator(i, p):
                c = number(i, p)
                dve.wait_ge(products, ND * c + ND)
                dve.wait_ge(added, 2 * c + 1)
                v.tensor_tensor(f(W), f(W), f(W + 4), ALU.add).then_inc(numerator, 1)
                dve.wait_ge(numerator, 2 * c + 1)
                dve.wait_ge(added, 2 * c + 2)
                v.tensor_tensor(f(W), f(W), f(W + 2), ALU.add).then_inc(numerator, 1)

            def divide(i, p):
                c = number(i, p)
                dve.wait_ge(numerator, 2 * c + 2)
                for k in range(KD):
                    dve.wait_ge(inv_spread, 2 * c + k + 1)
                    v.tensor_tensor(attn[:, k], feat[:, W, k], tr[k][:, :], ALU.mult).then_inc(attn_ready, 1)

            def residual(i, p):
                c = number(i, p)
                dve.wait_ge(gate_loaded[0], 16 * (i + 1))
                for h in range(2):
                    dve.wait_ge(projected, 2 * c + h + 1)
                    v.tensor_tensor(gated[:, h], tr[h][:, :].rearrange("p (t d) -> p t d", t=2), gate(0),
                                    ALU.mult).then_inc(gated_ready, 1)
                ge(dve, fin_ready, 2 * c - 2)
                for h in range(2):
                    dve.wait_ge(gated_ready, 2 * c + h + 1)
                    v.tensor_tensor(x1[:, p, 2 * h:2 * h + 2], gated[:, h], xin_of(i, p)[:, 2 * h:2 * h + 2],
                                    ALU.add).then_inc(x1_ready, 1)

            def logit_parts(i, p):
                c = number(i, p)
                dve.wait_ge(log_tok, c + 1)
                ge(dve, score_steps, NSCORE * c)
                ge(dve, rank_steps, NRANK * c)
                terms = misc.rearrange("p (t q e) -> p t e q", t=NT, q=P // QS)[:, :, 0:E, 0:LQ // QS]
                v.tensor_reduce(route[:, L_].rearrange("p (t e) -> p t e", t=NT), terms, AX.X, ALU.add).then_inc(log_parts, 1)
                dve.wait_ge(log_parts, 3 * c + 1)
                v.scalar_tensor_tensor(out=route[:, NEG], in0=route[:, L_], scalar=-1.0, in1=route[:, L_],
                                       op0=ALU.mult, op1=ALU.min).then_inc(log_parts, 1)
                v.tensor_scalar(route[:, MX], route[:, L_], 0.0, None, ALU.max).then_inc(log_parts, 1)

            def inverse2(i, p):
                c = number(i, p)
                dve.wait_ge(exp_ready, c + 1)
                v.tensor_scalar(route[:, DN], route[:, U], 2.0, None, ALU.add).then_inc(inv2_ready, 1)
                dve.wait_ge(inv2_ready, 2 * c + 1)
                v.reciprocal(route[:, RC], route[:, DN]).then_inc(inv2_ready, 1)

            def choose(i, p):
                c = number(i, p)
                at = NRANK * c
                dve.wait_ge(score_steps, NSCORE * c + NSCORE)
                s = route[:, AC].rearrange("p (t e) -> p t e", t=NT)
                others = s.unsqueeze(2).to_broadcast([P, NT, E, E])
                own = s.unsqueeze(3).to_broadcast([P, NT, E, E])
                v.tensor_tensor(pair[:, 0], others, own, ALU.is_ge).then_inc(rank_steps, 1)
                v.tensor_tensor(pair[:, 1], others, own, ALU.is_gt).then_inc(rank_steps, 1)
                dve.wait_ge(rank_steps, at + 1)
                g0, g1 = (pair[:, k].rearrange("p t e j -> p t (e j)") for k in range(2))
                v.tensor_tensor(g0, g0, before, ALU.mult).then_inc(rank_steps, 1)
                dve.wait_ge(rank_steps, at + 2)
                v.tensor_tensor(g1, g1, after, ALU.mult).then_inc(rank_steps, 1)
                dve.wait_ge(rank_steps, at + 4)
                v.tensor_tensor(pair[:, 0], pair[:, 0], pair[:, 1], ALU.add).then_inc(rank_steps, 1)
                dve.wait_ge(rank_steps, at + 5)
                v.tensor_reduce(rank, pair[:, 0].rearrange("p t e j -> p (t e) j"), AX.X,
                                ALU.add).then_inc(rank_steps, 1)
                dve.wait_ge(rank_steps, at + 6)
                ge(dve, split_steps, NSPLIT * c)
                v.scalar_tensor_tensor(out=route[:, CF], in0=rank, scalar=2.0, in1=route[:, AC],
                                       op0=ALU.is_lt, op1=ALU.mult).then_inc(rank_steps, 1)

            def weigh_hidden(i, p, use, e):
                c = number(i, p)
                dve.wait_ge(ring_copied, use[f"e{e}"][0] + 1)
                dve.wait_ge(cfb_ready, E * c + e)
                v.tensor_tensor(hid[:, e % NG], hid[:, e % NG], cfb[:, :], ALU.mult).then_inc(hidw_ready, 1)

            def hidden_low(i, p, e):
                dve.wait_ge(hidH_ready, len(SPLIT) * number(i, p) + e // 2 + 1)
                v.tensor_tensor(hidL[:, :], hid[:, e % NG], hidH[:, :].bitcast(f32), ALU.subtract).then_inc(hidL_ready, 1)

            def output(i, p):
                c = number(i, p)
                dve.wait_ge(expert_done, NE * c + NE)
                dve.wait_ge(gate_loaded[1], 16 * (i + 1))
                ge(dve, stored[1 - p], 16 * (i + p))
                for h in range(2):
                    v.tensor_tensor(fin[:, 2 * h:2 * h + 2], acc[h][:, :, :], gate(1), ALU.mult).then_inc(ffn_gated, 1)

            def step(i, p, st):
                use = ring_of(i, p, st)
                nxt, prev, exp, after2 = later(i, p, 1), later(i, p, -1), later(i, p, -2), later(i, p, 2)
                norm, qkv, attn_, second, ffn = (st[k] for k in ("norm", "qkv", "attn", "second", "ffn"))

                def expert(e):
                    if ffn:
                        weigh_hidden(*exp, use, e)

                def low(e):
                    if ffn:
                        hidden_low(*exp, e)

                if second:
                    residual(*prev)
                if second:
                    token_stats(dve, 1, *prev)
                low(0)
                if qkv:
                    lows(0, *nxt)
                if attn_:
                    weigh(i, p, 0)
                expert(1)
                if attn_:
                    weigh(i, p, 1)
                    weigh(i, p, 2)
                if second:
                    normalise_second(dve, *prev)
                if attn_:
                    weigh(i, p, 3)
                expert(2)
                if norm:
                    token_stats(dve, 0, *after2)
                low(2)
                if second:
                    lows(1, *prev)
                if attn_:
                    prefix(i, p, 0)
                    prefix(i, p, 1)
                expert(3)
                if attn_:
                    prefix(i, p, 2)
                if qkv:
                    clip(*nxt, use, 0)
                    clip(*nxt, use, 1)
                if second:
                    logit_parts(*prev)
                if attn_:
                    den_key_sums(i, p)
                    prefix(i, p, 3)
                    den_products(i, p)
                if second:
                    inverse2(*prev)
                expert(4)
                if attn_:
                    prefix(i, p, 4)
                low(4)
                if attn_:
                    carry_over(i, p)
                    order_product(i, p, 0)
                    order_product(i, p, 1)
                    order_product(i, p, 2)
                expert(5)
                if attn_:
                    order_product(i, p, 3)
                    invert(i, p)
                expert(6)
                if attn_:
                    order_product(i, p, 4)
                low(6)
                if second:
                    choose(*prev)
                expert(7)
                expert(8)
                if attn_:
                    finish_numerator(i, p)
                    divide(i, p)
                if ffn:
                    output(*exp)
                if qkv:
                    odd(*nxt, 0)
                    odd(*nxt, 1)

            def low_weights():
                nc.vector.tensor_tensor(w1L[:, 0], w1f[0], w1H[:, 0].bitcast(f32), ALU.subtract).then_inc(late_weights, 1)
                nc.vector.tensor_tensor(w1L[:, 1:NE], w1f_routed, w1H[:, 1:NE].bitcast(f32),
                                        ALU.subtract).then_inc(late_weights, 1)
                dve.wait_ge(in_r2, 8 * 16)
                nc.vector.tensor_copy(r2[:, :], r2f[0:SPL, :]).then_inc(s_r2, 1)
                dve.wait_ge(s_r2, 1)
                nc.vector.tensor_tensor(r2l[0:SPL, :], r2f[0:SPL, :], r2[:, :].bitcast(f32), ALU.subtract).then_inc(s_r2, 1)
                nc.vector.tensor_scalar(r2h[0:SPL, :], r2[:, :].bitcast(f32), cv["rowmask"][0:SPL, 0:1], None,
                                        ALU.mult).then_inc(s_r2, 1)
                dve.wait_ge(s_r2, 3)
                nc.vector.scalar_tensor_tensor(out=r2[:, :], in0=r2l[0:SPL, :], scalar=cv["rowmask"][0:SPL, 1:2],
                                               in1=r2h[0:SPL, :], op0=ALU.mult, op1=ALU.add).then_inc(s_r2, 1)
                nc.vector.tensor_copy(cfsel[:, :, :], cfself[0:SPL // 2, :].rearrange("p (e m) -> p e m", e=E)).then_inc(late_weights, 1)

            def biases_out():
                dve.wait_ge(late_products, 1)
                v.tensor_tensor(b1.rearrange("p b m -> p m b"), cfb[:, 0:NE * B].rearrange("p (m b) -> p m b", m=NE),
                                b1T.unsqueeze(2).to_broadcast([P, NE, B]), ALU.add).then_inc(late_biases, 1)
                v.tensor_scalar(blog[0:E, :], cfb[0:E, 128:128 + B], eb[0:E, :], None, ALU.add).then_inc(late_biases, 1)

            lows(0, 0, 0)
            low_weights()
            for q in range(2):
                clip(0, 0, CHUNK0, q)
            for q in range(2):
                odd(0, 0, q)
            for i, p, st in FIRST:
                step(i, p, st)
                if number(i, p) == 0:
                    biases_out()
                    dve.wait_ge(late_biases, 2)
                    dve.wait_ge(late_weights, 3)
            for p in range(CB):
                step(1, p, ALL)
            with dve.Fori(2, B - 1) as i:
                for p in range(CB):
                    step(i, p, ALL)
            for i, p, st in LAST:
                step(i, p, st)

        @block.tensor
        def _(pe):
            mm = nc.tensor.matmul

            def transposes(n, i, p, behind_norm=False):
                c = number(i, p)
                pe.wait_ge(norm_ready[n], c + 1)
                if behind_norm:
                    pe.wait_ge(low_ready[0], 2 * (c + 3))
                else:
                    ge(pe, gated_ready, 2 * (c - 1 if n == 0 else c + 1))
                for k in range(KD):
                    for t in range(NT):
                        last = nc.tensor.transpose(tr[k][:, t * P:(t + 1) * P], ntok[:, t, k * P:(k + 1) * P], ident)
                    last.then_inc(transposed[n], 1)

            def split_product(out, wH, wL, xH, xL):
                terms = [(wH[k], xH[k]) for k in range(KD)] + [(wH[k], xL[k]) for k in range(KD)] \
                    + [(wL[k], xH[k]) for k in range(KD)]
                for n, (w, x) in enumerate(terms):
                    last = mm(out, w, x, start=(n == 0), stop=(n == len(terms) - 1))
                return last

            halves = lambda t: [t[:, k] for k in range(KD)]

            def project(i, p, use, half):
                c = number(i, p)
                pe.wait_ge(high_ready[0], 2 * c + 2)
                pe.wait_ge(low_ready[0], 2 * c + 2)
                at, bank = use[half]
                ge(pe, ring_copied, at - 1)
                w = (2, 3, 0, 1, 4, 5)[HALVES.index(half)]
                cols = slice(w * P, (w + 1) * P)
                split_product(ring[bank][:, :], [winH[:, k, cols] for k in range(KD)],
                              [winL[:, k, cols] for k in range(KD)], halves(n1H), halves(n1L)).then_inc(ring_filled, 1)

            def route_logits(i, p):
                c = number(i, p)
                pe.wait_ge(high_ready[1], 2 * c + 2)
                pe.wait_ge(low_ready[1], 2 * c + 2)
                ge(pe, cf_ready, 2 * c)
                pe.wait_ge(den_eps, c + 1)
                terms = [(k, x) for k in range(KD) for x in (n2H, n2L)]
                for n, (k, x) in enumerate(terms):
                    last = mm(misc[0:LQ, :], rt[:, k].rearrange("p g e -> p (g e)"), x[:, p, k], start=(n == 0),
                              stop=(n == len(terms) - 1))
                last.then_inc(logits_ready, 1)

            def logits_by_token(i, p):
                c = number(i, p)
                pe.wait_ge(logT_ready, c + 1)
                for t in range(NT):
                    last = nc.tensor.transpose(misc[:, t * P:(t + 1) * P], logT[:, t * P:(t + 1) * P], ident)
                last.then_inc(log_tok, 1)

            def head_sums(i, p, q, behind_second):
                c = number(i, p)
                if behind_second:
                    pe.wait_ge(low_ready[1], 2 * c)
                else:
                    pe.wait_ge(low_ready[0], 2 * (c + 2))
                srcs = ((K0 + p, KS, KT3, KA, KT5), (Q0 + p, QSQ, QT3, QA, QT5))[q]
                pe.wait_ge(odd_ready, 4 * c + 2 * q + 2)
                if q:
                    pe.wait_ge(even_scaled, 2 * c + 2)
                order = [(0, 0), (1, 0), (2, 0), (3, 0), (0, 1), (1, 1), (2, 1), (3, 1), (4, 0), (4, 1)]
                final = {0: (4, 0), 1: (4, 1), 2: (2, 1), 3: (3, 1)}
                for n, h in order:
                    g_, r = ROWS[n, h]
                    last = mm(tr[q][g_ * QS:(g_ + 1) * QS, :],
                              cv["headsum"][:, (r // HPH) * QS:(r // HPH + 1) * QS], feat[:, srcs[n], h],
                              start=(n < 4 and h == 0), stop=(final[g_] == (n, h)))
                last.then_inc(summed, 1)

            def denominators(i, p):
                c = number(i, p)
                pe.wait_ge(prod_ready, c + 1)
                ge(pe, log_parts, 3 * (c - 1) + 1)
                for t in range(NT):
                    last = mm(misc[t * QS:(t + 1) * QS, 0:P], cv["densum"],
                              prod[:, t * P:(t + 1) * P], start=True, stop=True)
                last.then_inc(den_ready, 1)

            def spread_inverse(i, p):
                c = number(i, p)
                pe.wait_ge(den_inv, c + 1)
                for k in range(KD):
                    for t in range(NT):
                        last = mm(tr[k][:, t * P:(t + 1) * P], cv["headsel"][:, (t * KD + k) * P:(t * KD + k + 1) * P], denom[:, 1],
                                  start=True, stop=True)
                    last.then_inc(inv_spread, 1)

            def project_out(i, p):
                c = number(i, p)
                pe.wait_ge(attn_ready, 2 * c + 2)
                for t in range(NT):
                    for k in range(KD):
                        last = mm(tr[t // 2][:, (t % 2) * D:(t % 2 + 1) * D], attn[:, k, t * P:(t + 1) * P], wo[:, k],
                                  start=(k == 0), stop=(k == KD - 1))
                    if t % 2:
                        last.then_inc(projected, 1)

            def combine_by_expert(i, p, behind_attn):
                c = number(i, p)
                pe.wait_ge(split_steps, NSPLIT * c + NSPLIT)
                if behind_attn:
                    pe.wait_ge(den_eps, c + 2)
                else:
                    pe.wait_ge(log_parts, 3 * c + 1)
                for t in range(NT):
                    last = nc.tensor.transpose(misc[:, t * P:(t + 1) * P], split[:, t], ident)
                last.then_inc(split_T, 1)

            def expert_up(i, p, use, e):
                at, bank = use[f"e{e}"]
                pe.wait_ge(ring_copied, at - 1)
                split_product(ring[bank][:, :], halves(w1H[:, e]), halves(w1L[:, e]),
                              halves(n2H[:, p]), halves(n2L[:, p])).then_inc(ring_filled, 1)

            def spread_weights(i, p, e):
                mm(cfb[:, :], cfsel[:, e - 1], cfB[:, :], start=True, stop=True).then_inc(cfb_ready, 1)

            def second_biases(i, p):
                c = number(i, p)
                pe.wait_ge(cf_ready, 2 * c + 2)
                ge(pe, ffn_gated, 2 * c)
                for t in range(NT):
                    mm(acc[t // 2][:, t % 2], cfR[:, t * P:(t + 1) * P], r2[:, :], start=(t % 2 == 0), stop=False,
                       skip_group_check=True)

            def expert_down(i, p, use, e):
                c = number(i, p)
                if e:
                    pe.wait_ge(hidw_ready, E * c + e)
                if e < E:
                    spread_weights(i, p, e + 1)
                if e in SPLIT:
                    pe.wait_ge(hidL_ready, len(SPLIT) * c + e // 2 + 1)
                    terms = ((hidH, w2H), (hidH, w2L), (hidL, w2H))
                else:
                    terms = ((hid[:, e % NG], w2),)
                for t in range(NT):
                    for x, w in terms:
                        last = mm(acc[t // 2][:, t % 2], x[:, t * P:(t + 1) * P], w[:, e // 2], start=False,
                                  stop=(e == E), skip_group_check=True)
                last.then_inc(expert_done, 1)

            def step(i, p, st):
                use = ring_of(i, p, st)
                nxt, prev, exp = later(i, p, 1), later(i, p, -1), later(i, p, -2)
                qkv, attn_, second, ffn = st["qkv"], st["attn"], st["second"], st["ffn"]

                def expert(e):
                    if ffn:
                        if e + 2 < NE:
                            expert_up(*exp, use, e + 2)
                        expert_down(*exp, use, e)

                if ffn:
                    expert_up(*exp, use, 0)
                    expert_up(*exp, use, 1)
                    second_biases(*exp)
                if qkv:
                    transposes(0, *nxt)
                if isinstance(i, int) and number(i, p) == 0:
                    bias_products()
                expert(0)
                if qkv:
                    for half in HALVES[:4]:
                        project(*nxt, use, half)
                expert(1)
                if second:
                    transposes(1, *prev, behind_norm=qkv)
                expert(2)
                if second:
                    route_logits(*prev)
                if attn_:
                    head_sums(i, p, 0, second)
                if second:
                    logits_by_token(*prev)
                if attn_:
                    head_sums(i, p, 1, second)
                expert(3)
                if qkv:
                    project(*nxt, use, "v0")
                    project(*nxt, use, "v1")
                expert(4)
                if attn_:
                    denominators(i, p)
                expert(5)
                if attn_:
                    spread_inverse(i, p)
                expert(6)
                expert(7)
                expert(8)
                if attn_:
                    project_out(i, p)
                if second:
                    combine_by_expert(*prev, attn_)

            def bias_products():
                for e in range(NE):
                    for k in range(KD):
                        mm(cfb[:, e * B:(e + 1) * B], w1f[e][:, k], mods[:, 2, k], start=(k == 0), stop=(k == KD - 1))
                for k in range(KD):
                    last = mm(cfb[0:E, 128:128 + B], rtF[:, k, 0:E], mods[:, 2, k], start=(k == 0), stop=(k == KD - 1))
                last.then_inc(late_products, 1)

            transposes(0, 0, 0)
            for half in HALVES:
                project(0, 0, CHUNK0, half)
            for i, p, st in FIRST:
                step(i, p, st)
            pe.wait_ge(late_weights, 3)
            pe.wait_ge(s_r2, 4)
            for p in range(CB):
                step(1, p, ALL)
            with pe.Fori(2, B - 1) as i:
                for p in range(CB):
                    step(i, p, ALL)
            for i, p, st in LAST:
                step(i, p, st)


_INS = ['L0_attn_x', 'L0_attn_W_in', 'L0_attn_W_out', 'L0_ffn_routing_W', 'L0_ffn_expert_bias', 'L0_ffn_sW1',
        'L0_ffn_sb1', 'L0_ffn_sW2', 'L0_ffn_sb2', 'L0_ffn_rW1', 'L0_ffn_rb1', 'L0_ffn_rW2', 'L0_ffn_rb2', 'L0_c',
        'L0_wmod']


def kernel(**inputs):
    import concourse.bacc as _bacc
    from concourse.bass_utils import run_bass_kernel_spmd as _run

    nc = _bacc.Bacc("TRN2", target_bir_lowering=False, num_devices=1)
    arrays, args = {}, []
    for name in _INS:
        a = np.ascontiguousarray(inputs[name])
        arrays[f"in_{name}"] = a
        args.append(nc.dram_tensor(f"in_{name}", a.shape, mybir.dt.from_np(a.dtype), kind="ExternalInput").ap())
    a = constants()
    arrays["in_constants"] = a
    args.append(nc.dram_tensor("in_constants", a.shape, mybir.dt.float32, kind="ExternalInput").ap())
    args.append(nc.dram_tensor("out", (B, S, D), mybir.dt.float32, kind="ExternalOutput").ap())
    build(nc, *args)
    r = _run(nc, [arrays], core_ids=[0])
    return r.results[0]["out"]
```
